# Optimizing a Trainium2 kernel written in Bass

```python
import numpy as np
import jax
import jax.numpy as jnp

def _softmax(x, axis=-1):
    return jax.nn.softmax(x, axis=axis)

def _gelu(x):
    return jax.nn.gelu(x, approximate=True)

def _silu(x):
    return jax.nn.silu(x)

def _sigmoid(x):
    return jax.nn.sigmoid(x)

def _layernorm(x, axis=-1, eps=1e-05):
    m = jnp.mean(x, axis=axis, keepdims=True)
    v = jnp.var(x, axis=axis, keepdims=True)
    return (x - m) / jnp.sqrt(v + eps)

def _scatter_add(tgt, idx, src, axis=0):
    return tgt.at[idx].add(src)

def _segment_sum(src, seg, n):
    return jax.ops.segment_sum(src, seg, n)
kernel_name = 'mk_seq_postln_d2_jaxref_r8_1ed09e'

def setup_inputs(seed: int=0):
    np.random.seed(seed)
    _w = jnp.asarray

    def _L0_attn_setup():
        import jax, jax.numpy as jnp
        import numpy as np
        DEPTH, DIM, DFF, VOCAB = (4, 64, 256, 512)
        EPS = 1e-05

        def layernorm(x, w, b):
            mu = jnp.mean(x, axis=-1, keepdims=True)
            var = jnp.mean((x - mu) ** 2, axis=-1, keepdims=True)
            return (x - mu) * jax.lax.rsqrt(var + EPS) * w + b

        def sconv(x, phazor_c, last_conv_c):
            B, L, D = x.shape
            r = jnp.abs(phazor_c)
            p = jnp.tanh(r) * jnp.exp(1j * jnp.angle(phazor_c))
            prog = p[None, :] ** jnp.arange(L, dtype=jnp.float32)[:, None]
            filt_fft = jnp.fft.fft(prog, n=2 * L, axis=0)
            x_fft = jnp.fft.fft(x.astype(jnp.complex64), n=2 * L, axis=1)
            conv = jnp.fft.ifft(filt_fft[None] * x_fft, axis=1)[:, :L]
            conv = conv + last_conv_c[None, None, :] * prog[None] * p[None, None, :]
            return conv.real.astype(x.dtype)

        def _forward(x, Win, bin, ln1_w, ln1_b, phz_re, phz_im, lc_re, lc_im, sc_lin, ln2_w, ln2_b, W1, b1, W2, b2, lnl_w, lnl_b, Wout, bout):
            h = jnp.einsum('blv,dv->bld', x, Win) + bin

            def body(h, p):
                l1w, l1b, pr, pi, lr, li, scl, l2w, l2b, w1, b1_, w2, b2_ = p
                y = jax.nn.silu(layernorm(h, l1w, l1b))
                y = sconv(y, pr + 1j * pi, lr + 1j * li)
                h = h + y * scl
                y = layernorm(h, l2w, l2b)
                y = jax.nn.silu(jnp.einsum('bld,fd->blf', y, w1) + b1_)
                y = jnp.einsum('blf,df->bld', y, w2) + b2_
                return (h + y, None)
            xs = (ln1_w, ln1_b, phz_re, phz_im, lc_re, lc_im, sc_lin, ln2_w, ln2_b, W1, b1, W2, b2)
            h, _ = jax.lax.scan(body, h, xs)
            h = layernorm(h, lnl_w, lnl_b)
            return jnp.einsum('bld,vd->blv', h, Wout) + bout
        key = jax.random.key(seed)
        ks = jax.random.split(key, 20)
        f32 = jnp.float32
        inp = {}
        inp['x'] = jax.random.normal(ks[0], (2, 512, VOCAB), dtype=f32)
        inp['Win'] = jax.random.normal(ks[1], (DIM, VOCAB), dtype=f32) * VOCAB ** (-0.5)
        inp['bin'] = jnp.zeros((DIM,), f32)
        inp['ln1_w'] = jnp.ones((DEPTH, DIM), f32)
        inp['ln1_b'] = jnp.zeros((DEPTH, DIM), f32)
        ang = 2 * np.pi * jnp.arange(DIM, dtype=f32) / DIM
        mag = jnp.abs(jax.random.normal(ks[2], (DEPTH, DIM), dtype=f32))
        inp['phz_re'] = mag * jnp.cos(ang)[None]
        inp['phz_im'] = mag * jnp.sin(ang)[None]
        inp['lc_re'] = jax.random.normal(ks[3], (DEPTH, DIM), dtype=f32)
        inp['lc_im'] = jax.random.normal(ks[4], (DEPTH, DIM), dtype=f32)
        inp['sc_lin'] = jnp.ones((DEPTH, DIM), f32)
        inp['ln2_w'] = jnp.ones((DEPTH, DIM), f32)
        inp['ln2_b'] = jnp.zeros((DEPTH, DIM), f32)
        inp['W1'] = jax.random.normal(ks[5], (DEPTH, DFF, DIM), dtype=f32) * DIM ** (-0.5)
        inp['b1'] = jnp.zeros((DEPTH, DFF), f32)
        inp['W2'] = jax.random.normal(ks[6], (DEPTH, DIM, DFF), dtype=f32) * DFF ** (-0.5)
        inp['b2'] = jnp.zeros((DEPTH, DIM), f32)
        inp['lnl_w'] = jnp.ones((DIM,), f32)
        inp['lnl_b'] = jnp.zeros((DIM,), f32)
        inp['Wout'] = jax.random.normal(ks[7], (VOCAB, DIM), dtype=f32) * DIM ** (-0.5)
        inp['bout'] = jnp.zeros((VOCAB,), f32)
        return inp
    _L0_attn_in = _L0_attn_setup()

    def _L0_ffn_setup():
        import jax, jax.numpy as jnp
        import numpy as np
        B, S, IN, OUT = (4, 256, 512, 512)
        E, K, R = (8, 2, 16)
        CAP_FACTOR = 3.0
        ALPHA = 1.0 / R
        LN_EPS = 1e-05
        key = jax.random.key(seed)
        ks = jax.random.split(key, 6)
        return {'x': jax.random.normal(ks[0], (B, S, IN), dtype=jnp.float32), 'weight': jax.random.normal(ks[1], (OUT, IN), dtype=jnp.float32) * 0.02, 'lora_A': jax.random.normal(ks[2], (E, IN, R), dtype=jnp.float32) / np.sqrt(R), 'lora_B': jax.random.normal(ks[3], (E, R, OUT), dtype=jnp.float32) * 0.02, 'gw1': jax.random.normal(ks[4], (4 * E, IN), dtype=jnp.float32) * 0.02, 'gb1': jnp.zeros((4 * E,), dtype=jnp.float32), 'ln_gamma': jnp.ones((4 * E,), dtype=jnp.float32), 'ln_beta': jnp.zeros((4 * E,), dtype=jnp.float32), 'gw2': jax.random.normal(ks[5], (E, 4 * E), dtype=jnp.float32) * 0.02, 'gb2': jnp.zeros((E,), dtype=jnp.float32)}
    _L0_ffn_in = _L0_ffn_setup()

    def _L1_attn_setup():
        import jax, jax.numpy as jnp
        import numpy as np
        HIDDEN = 512
        HEADS = 32
        D_K = HIDDEN // HEADS
        key = jax.random.key(seed)
        ks = jax.random.split(key, 5)
        scale = 1.0 / np.sqrt(HIDDEN)
        x = jax.random.normal(ks[0], (2, 256, HIDDEN), dtype=jnp.float32)
        w_q = jax.random.uniform(ks[1], (HIDDEN, HIDDEN), jnp.float32, -scale, scale)
        w_k = jax.random.uniform(ks[2], (HIDDEN, HIDDEN), jnp.float32, -scale, scale)
        w_v = jax.random.uniform(ks[3], (HIDDEN, HIDDEN), jnp.float32, -scale, scale)
        w_o = jax.random.uniform(ks[4], (HIDDEN, HIDDEN), jnp.float32, -scale, scale)
        return {'x': x, 'w_q': w_q, 'w_k': w_k, 'w_v': w_v, 'w_o': w_o}
    _L1_attn_in = _L1_attn_setup()

    def _L1_ffn_setup():
        import jax, jax.numpy as jnp
        import numpy as np
        THRESH_FACTOR = 0.7

        def _bitlinear(x, w, scale):
            w_abs = jnp.abs(w)
            thr = jnp.mean(w_abs) * THRESH_FACTOR
            wq = jnp.sign(w) * (w_abs > thr).astype(w.dtype)
            w_scaled = wq * scale
            return jnp.einsum('bsd,od->bso', x, w_scaled)
        key = jax.random.key(seed)
        k1, k2, k3, k4 = jax.random.split(key, 4)
        dim, hidden = (512, 2048)
        x = jax.random.normal(k1, (2, 256, dim), dtype=jnp.float32)
        gate_w = jax.random.normal(k2, (hidden, dim), dtype=jnp.float32) / np.sqrt(dim)
        up_w = jax.random.normal(k3, (hidden, dim), dtype=jnp.float32) / np.sqrt(dim)
        down_w = jax.random.normal(k4, (dim, hidden), dtype=jnp.float32) / np.sqrt(hidden)
        return {'x': x, 'gate_w': gate_w, 'gate_scale': jnp.ones((hidden, 1), jnp.float32), 'up_w': up_w, 'up_scale': jnp.ones((hidden, 1), jnp.float32), 'down_w': down_w, 'down_scale': jnp.ones((dim, 1), jnp.float32)}
    _L1_ffn_in = _L1_ffn_setup()
    _d = {'L0_attn_x': _L0_attn_in['x'], 'L0_attn_Win': _L0_attn_in['Win'], 'L0_attn_bin': _L0_attn_in['bin'], 'L0_attn_ln1_w': _L0_attn_in['ln1_w'], 'L0_attn_ln1_b': _L0_attn_in['ln1_b'], 'L0_attn_phz_re': _L0_attn_in['phz_re'], 'L0_attn_phz_im': _L0_attn_in['phz_im'], 'L0_attn_lc_re': _L0_attn_in['lc_re'], 'L0_attn_lc_im': _L0_attn_in['lc_im'], 'L0_attn_sc_lin': _L0_attn_in['sc_lin'], 'L0_attn_ln2_w': _L0_attn_in['ln2_w'], 'L0_attn_ln2_b': _L0_attn_in['ln2_b'], 'L0_attn_W1': _L0_attn_in['W1'], 'L0_attn_b1': _L0_attn_in['b1'], 'L0_attn_W2': _L0_attn_in['W2'], 'L0_attn_b2': _L0_attn_in['b2'], 'L0_attn_lnl_w': _L0_attn_in['lnl_w'], 'L0_attn_lnl_b': _L0_attn_in['lnl_b'], 'L0_attn_Wout': _L0_attn_in['Wout'], 'L0_attn_bout': _L0_attn_in['bout'], 'L0_ffn_weight': _L0_ffn_in['weight'], 'L0_ffn_lora_A': _L0_ffn_in['lora_A'], 'L0_ffn_lora_B': _L0_ffn_in['lora_B'], 'L0_ffn_gw1': _L0_ffn_in['gw1'], 'L0_ffn_gb1': _L0_ffn_in['gb1'], 'L0_ffn_ln_gamma': _L0_ffn_in['ln_gamma'], 'L0_ffn_ln_beta': _L0_ffn_in['ln_beta'], 'L0_ffn_gw2': _L0_ffn_in['gw2'], 'L0_ffn_gb2': _L0_ffn_in['gb2'], 'L1_attn_w_q': _L1_attn_in['w_q'], 'L1_attn_w_k': _L1_attn_in['w_k'], 'L1_attn_w_v': _L1_attn_in['w_v'], 'L1_attn_w_o': _L1_attn_in['w_o'], 'L1_ffn_gate_w': _L1_ffn_in['gate_w'], 'L1_ffn_gate_scale': _L1_ffn_in['gate_scale'], 'L1_ffn_up_w': _L1_ffn_in['up_w'], 'L1_ffn_up_scale': _L1_ffn_in['up_scale'], 'L1_ffn_down_w': _L1_ffn_in['down_w'], 'L1_ffn_down_scale': _L1_ffn_in['down_scale']}
    _x0 = _d['L0_attn_x']
    _d['L0_attn_x'] = jax.random.normal(jax.random.fold_in(jax.random.key(seed), 1), (2, 1024, 512), dtype=_x0.dtype)
    del _x0
    return _d

def reference(L0_attn_x, L0_attn_Win, L0_attn_bin, L0_attn_ln1_w, L0_attn_ln1_b, L0_attn_phz_re, L0_attn_phz_im, L0_attn_lc_re, L0_attn_lc_im, L0_attn_sc_lin, L0_attn_ln2_w, L0_attn_ln2_b, L0_attn_W1, L0_attn_b1, L0_attn_W2, L0_attn_b2, L0_attn_lnl_w, L0_attn_lnl_b, L0_attn_Wout, L0_attn_bout, L0_ffn_weight, L0_ffn_lora_A, L0_ffn_lora_B, L0_ffn_gw1, L0_ffn_gb1, L0_ffn_ln_gamma, L0_ffn_ln_beta, L0_ffn_gw2, L0_ffn_gb2, L1_attn_w_q, L1_attn_w_k, L1_attn_w_v, L1_attn_w_o, L1_ffn_gate_w, L1_ffn_gate_scale, L1_ffn_up_w, L1_ffn_up_scale, L1_ffn_down_w, L1_ffn_down_scale):

    def _L0_attn_ref(x, Win, bin, ln1_w, ln1_b, phz_re, phz_im, lc_re, lc_im, sc_lin, ln2_w, ln2_b, W1, b1, W2, b2, lnl_w, lnl_b, Wout, bout):
        import jax, jax.numpy as jnp
        import numpy as np
        DEPTH, DIM, DFF, VOCAB = (4, 64, 256, 512)
        EPS = 1e-05

        def layernorm(x, w, b):
            mu = jnp.mean(x, axis=-1, keepdims=True)
            var = jnp.mean((x - mu) ** 2, axis=-1, keepdims=True)
            return (x - mu) * jax.lax.rsqrt(var + EPS) * w + b

        def sconv(x, phazor_c, last_conv_c):
            B, L, D = x.shape
            r = jnp.abs(phazor_c)
            p = jnp.tanh(r) * jnp.exp(1j * jnp.angle(phazor_c))
            prog = p[None, :] ** jnp.arange(L, dtype=jnp.float32)[:, None]
            filt_fft = jnp.fft.fft(prog, n=2 * L, axis=0)
            x_fft = jnp.fft.fft(x.astype(jnp.complex64), n=2 * L, axis=1)
            conv = jnp.fft.ifft(filt_fft[None] * x_fft, axis=1)[:, :L]
            conv = conv + last_conv_c[None, None, :] * prog[None] * p[None, None, :]
            return conv.real.astype(x.dtype)

        def _forward(x, Win, bin, ln1_w, ln1_b, phz_re, phz_im, lc_re, lc_im, sc_lin, ln2_w, ln2_b, W1, b1, W2, b2, lnl_w, lnl_b, Wout, bout):
            h = jnp.einsum('blv,dv->bld', x, Win) + bin

            def body(h, p):
                l1w, l1b, pr, pi, lr, li, scl, l2w, l2b, w1, b1_, w2, b2_ = p
                y = jax.nn.silu(layernorm(h, l1w, l1b))
                y = sconv(y, pr + 1j * pi, lr + 1j * li)
                h = h + y * scl
                y = layernorm(h, l2w, l2b)
                y = jax.nn.silu(jnp.einsum('bld,fd->blf', y, w1) + b1_)
                y = jnp.einsum('blf,df->bld', y, w2) + b2_
                return (h + y, None)
            xs = (ln1_w, ln1_b, phz_re, phz_im, lc_re, lc_im, sc_lin, ln2_w, ln2_b, W1, b1, W2, b2)
            h, _ = jax.lax.scan(body, h, xs)
            h = layernorm(h, lnl_w, lnl_b)
            return jnp.einsum('bld,vd->blv', h, Wout) + bout
        return _forward(x, Win, bin, ln1_w, ln1_b, phz_re, phz_im, lc_re, lc_im, sc_lin, ln2_w, ln2_b, W1, b1, W2, b2, lnl_w, lnl_b, Wout, bout)

    def _L0_ffn_ref(x, weight, lora_A, lora_B, gw1, gb1, ln_gamma, ln_beta, gw2, gb2):
        import jax, jax.numpy as jnp
        import numpy as np
        B, S, IN, OUT = (4, 256, 512, 512)
        E, K, R = (8, 2, 16)
        CAP_FACTOR = 3.0
        ALPHA = 1.0 / R
        LN_EPS = 1e-05
        orig_shape = x.shape
        xf = x.reshape(-1, orig_shape[-1])
        N = xf.shape[0]
        capacity = int(CAP_FACTOR * N / E)
        h = xf @ gw1.T + gb1
        mu = jnp.mean(h, axis=-1, keepdims=True)
        var = jnp.mean((h - mu) ** 2, axis=-1, keepdims=True)
        h = (h - mu) * jax.lax.rsqrt(var + LN_EPS) * ln_gamma + ln_beta
        h = jax.nn.relu(h)
        gates = h @ gw2.T + gb2
        top_v, top_i = jax.lax.top_k(gates, K)
        top_g = jax.nn.softmax(top_v, axis=-1)
        onehot = (top_i[..., None] == jnp.arange(E)).astype(xf.dtype)
        counts = onehot.sum(axis=0)
        allowed = (counts <= capacity).astype(xf.dtype)
        w = jnp.einsum('nke,nk,ke->ne', onehot, top_g, allowed)
        main = xf @ weight.T
        tmp = jnp.einsum('ni,eir->enr', xf, lora_A)
        tmp = tmp * w.T[:, :, None]
        lora = jnp.einsum('enr,ero->no', tmp, lora_B) * ALPHA
        out = main + lora
        return out.reshape(*orig_shape[:-1], weight.shape[0])

    def _L1_attn_ref(x, w_q, w_k, w_v, w_o):
        import jax, jax.numpy as jnp
        import numpy as np
        HIDDEN = 512
        HEADS = 32
        D_K = HIDDEN // HEADS
        B, S, _ = x.shape

        def proj(w):
            y = jnp.einsum('bsd,ed->bse', x, w)
            return y.reshape(B, S, HEADS, D_K).transpose(0, 2, 1, 3)
        q, k, v = (proj(w_q), proj(w_k), proj(w_v))
        scores = jnp.einsum('bhqd,bhkd->bhqk', q, k) / jnp.sqrt(jnp.float32(D_K))
        attn = jax.nn.softmax(scores, axis=-1)
        out = jnp.einsum('bhqk,bhkd->bhqd', attn, v)
        out = out.transpose(0, 2, 1, 3).reshape(B, S, HIDDEN)
        return jnp.einsum('bse,oe->bso', out, w_o)

    def _L1_ffn_ref(x, gate_w, gate_scale, up_w, up_scale, down_w, down_scale):
        import jax, jax.numpy as jnp
        import numpy as np
        THRESH_FACTOR = 0.7

        def _bitlinear(x, w, scale):
            w_abs = jnp.abs(w)
            thr = jnp.mean(w_abs) * THRESH_FACTOR
            wq = jnp.sign(w) * (w_abs > thr).astype(w.dtype)
            w_scaled = wq * scale
            return jnp.einsum('bsd,od->bso', x, w_scaled)
        gate = _bitlinear(x, gate_w, gate_scale)
        up = _bitlinear(x, up_w, up_scale)
        hidden = jax.nn.silu(gate) * up
        out = _bitlinear(hidden, down_w, down_scale)
        return out
    x = L0_attn_x
    x = _layernorm(x + _L0_attn_ref(x, L0_attn_Win, L0_attn_bin, L0_attn_ln1_w, L0_attn_ln1_b, L0_attn_phz_re, L0_attn_phz_im, L0_attn_lc_re, L0_attn_lc_im, L0_attn_sc_lin, L0_attn_ln2_w, L0_attn_ln2_b, L0_attn_W1, L0_attn_b1, L0_attn_W2, L0_attn_b2, L0_attn_lnl_w, L0_attn_lnl_b, L0_attn_Wout, L0_attn_bout), axis=-1)
    x = _layernorm(x + _L0_ffn_ref(x, L0_ffn_weight, L0_ffn_lora_A, L0_ffn_lora_B, L0_ffn_gw1, L0_ffn_gb1, L0_ffn_ln_gamma, L0_ffn_ln_beta, L0_ffn_gw2, L0_ffn_gb2), axis=-1)
    x = _layernorm(x + _L1_attn_ref(x, L1_attn_w_q, L1_attn_w_k, L1_attn_w_v, L1_attn_w_o), axis=-1)
    x = _layernorm(x + _L1_ffn_ref(x, L1_ffn_gate_w, L1_ffn_gate_scale, L1_ffn_up_w, L1_ffn_up_scale, L1_ffn_down_w, L1_ffn_down_scale), axis=-1)
    return x

_drawn_inputs = setup_inputs


def setup_inputs(seed=0):
    import zlib

    import numpy as np

    out = dict(_drawn_inputs(seed))
    spreads = {'L0_attn_bin': (0.0, 0.1),
     'L0_attn_ln1_w': (1.0, 0.2),
     'L0_attn_ln1_b': (0.0, 0.1),
     'L0_attn_sc_lin': (1.0, 0.2),
     'L0_attn_ln2_w': (1.0, 0.2),
     'L0_attn_ln2_b': (0.0, 0.1),
     'L0_attn_b1': (0.0, 0.1),
     'L0_attn_b2': (0.0, 0.1),
     'L0_attn_lnl_w': (1.0, 0.2),
     'L0_attn_lnl_b': (0.0, 0.1),
     'L0_attn_bout': (0.0, 0.1),
     'L0_ffn_gb1': (0.0, 0.778),
     'L0_ffn_ln_gamma': (1.0, 0.6),
     'L0_ffn_ln_beta': (0.0, 0.8),
     'L0_ffn_gb2': (0.0, 0.334),
     'L1_ffn_gate_scale': (1.0, 0.2),
     'L1_ffn_up_scale': (1.0, 0.2),
     'L1_ffn_down_scale': (1.0, 0.2)}
    factors = {'L0_ffn_lora_A': 3.188,
     'L0_ffn_lora_B': 3.156,
     'L0_ffn_gw1': 3.727,
     'L0_ffn_gw2': 3.97,
     'L1_attn_w_q': 2.833,
     'L1_attn_w_k': 2.735}
    for name, (base, spread) in spreads.items():
        noise = np.random.default_rng([zlib.crc32(name.encode()), seed]).standard_normal(out[name].shape)
        drawn = base * np.exp(spread * noise) if base else spread * noise
        out[name] = jnp.asarray(drawn.astype(out[name].dtype))
    for name, factor in factors.items():
        out[name] = (out[name] * factor).astype(out[name].dtype)
    return out
```

```python
import numpy as np
from contextlib import ExitStack

import concourse.bass as bass
from concourse import mybir
from concourse.alu_op_type import AluOpType as ALU

ACT = mybir.ActivationFunctionType
AX = mybir.AxisListType
F32 = mybir.dt.float32
F32R = mybir.dt.float32r
BF16 = mybir.dt.bfloat16

P = 128
B, L, D = 2, 1024, 512
TOK = B * L
KC = D // P
NT = TOK // P
HALF = L // 2
NL, DH, DFF = 4, 64, 256
FC = DFF // DH
NE, ER = 8, 16
NG = 4 * NE
CAPACITY = int(3.0 * TOK / NE)
NH, DK = 32, 16
GH = 4
NGRP = B * NH // GH
KT = L // P
HID = 2048
HC = HID // P
EPS = 1e-5
THRESH = 0.7

C_ID, C_CEN, C_ONE, C_BLK, C_REV = 0, P, 2 * P, 3 * P, 3 * P + 2
C_END = C_REV + NE
(Q_L1W, Q_L1B, Q_RE, Q_IM, Q_LR, Q_LI, Q_SCL, Q_L2W, Q_L2B, Q_B2, Q_BIN, Q_LNW, Q_LNB) = range(0, 52, 4)
Q_B1 = 52
Q_GS = Q_B1 + NL * FC
Q_US = Q_GS + HC
Q_END = Q_US + HC
R_BOUT, R_DS = 0, D
R_GB1 = 2 * D
R_GAM, R_BET, R_GB2 = R_GB1 + NG, R_GB1 + 2 * NG, R_GB1 + 3 * NG
R_END = R_GB2 + NE


class Chain:

    def __init__(self, engine, sem):
        self.engine, self.sem, self.base, self.n = engine, sem, 0, 0

    def step(self, instruction):
        instruction.then_inc(self.sem, 1)
        self.n += 1
        self.engine.wait_ge(self.sem, self.base + self.n)


def build(nc, x_tok, x_feat, win, w1, w2, wout, main_w, ag_w, lora_b, gw2, wqkv, wo, tern, consts, pcol, prow, out):
    ctx = ExitStack()
    with ctx:
        sem = lambda name: ctx.enter_context(nc.semaphore(name))
        sems = lambda name, n=2: [sem(f"{name}{i}") for i in range(n)]

        def sb(stack, name, shape, dt=F32):
            return stack.enter_context(nc.sbuf_tensor(name, shape, dt))

        psum = ctx.enter_context(nc.psum_tensor("psum", [P, 8, 512], F32))

        cst = sb(ctx, "cst", [P, C_END])
        pc = sb(ctx, "pc", [P, Q_END])
        pr = sb(ctx, "pr", [P, R_END])
        mhalf = sb(ctx, "mhalf", [P, NT])
        ident = cst[:, C_ID:C_ID + P]
        center = cst[:, C_CEN:C_CEN + P]
        ones = cst[:, C_ONE:C_ONE + P]
        blk_mean = cst[:, C_BLK:C_BLK + 2]
        rev = cst[:, C_REV:C_REV + NE]
        stats = sb(ctx, "stats", [P, 4, 6])
        mv = sb(ctx, "mv", [P, NT, 2])
        varr = sb(ctx, "varr", [P, NT])
        rstd = sb(ctx, "rstd", [P, NT])
        thr = sb(ctx, "thr", [P, 3])
        nthr = sb(ctx, "nthr", [P, 3])

        ab = ExitStack()
        xres = sb(ab, "xres", [P, NT, D])
        y = [sb(ab, f"y{s}", [P, HALF]) for s in range(2)]
        wout_sb = sb(ab, "wout_sb", [P, B, D])
        main_sb = sb(ab, "main_sb", [P, KC, D])
        ag_sb = sb(ab, "ag_sb", [P, KC, P + NG])
        lorab_sb = sb(ab, "lorab_sb", [P, D])
        gw2_sb = sb(ab, "gw2_sb", [P, 4, NE])
        sa = ExitStack()
        xt = sb(sa, "xt", [P, KC, TOK])
        win_sb = sb(sa, "win_sb", [P, KC, DH])
        cos = sb(sa, "cos", [P, NL, L])
        sin = sb(sa, "sin", [P, NL, L])
        tab1 = sb(sa, "tab1", [P, NL, HALF])
        tab2 = sb(sa, "tab2", [P, NL, HALF])
        pw = sb(sa, "pw", [P, 16, NL])
        w1bd = sb(sa, "w1bd", [P, FC, P])
        w2bd = sb(sa, "w2bd", [P, FC, P])
        h = sb(sa, "h", [P, 2, HALF])
        half = lambda name, n=HALF: [sb(sa, f"{name}{s}", [P, n]) for s in range(2)]
        hc, sq, z = half("hc"), half("sq"), half("z")
        re_in, im_in, zr, zi, re_p, im_p = (half(n) for n in ("re_in", "im_in", "zr", "zi", "re_p", "im_p"))
        g = [sb(sa, f"g{s}", [P, FC, HALF]) for s in range(2)]
        var8, rstd8 = half("var8", 8), half("rstd8", 8)
        sa.close()
        xts = ExitStack()
        x1t = sb(xts, "x1t", [P, KC, TOK])
        sbk = ExitStack()
        lg = sb(sbk, "lg", [P, NT, P + NG])
        gh = sb(sbk, "gh", [P, NT, NG])
        gsq = sb(sbk, "gsq", [P, NT, NG])
        ght = sb(sbk, "ght", [P, 4, P])
        gs = sb(sbk, "gs", [P, 10, NT])
        ge = sb(sbk, "ge", [P, 6, NT, NE])
        oh = sb(sbk, "oh", [P, 2, NT, NE])
        cnt = sb(sbk, "cnt", [P, 2, NE])
        wexp = sb(sbk, "wexp", [P, NT, NE])
        tmpw = sb(sbk, "tmpw", [P, NT, P])
        tmpwt = sb(sbk, "tmpwt", [P, NT, P])
        sbk.close()
        sq_ = ExitStack()
        wqkv_sb = sb(sq_, "wqkv_sb", [P, 3 * KC, D])
        parts = [sb(sq_, f"parts{i}", [P, 3, L], BF16) for i in range(2)]
        resid = [sb(sq_, f"resid{i}", [P, L]) for i in range(2)]
        vpad = [sb(sq_, f"vpad{i}", [P, NH, 2 * DK]) for i in range(2)]
        wabs = sb(sq_, "wabs", [P, 2, L])
        absum = sb(sq_, "absum", [P, 3 * 8])
        absum3 = sb(sq_, "absum3", [P, 3])
        sq_.close()
        xts.close()
        ab.close()
        cd = ExitStack()
        tern_sb = sb(cd, "tern_sb", [P, 24, L], F32R)
        at = ExitStack()
        qst = [sb(at, f"qst{i}", [P, GH, L], BF16) for i in range(3)]
        kst = [sb(at, f"kst{i}", [P, GH, L], BF16) for i in range(3)]
        vg = [sb(at, f"vg{i}", [P, KT, GH * 2 * DK]) for i in range(3)]
        NP = 6
        probs = [sb(at, f"probs{i}", [P, L]) for i in range(NP)]
        o_sb = sb(at, "o_sb", [P, L])
        wraw = sb(at, "wraw", [P, L])
        wpos = sb(at, "wpos", [P, L])
        mx = [sb(at, f"mx{i}", [P, GH, KT, 2]) for i in range(2)]
        nm = sb(at, "nm", [P, GH * KT])
        nmh = sb(at, "nmh", [GH * KT, P], BF16)
        nml = sb(at, "nml", [GH * KT, P], BF16)
        at.close()
        x3s = ExitStack()
        x3h = sb(x3s, "x3h", [P, KC, TOK], F32R)
        x3l = sb(x3s, "x3l", [P, KC, TOK], F32R)
        op = ExitStack()
        wo_sb = sb(op, "wo_sb", [P, KC, D])
        rb = sb(op, "rb", [P, KC, HALF])
        od = [sb(op, f"od{k}", [P, KC, P]) for k in range(4)]
        x3t = [sb(op, f"x3t{k}", [P, D]) for k in range(8)]
        den_sb = od[0]
        op.close()
        ff = ExitStack()
        hh = [sb(ff, f"hh{k}", [P, HALF], F32R) for k in range(2)]
        hl = [sb(ff, f"hl{k}", [P, HALF], F32R) for k in range(2)]
        sg = [sb(ff, f"sg{k}", [P, HALF]) for k in range(2)]
        hid = [sb(ff, f"hid{k}", [P, HALF]) for k in range(2)]
        yt = sb(ff, "yt", [P, 4, D])
        xin = sb(ff, "xin", [P, 4, D])
        ff.close()
        x3s.close()
        cd.close()

        ps_c = [psum[:, s, :] for s in range(2)]
        ps_b = [psum[:, 2 + s, :] for s in range(2)]
        ps_f = [[psum[:, 4 + 2 * s + k, :] for k in range(2)] for s in range(2)]

        ld_const, ld_x, ld_win, ld_wout = sem("ld_const"), sems("ld_x"), sem("ld_win"), sem("ld_wout")
        ld_xres = sem("ld_xres")
        zeroed, ld_w = sem("zeroed"), sem("ld_w")
        dve_chain, pool_chain, act_chain = sem("dve_chain"), sem("pool_chain"), sem("act_chain")
        mag2_ready, invm_ready, mag_ready, decay_ready = sem("mag2_ready"), sem("invm_ready"), sem("mag_ready"), sem("decay_ready")
        tables_ready = sem("tables_ready")
        inproj = sems("inproj")
        h_ready, centered, squared, hc_copied = sems("h_ready"), sems("centered"), sems("squared"), sems("hc_copied")
        var_sums, var_ready, rstd_ready = sems("var_sums"), sems("var_ready"), sems("rstd_ready")
        spread, z_ready, y_ready, yn_ready = sems("spread"), sems("z_ready"), sems("y_ready"), sems("yn_ready")
        im_in_ready, zi_ready, im_p_ready = sems("im_in_ready"), sems("zi_ready"), sems("im_p_ready")
        up_done, g_ready, down_done = sems("up_done"), sems("g_ready"), sems("down_done")
        ld_bw = sem("ld_bw")
        xres_biased = sem("xres_biased")
        proj_done, var4_ready, rstd4_ready, tile_ready = sem("proj_done"), sem("var4_ready"), sem("rstd4_ready"), sem("tile_ready")
        tr_done, xt_ready, lg_done, lg_ready = sem("tr_done"), sem("xt_ready"), sem("lg_done"), sem("lg_ready")
        gvar_ready, grstd_ready, gh_ready, ght_done, ght_ready = (sem(n) for n in ("gvar_ready", "grstd_ready", "gh_ready", "ght_done", "ght_ready"))
        gates_done, gap_ready, gexp_ready, oh_ready, cnt_done = (sem(n) for n in ("gates_done", "gap_ready", "gexp_ready", "oh_ready", "cnt_done"))
        tmpw_ready, wtr_done, tmpwt_ready = sem("tmpw_ready"), sem("wtr_done"), sem("tmpwt_ready")
        bproj_done, added = sem("bproj_done"), sem("added")
        st_x2 = sem("st_x2")
        ld_qkv, hi_ready, r1_ready, mid_ready, lo_ready, qk_done = (sem(n) for n in ("ld_qkv", "hi_ready", "r1_ready", "mid_ready", "lo_ready", "qk_done"))
        v_done, v_ready, vpad_ready = (sem(n) for n in ("v_done", "v_ready", "vpad_ready"))
        st_parts, st_v, ld_abs = sems("st_parts"), sems("st_v"), sems("ld_abs")
        abs_done, abs_sum, abs_all, thr_ready = (sem(n) for n in ("abs_done", "abs_sum", "abs_all", "thr_ready"))
        ld_stack, ld_v, ld_nm = sems("ld_stack", 3), sems("ld_v", 3), sems("ld_nm", 3)
        ones_ready, mx_done, mx_read, nm_ready, nmt_done, nmt_read = (sem(n) for n in ("ones_ready", "mx_done", "mx_read", "nm_ready", "nmt_done", "nmt_read"))
        nmh_ready = sem("nmh_ready")
        score_done, exp_done, pv_done, o_ready, st_o = (sem(n) for n in ("score_done", "exp_done", "pv_done", "o_ready", "st_o"))
        st_nm = sem("st_nm")
        ld_tern = sem("ld_tern")
        tern_chain = sem("tern_chain")
        qk_dram = nc.dram_tensor("qk_dram", [2, 3, B * D, L], BF16).ap()
        v_dram = nc.dram_tensor("v_dram", [NGRP, L, GH * 2 * DK], F32).ap()
        nm_dram = nc.dram_tensor("nm_dram", [2, GH * KT, P], BF16).ap()
        o_dram = nc.dram_tensor("o_dram", [B * D, L], F32).ap()
        den_dram = nc.dram_tensor("den_dram", [B * NH, L], F32).ap()
        x2_dram = nc.dram_tensor("x2_dram", [TOK, D], F32).ap()
        rec_dram = nc.dram_tensor("rec_dram", [B * NH, L], F32).ap()
        x3_dram = nc.dram_tensor("x3_dram", [TOK, D], F32).ap()
        ld_den, den_ready, st_rec = (sem(n) for n in ("ld_den", "den_ready", "st_rec"))
        ld_rb, normed, oproj_done = sem("ld_rb"), sem("normed"), sem("oproj_done")
        ld_od, ld_x2t, st_x3 = sems("ld_od"), sems("ld_x2t"), sem("st_x3")
        x_added, x_stats, x_mv, x_var, x_rstd, x3_ready = (sem(n) for n in ("x_added", "x_stats", "x_mv", "x_var", "x_rstd", "x3_ready"))
        x3_tr, x3h_ready, x3l_ready = sem("x3_tr"), sem("x3h_ready"), sem("x3l_ready")
        gate_up_done, silu_ready, hid_ready, hh_ready, hl_ready = (sem(n) for n in ("gate_up_done", "silu_ready", "hid_ready", "hh_ready", "hl_ready"))
        ffn_done, yt_ready, ld_xin, st_out = sem("ffn_done"), sem("yt_ready"), sem("ld_xin"), sem("st_out")
        f_added, out_ready = sem("f_added"), sem("out_ready")

        Q_PART, K_PART = (0, 0, 1, 0, 2, 1), (0, 1, 0, 2, 0, 1)
        SR = 6 * DK

        def over_groups(engine, body):
            body(0, 0)
            with engine.Fori(0, (NGRP - 4) // 3) as i:
                for c in range(1, 4):
                    body(i, c)
            for g in range(NGRP - 3, NGRP):
                body(0, g)

        def at_least(engine, semaphore, i, per, c):
            wait_for(engine, semaphore, i * per + c)

        def wait_for(engine, semaphore, count):
            if not isinstance(count, int) or count > 0:
                engine.wait_ge(semaphore, count)

        def ahead(engine):
            engine.wait_ge(ld_const, 48)

        block = ctx.enter_context(nc.Block())

        @block.sync
        def _(sp):
            sp.dma_start(pc[:, :], pcol).then_inc(ld_const, 16)
            sp.dma_start(cst[:, :], consts).then_inc(ld_const, 16)
            sp.dma_start(pr[:, :], prow).then_inc(ld_const, 16)
            sp.dma_start(win_sb[:, :, :], win.rearrange("(k p) d -> p k d", p=P)).then_inc(ld_win, 16)
            xf = x_feat.rearrange("(k p) t -> p k t", p=P)
            for s in range(2):
                for b in range(B):
                    t0 = b * L + s * HALF
                    sp.dma_start(xt[:, :, t0:t0 + HALF], xf[:, :, t0:t0 + HALF]).then_inc(ld_x[s], 16)

            def load_layer(i):
                for b in range(B):
                    r = slice(DH * b, DH * b + DH)
                    sp.dma_start(w1bd[r, :, r], w1[i].rearrange("d (c f) -> d c f", c=FC)).then_inc(ld_w, 16)
                    sp.dma_start(w2bd[r, :, r], w2[i].rearrange("(c f) d -> f c d", c=FC)).then_inc(ld_w, 16)

            sp.wait_ge(zeroed, 4)
            load_layer(0)
            for b in range(B):
                sp.dma_start(wout_sb[DH * b:DH * b + DH, b, :], wout).then_inc(ld_wout, 16)
            sp.dma_start(xres[:, :, :], x_tok.rearrange("(t p) d -> p t d", p=P)).then_inc(ld_xres, 16)
            sp.dma_start(main_sb[:, :, :], main_w.rearrange("(k p) n -> p k n", p=P)).then_inc(ld_bw, 16)
            sp.dma_start(ag_sb[:, :, :], ag_w.rearrange("(k p) n -> p k n", p=P)).then_inc(ld_bw, 16)
            sp.dma_start(lorab_sb[:, :], lora_b).then_inc(ld_bw, 16)
            for t in range(4):
                sp.dma_start(gw2_sb[NG * t:NG * t + NG, t, :], gw2).then_inc(ld_bw, 16)
            with sp.Fori(1, NL) as i:
                for s in range(2):
                    sp.wait_ge(down_done[s], i)
                for b in range(B):
                    r = slice(DH * b, DH * b + DH)
                    sp.dma_start(w1bd[r, :, r], w1[bass.ds(i, 1)].rearrange("o d (c f) -> (o d) c f", c=FC)).then_inc(ld_w, 16)
                    sp.dma_start(w2bd[r, :, r], w2[bass.ds(i, 1)].rearrange("o (c f) d -> (o f) c d", c=FC)).then_inc(ld_w, 16)
            for q in range(4):
                sp.wait_ge(tile_ready, NT + 4 * q + 4)
                sp.dma_start(x2_dram.rearrange("(t p) d -> p t d", p=P)[:, 4 * q:4 * q + 4, :], xres[:, 4 * q:4 * q + 4, :]).then_inc(st_x2, 16)
            sp.dma_start(wqkv_sb[:, :, :], wqkv.rearrange("w (k p) n -> p (w k) n", p=P)).then_inc(ld_qkv, 16)
            for t in range(NT):
                sp.wait_ge(v_ready, t + 1)
                b, t0 = t // KT, t % KT * P
                dst = v_dram[b * NGRP // B:(b + 1) * NGRP // B, t0:t0 + P, :].rearrange("g p n -> p g n")
                sp.dma_start(dst, vpad[t % 2][:, :, :].rearrange("p (g j) e -> p g (j e)", j=GH)).then_inc(st_v[t % 2], 16)
            for u in range(16):
                b, w, c = u // 8, u // 4 % 2, u % 4
                sp.wait_ge(lo_ready, u + 1)
                r0 = b * D + P * c
                sp.dma_start(qk_dram[w, :, r0:r0 + P, :].rearrange("n p t -> p n t"), parts[u % 2][:, :, :]).then_inc(st_parts[u % 2], 16)

            def load_stack(i, c):
                rows = lambda w, n: qk_dram[w, n].rearrange("(g j d) t -> g d j t", j=GH, d=DK)[i * 3 + c] if isinstance(i, int) else \
                    qk_dram[w, n].rearrange("(g j d) t -> g d j t", j=GH, d=DK)[bass.ds(i * 3 + c, 1)].rearrange("o d j t -> (o d) j t")
                for st, w, order in ((qst, 0, Q_PART), (kst, 1, K_PART)):
                    for m, n in enumerate(order):
                        sp.dma_start(st[c % 3][DK * m:DK * m + DK, :, :], rows(w, n)).then_inc(ld_stack[c % 3], 16)

            def load_v(i, c):
                src = v_dram[bass.ds(i * 3 + c, 1)].rearrange("o (k p) n -> p (o k) n", p=P)
                sp.dma_start(vg[c % 3][:, :, :], src).then_inc(ld_v[c % 3], 16)

            for k in range(2):
                sp.wait_ge(st_parts[k], 128)
            for k in range(2):
                sp.wait_ge(st_v[k], 128)
            sp.wait_ge(thr_ready, 1)
            for c in range(2):
                load_stack(0, c)
                load_v(0, c)

            def store_o(i, c):
                at_least(sp, o_ready, i, 3, c + 1)
                for j in range(GH):
                    r0 = (i * 3 + c) * (GH * DK) + DK * j
                    sp.dma_start(o_dram[bass.ds(r0, DK), :], o_sb[2 * DK * j:2 * DK * j + DK, :]).then_inc(st_o, 16)
                    sp.dma_start(den_dram[bass.ds((i * 3 + c) * GH + j, 1), :], o_sb[2 * DK * j + DK:2 * DK * j + DK + 1, :]).then_inc(st_o, 16)

            def load_nm(i, c):
                at_least(sp, nmt_read, i, 3, c + 1)
                for r, src in ((0, nmh), (1, nml)):
                    sp.dma_start(nm_dram[r], src[:, :]).then_inc(st_nm, 16)
                at_least(sp, st_nm, i, 3 * 32, 32 * (c + 1))
                sp.dma_start(qst[c % 3][SR:SR + 2, :, :].rearrange("r j t -> r (j t)"), nm_dram.rearrange("r p t -> r (p t)")).then_inc(ld_nm[c % 3], 16)

            load_nm(0, 0)

            def group(i, c):
                last = isinstance(i, int) and 3 * i + c + 2 >= NGRP
                if not last:
                    at_least(sp, score_done, i, 96, 32 * c)
                    load_stack(i, c + 2)
                if not (isinstance(i, int) and 3 * i + c == 0):
                    store_o(i, c - 1)
                if not last:
                    at_least(sp, pv_done, i, 24, 8 * c)
                    load_v(i, c + 2)
                if not (isinstance(i, int) and 3 * i + c + 1 >= NGRP):
                    load_nm(i, c + 1)

            over_groups(sp, group)
            store_o(0, NGRP - 1)
            sp.wait_ge(st_o, 128 * NGRP)
            sp.wait_ge(score_done, 32 * NGRP)
            sp.wait_ge(exp_done, 32 * NGRP)
            sp.wait_ge(pv_done, KT * NGRP)
            sp.wait_ge(tern_chain, 72)
            sp.wait_ge(nmt_read, NGRP)
            sp.dma_start(den_sb[:, :, :].rearrange("p k t -> p (k t)"), den_dram.rearrange("n (a t) -> (n a) t", a=2)).then_inc(ld_den, 16)
            sp.dma_start(wo_sb[:, :, :], wo.rearrange("(k p) n -> p k n", p=P)).then_inc(ld_qkv, 16)
            sp.wait_ge(den_ready, 1)
            sp.dma_start(rec_dram.rearrange("n (a t) -> (n a) t", a=2), den_sb[:, :, :].rearrange("p k t -> p (k t)")).then_inc(st_rec, 16)

            def load_attn(q):
                b, a = q // 2, q % 2
                for k in range(4):
                    if q == 0 and k == 0:
                        sp.wait_ge(st_rec, 16)
                    elif q > 0:
                        sp.wait_ge(oproj_done, 4 * q - 4 + k + 1)
                    t0 = a * HALF + k * P
                    sp.dma_start(od[k][:, :, :], o_dram[b * D:b * D + D, t0:t0 + P].rearrange("(k p) t -> p k t", p=P)).then_inc(ld_od[q % 2], 16)
                if q > 0:
                    sp.wait_ge(normed, 4 * q)
                for k in range(KC):
                    h0, n = b * NH + k * (NH // KC), NH // KC
                    sp.dma_start(rb[:, k, :], rec_dram[h0:h0 + n, a * HALF:a * HALF + HALF].unsqueeze(1).to_broadcast([n, DK, HALF])).then_inc(ld_rb, 16)
                if q >= 2:
                    sp.wait_ge(st_x3, 64 * (q - 1))
                for k in range(4):
                    t, slot = 4 * q + k, 4 * (q % 2) + k
                    if q >= 2:
                        sp.wait_ge(x3_tr, t - 8 + 1)
                    sp.dma_start(x3t[slot][:, :], x2_dram[P * t:P * t + P, :]).then_inc(ld_x2t[q % 2], 16)

            def store_x3(q):
                for k in range(4):
                    t, slot = 4 * q + k, 4 * (q % 2) + k
                    sp.wait_ge(x3_ready, t + 1)
                    sp.dma_start(x3_dram[P * t:P * t + P, :], x3t[slot][:, :]).then_inc(st_x3, 16)

            load_attn(0)
            load_attn(1)
            for q in range(4):
                store_x3(q)
                if q < 2:
                    load_attn(q + 2)
            sp.wait_ge(st_x3, 16 * NT)
            sp.wait_ge(x3_tr, NT)

            def write_out(n):
                wait_for(sp, f_added, n * 4)
                sp.dma_start(xin[:, :, :], x3_dram.rearrange("(n k p) d -> p n k d", p=P, k=4)[:, bass.ds(n, 1)].rearrange("p o k d -> p (o k) d")).then_inc(ld_xin, 16)
                for k in range(4):
                    sp.wait_ge(out_ready, n * 4 + k + 1)
                    sp.dma_start(out[bass.ds(n * HALF + k * P, P), :], yt[:, k, :]).then_inc(st_out, 16)

            write_out(0)
            with sp.Fori(1, 4) as n:
                write_out(n)
            sp.wait_ge(st_out, 16 * NT)

        @block.gpsimd
        def _(pool):
            nc.gpsimd.memset(mhalf[:, :], -0.5).then_inc(pool_chain, 1)
            pool.wait_ge(pool_chain, 1)
            pool.wait_ge(mag2_ready, 1)
            nc.gpsimd.tensor_tensor(pw[:, 3, :], pw[:, 2, :], mhalf[:, 0:NL], ALU.pow).then_inc(invm_ready, 1)

            def ln_rstd(n, s):
                pool.wait_ge(var_ready[s], n + 1)
                nc.gpsimd.tensor_tensor(rstd8[s][:, :], var8[s][:, :], mhalf[:, 0:8], ALU.pow).then_inc(rstd_ready[s], 1)

            pool.wait_ge(ld_const, 48)
            pool.wait_ge(ld_xres, 16)
            nc.gpsimd.tensor_tensor(xres[:, :, :], xres[:, :, :], pr[:, R_BOUT:R_BOUT + D].unsqueeze(1).to_broadcast([P, NT, D]), ALU.add).then_inc(xres_biased, 1)
            with pool.Fori(0, NL) as i:
                for s in range(2):
                    ln_rstd(i * 2, s)
                for s in range(2):
                    sl = slice(s * HALF, s * HALF + HALF)
                    ahead(pool)
                    pool.wait_ge(y_ready[s], i + 1)
                    nc.gpsimd.tensor_tensor(im_in[s][:, :], sin[:, bass.ds(i, 1), sl].rearrange("p o t -> p (o t)"), y[s][:, :], ALU.mult).then_inc(im_in_ready[s], 1)
                for s in range(2):
                    sl = slice(s * HALF, s * HALF + HALF)
                    ahead(pool)
                    pool.wait_ge(zi_ready[s], i + 1)
                    nc.gpsimd.tensor_tensor(im_p[s][:, :], sin[:, bass.ds(i, 1), sl].rearrange("p o t -> p (o t)"), zi[s][:, :], ALU.mult).then_inc(im_p_ready[s], 1)
                for s in range(2):
                    ln_rstd(i * 2 + 1, s)
            for s in range(2):
                ln_rstd(2 * NL, s)

            def rstd_tiles(r):
                for q in range(4):
                    sl = slice(4 * q, 4 * q + 4)
                    pool.wait_ge(var4_ready, 4 * r + q + 1)
                    nc.gpsimd.tensor_tensor(rstd[:, sl], varr[:, sl], mhalf[:, sl], ALU.pow).then_inc(rstd4_ready, 1)

            rstd_tiles(0)
            pool.wait_ge(gvar_ready, 1)
            nc.gpsimd.tensor_tensor(gs[:, 2, :], gs[:, 1, :], mhalf[:, :], ALU.pow).then_inc(grstd_ready, 1)
            rstd_tiles(1)

            for c in range(24):
                if c >= 2:
                    pool.wait_ge(abs_done, c - 1)
                elif c == 0:
                    pool.wait_ge(tile_ready, 2 * NT)
                    pool.wait_ge(tmpwt_ready, 4)
                pool.dma_start(wabs[:, c % 2, :], tern[c]).then_inc(ld_abs[c % 2], 16)
            pool.wait_ge(thr_ready, 1)
            for k in range(2):
                pool.wait_ge(st_parts[k], 128)
            pch = Chain(pool, tern_chain)
            for c in range(24):
                w = c // 8
                pool.dma_start(wraw[:, :], tern[c]).then_inc(ld_tern, 16)
                pool.wait_ge(ld_tern, 16 * c + 16)
                pch.step(nc.gpsimd.tensor_scalar(wpos[:, :], wraw[:, :], thr[:, w:w + 1], None, ALU.is_gt))
                pch.step(nc.gpsimd.tensor_scalar(wraw[:, :], wraw[:, :], nthr[:, w:w + 1], None, ALU.is_lt))
                pch.step(nc.gpsimd.tensor_tensor(tern_sb[:, c, :], wpos[:, :], wraw[:, :], ALU.subtract))
            for r, applied in ((0, x3_ready), (4, out_ready)):
                for q in range(4):
                    pool.wait_ge(x_var, q + r + 1)
                    wait_for(pool, applied, q * 4)
                    nc.gpsimd.tensor_tensor(rstd[:, 0:4], varr[:, 0:4], mhalf[:, 0:4], ALU.pow).then_inc(x_rstd, 1)

        @block.scalar
        def _(act):
            act.wait_ge(ld_const, 48)
            act.wait_ge(mag_ready, 1)
            nc.scalar.activation(pw[:, 5, :], pw[:, 4, :], ACT.Tanh).then_inc(decay_ready, 1)
            for s in range(2):
                act.wait_ge(inproj[s], 1)
                nc.scalar.activation(h[:, s, :], ps_c[s], ACT.Identity, bias=pc[:, Q_BIN:Q_BIN + 1]).then_inc(h_ready[s], 1)

            def ln_square(n, s):
                act.wait_ge(centered[s], n + 1)
                nc.scalar.activation(sq[s][:, :], ps_c[s], ACT.Square).then_inc(squared[s], 1)
                nc.scalar.activation(hc[s][:, :], ps_c[s], ACT.Copy).then_inc(hc_copied[s], 1)

            col = lambda base, i: pc[:, bass.ds(base + i, 1)]
            with act.Fori(0, NL) as i:
                for s in range(2):
                    ln_square(2 * i, s)
                for s in range(2):
                    ahead(act)
                    act.wait_ge(z_ready[s], 2 * i + 1)
                    nc.scalar.activation(y[s][:, :], z[s][:, :], ACT.Silu, bias=col(Q_L1B, i), scale=col(Q_L1W, i)).then_inc(y_ready[s], 1)
                for s in range(2):
                    ln_square(2 * i + 1, s)
                for s in range(2):
                    ahead(act)
                    act.wait_ge(z_ready[s], 2 * i + 2)
                    nc.scalar.activation(y[s][:, :], z[s][:, :], ACT.Identity, bias=col(Q_L2B, i), scale=col(Q_L2W, i)).then_inc(yn_ready[s], 1)
                for c in range(FC):
                    for s in range(2):
                        ahead(act)
                        act.wait_ge(up_done[s], FC * i + c + 1)
                        nc.scalar.activation(g[s][:, c, :], ps_f[s][c % 2], ACT.Silu, bias=pc[:, bass.ds(Q_B1 + i * FC + c, 1)]).then_inc(g_ready[s], 1)

            for s in range(2):
                ln_square(2 * NL, s)
            for s in range(2):
                act.wait_ge(z_ready[s], 2 * NL + 1)
                nc.scalar.activation(y[s][:, :], z[s][:, :], ACT.Identity, bias=pc[:, Q_LNB:Q_LNB + 1], scale=pc[:, Q_LNW:Q_LNW + 1]).then_inc(yn_ready[s], 1)

            def evac_x(n, t):
                act.wait_ge(tr_done, n + 1)
                nc.scalar.activation(x1t[:, :, P * t:P * t + P], psum[:, 4 + n % 2, :].rearrange("p (k t) -> p k t", k=KC), ACT.Copy).then_inc(xt_ready, 1)

            for t in range(NT):
                evac_x(t, t)
                if t >= 1:
                    act.wait_ge(lg_done, t)
                    nc.scalar.activation(lg[:, t - 1, :], psum[:, 6 + (t - 1) % 2, 0:P + NG], ACT.Copy).then_inc(lg_ready, 1)
            act.wait_ge(lg_done, NT)
            nc.scalar.activation(lg[:, NT - 1, :], psum[:, 6 + (NT - 1) % 2, 0:P + NG], ACT.Copy).then_inc(lg_ready, 1)
            act.wait_ge(ght_done, 1)
            nc.scalar.activation(ght[:, :, :], psum[:, 4, :].rearrange("p (q t) -> p q t", q=4), ACT.Copy).then_inc(ght_ready, 1)
            act.wait_ge(gap_ready, 1)
            nc.scalar.activation(gs[:, 5, :], gs[:, 4, :], ACT.Exp).then_inc(gexp_ready, 1)
            for q in range(4):
                act.wait_ge(wtr_done, q + 1)
                nc.scalar.activation(tmpwt[:, 4 * q:4 * q + 4, :], psum[:, 6 + q % 2, :].rearrange("p (t n) -> p t n", t=4), ACT.Copy).then_inc(tmpwt_ready, 1)
                if q >= 1:
                    for t in range(4 * q - 4, 4 * q):
                        evac_x(NT + t, t)
            for t in range(NT - 4, NT):
                evac_x(NT + t, t)

            def abs_chunk(c):
                act.wait_ge(ld_abs[c % 2], 16 * (c // 2) + 16)
                nc.scalar.activation(wabs[:, c % 2, :], wabs[:, c % 2, :], ACT.Abs, accum_out=absum[:, c:c + 1]).then_inc(abs_done, 1)

            act.wait_ge(vpad_ready, 4)
            for t in range(NT):
                act.wait_ge(v_done, t + 1)
                if t >= 2:
                    act.wait_ge(st_v[t % 2], 16 * (t // 2))
                nc.scalar.activation(vpad[t % 2][:, :, 0:DK], psum[:, 4 + t % 2, :].rearrange("p (h d) -> p h d", d=DK), ACT.Copy).then_inc(v_ready, 1)
                if t < 8:
                    abs_chunk(t)
            for u in range(17):
                if u < 16:
                    act.wait_ge(qk_done, u + 1)
                    if u >= 2:
                        act.wait_ge(st_parts[u % 2], 16 * (u // 2))
                    nc.scalar.activation(parts[u % 2][:, 0, :], psum[:, 2 * (u % 2):2 * (u % 2) + 2, :].rearrange("p a t -> p (a t)"), ACT.Copy).then_inc(hi_ready, 1)
                if u >= 1:
                    act.wait_ge(r1_ready, u)
                    nc.scalar.activation(parts[(u - 1) % 2][:, 1, :], resid[(u - 1) % 2][:, :], ACT.Copy).then_inc(mid_ready, 1)
                if u < 16:
                    abs_chunk(8 + u)

            def group(i, c):
                first = isinstance(i, int) and 3 * i + c == 0
                for n in range(4 * KT):
                    slot = (32 * c + n) % NP
                    at_least(act, score_done, i, 96, 32 * c + n + 1)
                    at_least(act, pv_done, i, 24, 8 * c + (n - NP) // 4 + 1)
                    nc.scalar.activation(probs[slot][:, :], psum[:, 2 * (n % 2):2 * (n % 2) + 2, :].rearrange("p a t -> p (a t)"), ACT.Exp, scale=DK ** -0.5).then_inc(exp_done, 1)
                    if n == 1 and not first:
                        copy_o(i, c - 1)

            def copy_o(i, c):
                at_least(act, pv_done, i, 24, 8 * c + 8)
                at_least(act, st_o, i, 3 * 128, 128 * c)
                nc.scalar.activation(o_sb[:, :], psum[:, 4:6, :].rearrange("p a t -> p (a t)"), ACT.Copy).then_inc(o_ready, 1)

            for k in range(2):
                act.wait_ge(st_v[k], 128)
            for k in range(2):
                act.wait_ge(st_parts[k], 128)
            act.wait_ge(thr_ready, 1)
            over_groups(act, group)
            copy_o(0, NGRP - 1)
            for t in range(NT):
                act.wait_ge(x3_tr, t + 1)
                nc.scalar.activation(x3h[:, :, P * t:P * t + P], psum[:, 4 + t % 4, :].rearrange("p (k t) -> p k t", k=KC), ACT.Copy).then_inc(x3h_ready, 1)
            act.wait_ge(x3l_ready, NT)

            def ffn_block(n):
                for f in range(HC):
                    act.wait_ge(gate_up_done, n * HC + f + 1)
                    wait_for(act, hid_ready, n * HC + f - 1)
                    nc.scalar.activation(sg[f % 2][:, :], psum[:, 4 + 2 * (f % 2), :], ACT.Silu, scale=pc[:, Q_GS + f:Q_GS + f + 1]).then_inc(silu_ready, 1)
                    act.wait_ge(hid_ready, n * HC + f + 1)
                    wait_for(act, ffn_done, n * HC + f - 1)
                    nc.scalar.activation(hh[f % 2][:, :], hid[f % 2][:, :], ACT.Copy).then_inc(hh_ready, 1)

            ffn_block(0)
            with act.Fori(1, 4) as n:
                ffn_block(n)

        @block.vector
        def _(dve):
            ch = Chain(dve, dve_chain)
            nc.vector.memset(w1bd[:, :, :], 0.0).then_inc(zeroed, 1)
            nc.vector.memset(w2bd[:, :, :], 0.0).then_inc(zeroed, 1)
            nc.vector.memset(wout_sb[:, :, :], 0.0).then_inc(zeroed, 1)
            nc.vector.memset(gw2_sb[:, :, :], 0.0).then_inc(zeroed, 1)
            nc.vector.memset(cos[:, :, 0:1], 1.0)
            nc.vector.memset(sin[:, :, 0:1], 0.0)
            dve.wait_ge(ld_const, 48)
            tt = lambda o, a, b_, op: ch.step(nc.vector.tensor_tensor(o, a, b_, op))
            ts = lambda o, a, s1, s2, o0, o1: ch.step(nc.vector.tensor_scalar(o, a, s1, s2, o0, o1))
            q = lambda base: pc[:, base:base + NL]
            w = lambda k: pw[:, k, :]
            tt(w(0), q(Q_RE), q(Q_RE), ALU.mult)
            tt(w(1), q(Q_IM), q(Q_IM), ALU.mult)
            tt(w(0), w(0), w(1), ALU.add)
            ts(w(8), w(0), 1e-30, None, ALU.is_ge, ALU.bypass)
            nc.vector.tensor_scalar(w(2), w(0), 1e-30, None, ALU.max).then_inc(mag2_ready, 1)
            dve.wait_ge(invm_ready, 1)
            nc.vector.tensor_tensor(w(4), w(2), w(3), ALU.mult).then_inc(mag_ready, 1)
            tt(w(9), w(3), w(8), ALU.mult)
            ts(w(10), w(8), -1.0, 1.0, ALU.mult, ALU.add)
            tt(w(6), q(Q_RE), w(9), ALU.mult)
            tt(w(6), w(6), w(10), ALU.add)
            tt(w(7), q(Q_IM), w(9), ALU.mult)
            tt(w(0), w(6), q(Q_LR), ALU.mult)
            tt(w(1), w(7), q(Q_LI), ALU.mult)
            tt(w(11), w(0), w(1), ALU.subtract)
            tt(w(0), w(6), q(Q_LI), ALU.mult)
            tt(w(1), w(7), q(Q_LR), ALU.mult)
            tt(w(0), w(0), w(1), ALU.add)
            ts(w(12), w(0), -1.0, None, ALU.mult, ALU.bypass)
            n = 1
            while n < L:
                bc = lambda k: w(k).unsqueeze(2).to_broadcast([P, NL, n])
                c0, s0, a, b_ = cos[:, :, 0:n], sin[:, :, 0:n], tab1[:, :, 0:n], tab2[:, :, 0:n]
                nc.vector.tensor_tensor(a, c0, bc(6), ALU.mult)
                tt(b_, s0, bc(7), ALU.mult)
                tt(cos[:, :, n:2 * n], a, b_, ALU.subtract)
                nc.vector.tensor_tensor(a, c0, bc(7), ALU.mult)
                tt(b_, s0, bc(6), ALU.mult)
                tt(sin[:, :, n:2 * n], a, b_, ALU.add)
                n *= 2
                if n < L:
                    tt(w(0), w(6), w(6), ALU.mult)
                    tt(w(1), w(7), w(7), ALU.mult)
                    tt(w(9), w(6), w(7), ALU.mult)
                    tt(w(6), w(0), w(1), ALU.subtract)
                    ts(w(7), w(9), 2.0, None, ALU.mult, ALU.bypass)
                    tt(w(0), w(6), w(6), ALU.mult)
                    tt(w(1), w(7), w(7), ALU.mult)
                    tt(w(0), w(0), w(1), ALU.add)
                    ts(w(0), w(0), -0.5, 1.5, ALU.mult, ALU.add)
                    tt(w(6), w(6), w(0), ALU.mult)
                    tt(w(7), w(7), w(0), ALU.mult)
            dve.wait_ge(decay_ready, 1)
            nc.vector.tensor_copy(w(13), w(5)).then_inc(tables_ready, 1)
            dve.wait_ge(tables_ready, 1)

            def ln_var(n, s):
                dve.wait_ge(var_sums[s], n + 1)
                nc.vector.tensor_scalar(var8[s][:, :], ps_b[s][:, 0:8], EPS, None, ALU.add).then_inc(var_ready[s], 1)

            def ln_scale(n, s):
                dve.wait_ge(spread[s], n + 1)
                dve.wait_ge(hc_copied[s], n + 1)
                nc.vector.tensor_tensor(z[s][:, :], ps_b[s], hc[s][:, :], ALU.mult).then_inc(z_ready[s], 1)

            start, PER = ch.n, 8
            with dve.Fori(0, NL) as i:
                ch.base, ch.n = start + i * PER, 0
                wcol = lambda k: pw[:, k, bass.ds(i, 1)]
                for s in range(2):
                    ln_var(2 * i, s)
                for s in range(2):
                    ln_scale(2 * i, s)
                for s in range(2):
                    sl = slice(s * HALF, s * HALF + HALF)
                    dve.wait_ge(y_ready[s], i + 1)
                    tt(re_in[s][:, :], cos[:, bass.ds(i, 1), sl].rearrange("p o t -> p (o t)"), y[s][:, :], ALU.mult)
                    first = wcol(11) if s == 0 else zr[0][:, HALF - 1:HALF]
                    ch.step(nc.vector.tensor_tensor_scan(zr[s][:, :], wcol(13).to_broadcast([P, HALF]), re_in[s][:, :], first, ALU.mult, ALU.add))
                    dve.wait_ge(im_in_ready[s], i + 1)
                    first = wcol(12) if s == 0 else zi[0][:, HALF - 1:HALF]
                    nc.vector.tensor_tensor_scan(zi[s][:, :], wcol(13).to_broadcast([P, HALF]), im_in[s][:, :], first, ALU.mult, ALU.add).then_inc(zi_ready[s], 1)
                    tt(re_p[s][:, :], cos[:, bass.ds(i, 1), sl].rearrange("p o t -> p (o t)"), zr[s][:, :], ALU.mult)
                    if s == 0:
                        dve.wait_ge(zi_ready[0], i + 1)
                for s in range(2):
                    dve.wait_ge(im_p_ready[s], i + 1)
                    tt(re_p[s][:, :], re_p[s][:, :], im_p[s][:, :], ALU.add)
                    nc.vector.scalar_tensor_tensor(h[:, s, :], re_p[s][:, :], pc[:, bass.ds(Q_SCL + i, 1)], h[:, s, :], ALU.mult, ALU.add).then_inc(h_ready[s], 1)
                for s in range(2):
                    ln_var(2 * i + 1, s)
                for s in range(2):
                    ln_scale(2 * i + 1, s)
                for s in range(2):
                    dve.wait_ge(down_done[s], i + 1)
                    nc.vector.scalar_tensor_tensor(h[:, s, :], ps_c[s], pc[:, bass.ds(Q_B2 + i, 1)], h[:, s, :], ALU.add, ALU.add).then_inc(h_ready[s], 1)
                assert ch.n == PER
            ch.base, ch.n = 0, start + NL * PER
            for s in range(2):
                ln_var(2 * NL, s)
            for s in range(2):
                ln_scale(2 * NL, s)

            def ln_tiles(r, q, projected):
                for t in range(4 * q, 4 * q + 4):
                    dve.wait_ge(projected, t + 1)
                    nc.vector.tensor_tensor(xres[:, t, :], psum[:, t % 4, :], xres[:, t, :], ALU.add).then_inc(added, 1)
                for t in range(4 * q, 4 * q + 4):
                    dve.wait_ge(added, NT * r + t + 1)
                    nc.vector.bn_stats(stats[:, t % 4, :], xres[:, t, :]).then_inc(dve_chain, 1)
                    ch.n += 1
                for t in range(4 * q, 4 * q + 4):
                    dve.wait_ge(dve_chain, ch.n - 3 if t % 4 == 0 else ch.n - 3)
                    ch.step(nc.vector.bn_aggr(mv[:, t, :], stats[:, t % 4, :]))
                sl = slice(4 * q, 4 * q + 4)
                nc.vector.tensor_scalar(varr[:, sl], mv[:, sl, 1], EPS, None, ALU.add).then_inc(var4_ready, 1)
                dve.wait_ge(rstd4_ready, 4 * r + q + 1)
                for t in range(4 * q, 4 * q + 4):
                    nc.vector.tensor_scalar(xres[:, t, :], xres[:, t, :], mv[:, t, 0:1], rstd[:, t:t + 1], ALU.subtract, ALU.mult).then_inc(tile_ready, 1)

            dve.wait_ge(xres_biased, 1)
            for q in range(4):
                ln_tiles(0, q, proj_done)

            row = lambda r0, n, t: pr[:, r0:r0 + n].unsqueeze(1).to_broadcast([P, t, n])
            over = lambda a, n: a.unsqueeze(2).to_broadcast([P, NT, n])
            G = lambda k: gs[:, k, :]
            red = lambda o, a, op: ch.step(nc.vector.tensor_reduce(o, a, AX.X, op))
            dve.wait_ge(lg_ready, NT)
            tt(gh[:, :, :], lg[:, :, P:P + NG], row(R_GB1, NG, NT), ALU.add)
            red(G(0), gh[:, :, :], ALU.add)
            ts(G(0), G(0), 1.0 / NG, None, ALU.mult, ALU.bypass)
            tt(gh[:, :, :], gh[:, :, :], over(G(0), NG), ALU.subtract)
            tt(gsq[:, :, :], gh[:, :, :], gh[:, :, :], ALU.mult)
            red(G(1), gsq[:, :, :], ALU.add)
            nc.vector.tensor_scalar(G(1), G(1), 1.0 / NG, EPS, ALU.mult, ALU.add).then_inc(gvar_ready, 1)
            dve.wait_ge(grstd_ready, 1)
            tt(gh[:, :, :], gh[:, :, :], over(G(2), NG), ALU.mult)
            tt(gh[:, :, :], gh[:, :, :], row(R_GAM, NG, NT), ALU.mult)
            tt(gh[:, :, :], gh[:, :, :], row(R_BET, NG, NT), ALU.add)
            nc.vector.tensor_scalar(gh[:, :, :], gh[:, :, :], 0.0, None, ALU.max).then_inc(gh_ready, 1)
            E_ = lambda k: ge[:, k, :, :]
            revb = rev.unsqueeze(1).to_broadcast([P, NT, NE])
            dve.wait_ge(gates_done, 1)
            tt(E_(0), psum[:, 5, 0:P].rearrange("p (t e) -> p t e", t=NT), row(R_GB2, NE, NT), ALU.add)

            def top(k, gates, best):
                red(best, gates, ALU.max)
                tt(E_(2), gates, over(best, NE), ALU.is_equal)
                tt(E_(2), E_(2), revb, ALU.mult)
                red(G(6), E_(2), ALU.max)
                tt(oh[:, k, :, :], E_(2), over(G(6), NE), ALU.is_equal)

            top(0, E_(0), G(3))
            ts(E_(3), oh[:, 0, :, :], -3e38, None, ALU.mult, ALU.bypass)
            tt(E_(1), E_(0), E_(3), ALU.add)
            top(1, E_(1), G(7))
            nc.vector.tensor_tensor(G(4), G(7), G(3), ALU.subtract).then_inc(gap_ready, 1)
            nc.vector.tensor_copy(E_(4), oh[:, 0, :, :]).then_inc(oh_ready, 1)
            dve.wait_ge(gexp_ready, 1)
            ts(G(8), G(5), 1.0, None, ALU.add, ALU.bypass)
            ch.step(nc.vector.reciprocal(G(8), G(8)))
            tt(G(9), G(5), G(8), ALU.mult)
            dve.wait_ge(cnt_done, 1)
            red(cnt[:, :, :], psum[:, 4, 0:2 * P].rearrange("p (k t e) -> p k e t", k=2, t=NT), ALU.add)
            ts(cnt[:, :, :], cnt[:, :, :], float(CAPACITY), 1.0 / ER, ALU.is_le, ALU.mult)
            for k in range(2):
                tt(E_(k), oh[:, k, :, :], over(G(8 + k), NE), ALU.mult)
                tt(E_(k), E_(k), cnt[:, k, :].unsqueeze(1).to_broadcast([P, NT, NE]), ALU.mult)
            tt(wexp[:, :, :], E_(0), E_(1), ALU.add)
            for q in range(4):
                sl = slice(4 * q, 4 * q + 4)
                nc.vector.tensor_tensor(tmpw[:, sl, :].rearrange("p t (e r) -> p t e r", e=NE), lg[:, sl, 0:P].rearrange("p t (e r) -> p t e r", e=NE),
                                        wexp[:, sl, :].unsqueeze(3).to_broadcast([P, 4, NE, ER]), ALU.mult).then_inc(tmpw_ready, 1)
            for q in range(4):
                ln_tiles(1, q, bproj_done)

            dve.wait_ge(tmpwt_ready, 4)
            dve.wait_ge(bproj_done, NT)
            for k in range(2):
                nc.vector.memset(vpad[k][:, :, DK:DK + 1], 1.0).then_inc(vpad_ready, 1)
                nc.vector.memset(vpad[k][:, :, DK + 1:], 0.0).then_inc(vpad_ready, 1)
            for u in range(17):
                if u < 16:
                    dve.wait_ge(hi_ready, u + 1)
                    if u >= 2:
                        dve.wait_ge(lo_ready, u - 1)
                    nc.vector.tensor_tensor(resid[u % 2][:, :], psum[:, 2 * (u % 2):2 * (u % 2) + 2, :].rearrange("p a t -> p (a t)"), parts[u % 2][:, 0, :], ALU.subtract).then_inc(r1_ready, 1)
                if u >= 1:
                    dve.wait_ge(mid_ready, u)
                    nc.vector.tensor_tensor(parts[(u - 1) % 2][:, 2, :], resid[(u - 1) % 2][:, :], parts[(u - 1) % 2][:, 1, :], ALU.subtract).then_inc(lo_ready, 1)
            dve.wait_ge(abs_done, 24)
            nc.vector.tensor_reduce(absum3[:, :], absum[:, :].rearrange("p (w c) -> p w c", w=3), AX.X, ALU.add).then_inc(abs_sum, 1)
            dve.wait_ge(abs_all, 1)
            ts(thr[:, :], psum[:, 0, 0:3], 1.0 / (D * HID), THRESH, ALU.mult, ALU.mult)
            nc.vector.tensor_scalar(nthr[:, :], thr[:, :], -1.0, None, ALU.mult).then_inc(thr_ready, 1)

            for k in range(2):
                dve.wait_ge(st_parts[k], 128)
            for k in range(2):
                dve.wait_ge(st_v[k], 128)
            for k in range(3):
                nc.vector.memset(kst[k][SR:SR + 2, :, :], 1.0).then_inc(ones_ready, 1)

            def maxima(i, c, qt):
                for j in range(GH):
                    for a in range(2):
                        m = 8 * qt + 2 * j + a
                        at_least(dve, mx_done, i, 192, 64 * c + m + 1)
                        nc.vector.tensor_reduce(mx[c % 2][:, j, qt, a:a + 1], psum[:, 6 + m % 2, :], AX.X, ALU.max).then_inc(mx_read, 1)

            def finish_maxima(i, c):
                at_least(dve, mx_read, i, 192, 64 * c + 64)
                at_least(dve, nmt_done, i, 3, c)
                nc.vector.tensor_reduce(nm[:, :].rearrange("p (j q) -> p j q", j=GH), mx[c % 2][:, :, :, :], AX.X, ALU.max, negate=True).then_inc(nm_ready, 1)
                at_least(dve, nmt_done, i, 3, c + 1)
                if not (isinstance(i, int) and 3 * i + c == 0):
                    dve.wait_ge(ld_nm[(c - 1) % 3], ((i + (c - 1) // 3) + 1) * 16)
                ch2.step(nc.vector.tensor_copy(nmh[:, :], psum[0:GH * KT, 6, 0:P]))
                nc.vector.tensor_tensor(nml[:, :], psum[0:GH * KT, 6, 0:P], nmh[:, :], ALU.subtract).then_inc(nmt_read, 1)

            ch2 = Chain(dve, nmh_ready)
            for qt in range(KT):
                maxima(0, 0, qt)
            finish_maxima(0, 0)
            for qt in range(KT // 2):
                maxima(0, 1, qt)

            def group(i, c):
                ch2.base, ch2.n = i * 3 + c + 1, 0
                g = 3 * i + c if isinstance(i, int) else 1
                for kt in range(KT):
                    if kt < KT // 2 and g + 1 < NGRP:
                        maxima(i, c + 1, kt + KT // 2)
                    if kt == KT // 2 - 1 and g + 1 < NGRP:
                        finish_maxima(i, c + 1)
                    if kt >= KT // 2 and g + 2 < NGRP:
                        maxima(i, c + 2, kt - KT // 2)

            over_groups(dve, group)
            dve.wait_ge(ld_den, 16)
            nc.vector.reciprocal(den_sb[:, :, :], den_sb[:, :, :]).then_inc(den_ready, 1)

            def normalise(q):
                dve.wait_ge(ld_rb, 64 * q + 64)
                dve.wait_ge(ld_od[q % 2], 64 * (q // 2) + 64)
                for k in range(4):
                    nc.vector.tensor_tensor(od[k][:, :, :], od[k][:, :, :], rb[:, :, P * k:P * k + P], ALU.mult).then_inc(normed, 1)

            def ln_stats(r, q, x, added):
                for k in range(4):
                    dve.wait_ge(added, q * 4 + k + 1)
                    nc.vector.bn_stats(stats[:, k, :], x(k)).then_inc(x_stats, 1)
                dve.wait_ge(x_stats, q * 4 + 4 * r + 4)
                nc.vector.memset(varr[:, 0:4], EPS).then_inc(x_mv, 1)
                for k in range(4):
                    nc.vector.bn_aggr(mv[:, k, :], stats[:, k, :]).then_inc(x_mv, 1)
                dve.wait_ge(x_mv, q * 5 + 5 * r + 5)
                nc.vector.tensor_tensor(varr[:, 0:4], mv[:, 0:4, 1], varr[:, 0:4], ALU.add).then_inc(x_var, 1)

            def ln_apply(r, q, x, ready):
                dve.wait_ge(x_rstd, q + r + 1)
                for k in range(4):
                    nc.vector.tensor_scalar(x(k), x(k), mv[:, k, 0:1], rstd[:, k:k + 1], ALU.subtract, ALU.mult).then_inc(ready, 1)

            normalise(0)
            for q in range(4):
                x = lambda k: x3t[4 * (q % 2) + k][:, :]
                dve.wait_ge(ld_x2t[q % 2], 64 * (q // 2) + 64)
                for k in range(4):
                    dve.wait_ge(oproj_done, 4 * q + k + 1)
                    nc.vector.tensor_tensor(x(k), psum[:, k, :], x(k), ALU.add).then_inc(x_added, 1)
                ln_stats(0, q, x, x_added)
                if q < 3:
                    normalise(q + 1)
                ln_apply(0, q, x, x3_ready)
                for t in range(4 * q, 4 * q + 4):
                    dve.wait_ge(x3h_ready, t + 1)
                    nc.vector.tensor_tensor(x3l[:, :, P * t:P * t + P], psum[:, 4 + t % 4, :].rearrange("p (k t) -> p k t", k=KC), x3h[:, :, P * t:P * t + P].bitcast(F32), ALU.subtract).then_inc(x3l_ready, 1)
            yk = lambda k: yt[:, k, :]

            def hidden(n, f):
                dve.wait_ge(silu_ready, n * HC + f + 1)
                wait_for(dve, hl_ready, n * HC + f - 1)
                nc.vector.scalar_tensor_tensor(hid[f % 2][:, :], psum[:, 5 + 2 * (f % 2), :], pc[:, Q_US + f:Q_US + f + 1], sg[f % 2][:, :], ALU.mult, ALU.mult).then_inc(hid_ready, 1)
                dve.wait_ge(hh_ready, n * HC + f + 1)
                wait_for(dve, ffn_done, n * HC + f - 1)
                nc.vector.tensor_tensor(hl[f % 2][:, :], hid[f % 2][:, :], hh[f % 2][:, :].bitcast(F32), ALU.subtract).then_inc(hl_ready, 1)

            def finish(n):
                dve.wait_ge(ld_xin, n * 16 + 16)
                for k in range(4):
                    dve.wait_ge(yt_ready, n * 4 + k + 1)
                    nc.vector.tensor_tensor(yk(k), yk(k), xin[:, k, :], ALU.add).then_inc(f_added, 1)
                ln_stats(4, n, yk, f_added)
                ln_apply(4, n, yk, out_ready)

            def block_of_tokens(n, first):
                for f in range(HC):
                    hidden(n, f)
                    if f == 0 and not first:
                        finish(n - 1)
                dve.wait_ge(ffn_done, n * HC + HC)
                wait_for(dve, st_out, n * 64)
                for k in range(4):
                    nc.vector.tensor_tensor(yk(k), psum[:, k, :], pr[:, R_DS:R_DS + D], ALU.mult).then_inc(yt_ready, 1)

            dve.wait_ge(x3_tr, NT)
            dve.wait_ge(x3l_ready, NT)
            dve.wait_ge(st_x3, 16 * NT)
            block_of_tokens(0, True)
            with dve.Fori(1, 4) as n:
                block_of_tokens(n, False)
            finish(3)

        @block.tensor
        def _(pe):
            mm = nc.tensor.matmul
            pe.wait_ge(ld_win, 16)
            for s in range(2):
                pe.wait_ge(ld_x[s], 32)
                for k in range(KC):
                    for b in range(B):
                        t0 = b * L + s * HALF
                        last = mm(ps_c[s][DH * b:DH * b + DH, :], win_sb[:, k, :], xt[:, k, t0:t0 + HALF], start=(k == 0), stop=(k == KC - 1))
                last.then_inc(inproj[s], 1)
            pe.wait_ge(ld_const, 48)

            def ln_center(n, s):
                pe.wait_ge(h_ready[s], n + 1)
                mm(ps_c[s], center, h[:, s, :], start=True, stop=True).then_inc(centered[s], 1)

            def ln_sums(n, s):
                pe.wait_ge(squared[s], n + 1)
                for t in range(4):
                    last = mm(ps_b[s][:, 2 * t:2 * t + 2], sq[s][:, P * t:P * t + P], blk_mean, start=True, stop=True)
                last.then_inc(var_sums[s], 1)

            def ln_spread(n, s):
                pe.wait_ge(rstd_ready[s], n + 1)
                for t in range(4):
                    for b in range(B):
                        last = mm(ps_b[s][DH * b:DH * b + DH, P * t:P * t + P], rstd8[s][:, 2 * t + b:2 * t + b + 1].to_broadcast([P, DH]), ident, start=True, stop=True)
                last.then_inc(spread[s], 1)

            with pe.Fori(0, NL) as i:
                for j in range(2):
                    for f in (ln_center, ln_sums, ln_spread):
                        for s in range(2):
                            f(2 * i + j, s)
                pe.wait_ge(ld_w, 64 * (i + 1))
                for c in range(FC + 2):
                    for s in range(2):
                        if c == 0:
                            pe.wait_ge(yn_ready[s], i + 1)
                        if c < FC:
                            if c >= 2:
                                pe.wait_ge(g_ready[s], FC * i + c - 1)
                            mm(ps_f[s][c % 2], w1bd[:, c, :], y[s][:, :], start=True, stop=True).then_inc(up_done[s], 1)
                        if c >= 2:
                            pe.wait_ge(g_ready[s], FC * i + c - 1)
                            last = mm(ps_c[s], w2bd[:, c - 2, :], g[s][:, c - 2, :], start=(c == 2), stop=(c == FC + 1))
                            if c == FC + 1:
                                last.then_inc(down_done[s], 1)

            for f in (ln_center, ln_sums, ln_spread):
                for s in range(2):
                    f(2 * NL, s)

            def out_proj(q):
                for t in range(4 * q, 4 * q + 4):
                    b, s = t // (NT // B), (t // 4) % 2
                    if t < 4:
                        pe.wait_ge(yn_ready[0], NL + 1)
                        pe.wait_ge(yn_ready[1], NL + 1)
                        pe.wait_ge(ld_wout, 32)
                    else:
                        pe.wait_ge(added, t - 3)
                    mm(psum[:, t % 4, :], y[s][:, P * (t % 4):P * (t % 4) + P], wout_sb[:, b, :], start=True, stop=True).then_inc(proj_done, 1)

            def transpose_x(n, t):
                pe.wait_ge(tile_ready, n + 1)
                if n >= 2:
                    pe.wait_ge(xt_ready, n - 1)
                if n == NT:
                    pe.wait_ge(ght_ready, 1)
                for k in range(KC):
                    last = nc.tensor.transpose(psum[:, 4 + n % 2, P * k:P * k + P], xres[:, t, P * k:P * k + P], ident)
                last.then_inc(tr_done, 1)

            def lora_gate(t):
                pe.wait_ge(xt_ready, t + 1)
                if t >= 2:
                    pe.wait_ge(lg_ready, t - 1)
                for k in range(KC):
                    last = mm(psum[:, 6 + t % 2, 0:P + NG], x1t[:, k, P * t:P * t + P], ag_sb[:, k, :], start=(k == 0), stop=(k == KC - 1))
                last.then_inc(lg_done, 1)

            def main_proj(q):
                for t in range(4 * q, 4 * q + 4):
                    pe.wait_ge(added, NT + t - 3)
                    for k in range(KC):
                        mm(psum[:, t % 4, :], x1t[:, k, P * t:P * t + P], main_sb[:, k, :], start=(k == 0), stop=False)

            out_proj(0)
            pe.wait_ge(ld_bw, 16 * 7)
            for q in range(4):
                if q < 3:
                    out_proj(q + 1)
                for t in range(4 * q, 4 * q + 4):
                    transpose_x(t, t)
                    if t >= 1:
                        lora_gate(t - 1)
            lora_gate(NT - 1)
            main_proj(0)
            pe.wait_ge(gh_ready, 1)
            for q in range(4):
                last = nc.tensor.transpose(psum[:, 4, P * q:P * q + P], gh[:, 4 * q:4 * q + 4, :].rearrange("p t n -> p (t n)"), ident)
            last.then_inc(ght_done, 1)
            pe.wait_ge(ght_ready, 1)
            for q in range(4):
                last = mm(psum[:, 5, 4 * NE * q:4 * NE * q + 4 * NE], ght[:, q, :], gw2_sb[:, :, :].rearrange("p t e -> p (t e)"), start=True, stop=True)
            last.then_inc(gates_done, 1)
            pe.wait_ge(oh_ready, 1)
            mm(psum[:, 4, 0:2 * P], ones, oh[:, :, :, :].rearrange("p k t e -> p (k t e)"), start=True, stop=True).then_inc(cnt_done, 1)
            for q in range(4):
                if q >= 1:
                    main_proj(q)
                pe.wait_ge(tmpw_ready, q + 1)
                if q == 0:
                    pe.wait_ge(lg_ready, NT)
                if q >= 2:
                    pe.wait_ge(tmpwt_ready, q - 1)
                for t in range(4):
                    last = nc.tensor.transpose(psum[:, 6 + q % 2, P * t:P * t + P], tmpw[:, 4 * q + t, :], ident)
                last.then_inc(wtr_done, 1)
                pe.wait_ge(tmpwt_ready, q + 1)
                for t in range(4 * q, 4 * q + 4):
                    mm(psum[:, t % 4, :], tmpwt[:, t, :], lorab_sb[:, :], start=False, stop=True).then_inc(bproj_done, 1)
                if q >= 1:
                    for t in range(4 * q - 4, 4 * q):
                        transpose_x(NT + t, t)
            for t in range(NT - 4, NT):
                transpose_x(NT + t, t)

            pe.wait_ge(ld_qkv, 16)
            for t in range(NT):
                pe.wait_ge(xt_ready, NT + t + 1 if t >= NT - 2 else NT + t + 1)
                if t < 2:
                    pe.wait_ge(xt_ready, 2 * NT)
                else:
                    pe.wait_ge(v_ready, t - 1)
                for k in range(KC):
                    last = mm(psum[:, 4 + t % 2, :], x1t[:, k, P * t:P * t + P], wqkv_sb[:, 2 * KC + k, :], start=(k == 0), stop=(k == KC - 1))
                last.then_inc(v_done, 1)
            pe.wait_ge(added, 2 * NT)
            for u in range(16):
                b, w, c = u // 8, u // 4 % 2, u % 4
                if u >= 2:
                    pe.wait_ge(r1_ready, u - 1)
                for a in range(2):
                    for k in range(KC):
                        last = mm(psum[:, 2 * (u % 2) + a, :], wqkv_sb[:, w * KC + k, P * c:P * c + P], x1t[:, k, b * L + a * HALF:b * L + a * HALF + HALF], start=(k == 0), stop=(k == KC - 1))
                last.then_inc(qk_done, 1)
            pe.wait_ge(abs_sum, 1)
            pe.wait_ge(r1_ready, 16)
            mm(psum[:, 0, 0:3], ones, absum3[:, :], start=True, stop=True).then_inc(abs_all, 1)
            pe.wait_ge(thr_ready, 1)

            def maxima(i, c, qt):
                for j in range(GH):
                    for a in range(2):
                        m = 8 * qt + 2 * j + a
                        at_least(pe, mx_read, i, 192, 64 * c + m - 1)
                        mm(psum[:, 6 + m % 2, :], qst[c % 3][0:SR, j, P * qt:P * qt + P], kst[c % 3][0:SR, j, a * HALF:a * HALF + HALF], start=True, stop=True).then_inc(mx_done, 1)
                        yield

            def finish_maxima(i, c):
                at_least(pe, nm_ready, i, 3, c + 1)
                nc.tensor.transpose(psum[0:GH * KT, 6, 0:P], nm[:, :], ident).then_inc(nmt_done, 1)
                at_least(pe, nmt_read, i, 3, c + 1)

            def scores(i, c, n):
                kt, j = n // 4, n % 4
                at_least(pe, exp_done, i, 96, 32 * c + n - 1)
                for a in range(2):
                    last = mm(psum[:, 2 * (n % 2) + a, :], kst[c % 3][0:SR + 2, j, P * kt:P * kt + P], qst[c % 3][0:SR + 2, j, a * HALF:a * HALF + HALF], start=True, stop=True)
                last.then_inc(score_done, 1)

            def gather(i, c, kt):
                at_least(pe, exp_done, i, 96, 32 * c + 4 * kt + 4)
                if kt == 0:
                    at_least(pe, o_ready, i, 3, c)
                    pe.wait_ge(ld_v[c % 3], ((i + c // 3) + 1) * 16)
                for a in range(2):
                    for j in range(GH):
                        slot = (32 * c + 4 * kt + j) % NP
                        r = slice(2 * DK * j, 2 * DK * j + 2 * DK)
                        last = mm(psum[r, 4 + a, :], vg[c % 3][:, kt, r], probs[slot][:, a * HALF:a * HALF + HALF], start=(kt == 0), stop=(kt == KT - 1))
                last.then_inc(pv_done, 1)

            wait_stack = lambda i, c: pe.wait_ge(ld_stack[c % 3], ((i + c // 3) + 1) * 192)
            wait_stack(0, 0)
            for qt in range(KT):
                for _ in maxima(0, 0, qt):
                    pass
            finish_maxima(0, 0)
            wait_stack(0, 1)
            for qt in range(KT // 2):
                for _ in maxima(0, 1, qt):
                    pass
            pe.wait_ge(ones_ready, 3)

            def group(i, c):
                g = 3 * i + c if isinstance(i, int) else 1
                pe.wait_ge(ld_nm[c % 3], ((i + c // 3) + 1) * 16)
                for kt in range(KT):
                    todo = iter(())
                    if kt < KT // 2 and g + 1 < NGRP:
                        todo = maxima(i, c + 1, kt + KT // 2)
                    if kt >= KT // 2 and g + 2 < NGRP:
                        if kt == KT // 2:
                            wait_stack(i, c + 2)
                        todo = maxima(i, c + 2, kt - KT // 2)
                    for j in range(GH):
                        scores(i, c, 4 * kt + j)
                        next(todo, None)
                        if j == 1:
                            if kt > 0:
                                gather(i, c, kt - 1)
                            elif g > 0:
                                gather(i, c - 1, KT - 1)
                        next(todo, None)
                    if kt == KT // 2 - 1 and g + 1 < NGRP:
                        finish_maxima(i, c + 1)

            over_groups(pe, group)
            gather(0, NGRP - 1, KT - 1)
            def out_projection(q):
                if q == 0:
                    pe.wait_ge(ld_qkv, 32)
                    pe.wait_ge(o_ready, NGRP)
                for k in range(4):
                    pe.wait_ge(normed, 4 * q + k + 1)
                    if q > 0:
                        pe.wait_ge(x_added, 4 * q - 4 + k + 1)
                    for c in range(KC):
                        last = mm(psum[:, k, :], od[k][:, c, :], wo_sb[:, c, :], start=(c == 0), stop=(c == KC - 1))
                    last.then_inc(oproj_done, 1)

            out_projection(0)
            for q in range(4):
                if q < 3:
                    out_projection(q + 1)
                for k in range(4):
                    t = 4 * q + k
                    pe.wait_ge(x3_ready, t + 1)
                    if q > 0:
                        pe.wait_ge(x3l_ready, t - 3)
                    for c in range(KC):
                        last = nc.tensor.transpose(psum[:, 4 + k, P * c:P * c + P], x3t[4 * (q % 2) + k][:, P * c:P * c + P], ident)
                    last.then_inc(x3_tr, 1)
            def gate_up(n, f):
                wait_for(pe, hid_ready, n * HC + f - 1)
                cols = slice(P * (f % 8), P * (f % 8) + P)
                for w in range(2):
                    for k in range(KC):
                        for x in (x3h, x3l):
                            last = mm(psum[:, 4 + 2 * (f % 2) + w, :], tern_sb[:, 8 * w + 2 * k + f // 8, cols], x[:, k, bass.ds(n * HALF, HALF)],
                                      start=(k == 0 and x is x3h), stop=(k == KC - 1 and x is x3l))
                last.then_inc(gate_up_done, 1)

            def down(n, f):
                pe.wait_ge(hl_ready, n * HC + f + 1)
                if f == 0:
                    wait_for(pe, yt_ready, n * 4)
                cols = slice(D * (f % 2), D * (f % 2) + D)
                for k in range(4):
                    for x in (hh, hl):
                        last = mm(psum[:, k, :], x[f % 2][:, P * k:P * k + P], tern_sb[:, 16 + f // 2, cols], start=(f == 0 and x is hh), stop=(f == HC - 1 and x is hl))
                last.then_inc(ffn_done, 1)

            pe.wait_ge(x3l_ready, NT)
            pe.wait_ge(x_added, NT)
            gate_up(0, 0)
            gate_up(0, 1)

            def ffn_block(n, last):
                for f in range(HC):
                    down(n, f)
                    if f + 2 < HC:
                        gate_up(n, f + 2)
                    elif not last:
                        gate_up(n + 1, f + 2 - HC)

            ffn_block(0, False)
            with pe.Fori(1, 3) as n:
                ffn_block(n, False)
            ffn_block(3, True)


def kernel(**inputs):
    import numpy as np
    import concourse.bacc as bacc
    from concourse import mybir
    from concourse.bass_utils import run_bass_kernel_spmd

    a = {name: np.asarray(value) for name, value in inputs.items()}
    attn = lambda name: a["L0_attn_" + name]
    ffn = lambda name: a["L0_ffn_" + name]
    tf = lambda name: a["L1_ffn_" + name]
    x = attn("x").reshape(TOK, D)
    by_half = lambda w: w.T.reshape(KC, P, 2, L).transpose(0, 2, 1, 3).reshape(2 * KC, P, L)
    by_pair = lambda w: w.T.reshape(HC // 2, 2, P, D).transpose(0, 2, 1, 3).reshape(HC // 2, P, L)
    both = lambda v: np.concatenate([v, v], -1)
    consts = np.zeros((P, C_END), np.float32)
    consts[:, C_ID:C_ID + P] = np.eye(P)
    consts[:, C_CEN:C_CEN + P] = np.kron(np.eye(B), np.eye(DH) - 1 / DH)
    consts[:, C_ONE:C_ONE + P] = 1
    consts[:, C_BLK:C_BLK + B] = np.kron(np.eye(B), np.ones((DH, 1))) / DH
    consts[:, C_REV:] = NE - np.arange(NE)
    columns = [both(attn(n)).T for n in ("ln1_w", "ln1_b", "phz_re", "phz_im", "lc_re", "lc_im", "sc_lin", "ln2_w", "ln2_b", "b2")]
    columns += [np.broadcast_to(both(attn(n))[:, None], (P, 4)) for n in ("bin", "lnl_w", "lnl_b")]
    columns += [both(attn("b1").reshape(NL, FC, DH)).reshape(NL * FC, P).T]
    columns += [tf(n).reshape(HC, P).T for n in ("gate_scale", "up_scale")]
    row = np.concatenate([attn("bout"), tf("down_scale").ravel(), ffn("gb1"), ffn("ln_gamma"), ffn("ln_beta"), ffn("gb2")])
    arrays = {
        "x_tok": x,
        "x_feat": x.T,
        "win": attn("Win").T,
        "w1": attn("W1").transpose(0, 2, 1),
        "w2": attn("W2").transpose(0, 2, 1),
        "wout": attn("Wout").T,
        "main_w": ffn("weight").T,
        "ag_w": np.concatenate([ffn("lora_A").transpose(1, 0, 2).reshape(D, NE * ER), ffn("gw1").T], 1),
        "lora_b": ffn("lora_B").reshape(NE * ER, D),
        "gw2": ffn("gw2").T,
        "wqkv": np.stack([a["L1_attn_w_" + c].T for c in "qkv"]),
        "wo": a["L1_attn_w_o"].T,
        "tern": np.concatenate([by_half(tf("gate_w")), by_half(tf("up_w")), by_pair(tf("down_w"))]),
        "consts": consts,
        "pcol": np.concatenate(columns, 1),
        "prow": np.broadcast_to(row, (P, row.size)),
    }
    arrays = {name: np.ascontiguousarray(value) for name, value in arrays.items()}
    nc = bacc.Bacc("TRN2", target_bir_lowering=False, num_devices=1)
    args = [nc.dram_tensor(name, value.shape, mybir.dt.from_np(value.dtype), kind="ExternalInput").ap() for name, value in arrays.items()]
    out = nc.dram_tensor("out", [TOK, D], F32, kind="ExternalOutput").ap()
    build(nc, *args, out)
    result = run_bass_kernel_spmd(nc, [arrays], core_ids=[0])
    return result.results[0]["out"].reshape(B, L, D)
```

```python
import numpy as np
from contextlib import ExitStack

import concourse.bass as bass
from concourse import mybir
from concourse.alu_op_type import AluOpType as ALU

ACT = mybir.ActivationFunctionType
AX = mybir.AxisListType
F32 = mybir.dt.float32
F32R = mybir.dt.float32r
BF16 = mybir.dt.bfloat16

P = 128
B, L, D = 2, 1024, 512
TOK = B * L
KC = D // P
NT = TOK // P
HALF = L // 2
NL, DH, DFF = 4, 64, 256
FC = DFF // DH
NE, ER = 8, 16
NG = 4 * NE
CAPACITY = int(3.0 * TOK / NE)
NH, DK = 32, 16
GH = 4
NGRP = B * NH // GH
KT = L // P
HID = 2048
HC = HID // P
EPS = 1e-5
THRESH = 0.7

C_ID, C_CEN, C_ONE, C_BLK, C_REV = 0, P, 2 * P, 3 * P, 3 * P + 2
C_END = C_REV + NE
(Q_L1W, Q_L1B, Q_RE, Q_IM, Q_LR, Q_LI, Q_SCL, Q_L2W, Q_L2B, Q_B2, Q_BIN, Q_LNW, Q_LNB) = range(0, 52, 4)
Q_B1 = 52
Q_GS = Q_B1 + NL * FC
Q_US = Q_GS + HC
Q_END = Q_US + HC
R_BOUT, R_DS = 0, D
R_GB1 = 2 * D
R_GAM, R_BET, R_GB2 = R_GB1 + NG, R_GB1 + 2 * NG, R_GB1 + 3 * NG
R_END = R_GB2 + NE


class Chain:

    def __init__(self, engine, sem):
        self.engine, self.sem, self.base, self.n = engine, sem, 0, 0

    def step(self, instruction):
        instruction.then_inc(self.sem, 1)
        self.n += 1
        self.engine.wait_ge(self.sem, self.base + self.n)


def build(nc, x_tok, x_feat, win, w1, w2, wout, main_w, ag_w, lora_b, gw2, wqkv, wo, tern, consts, pcol, prow, out):
    ctx = ExitStack()
    with ctx:
        sem = lambda name: ctx.enter_context(nc.semaphore(name))
        sems = lambda name, n=2: [sem(f"{name}{i}") for i in range(n)]

        def sb(stack, name, shape, dt=F32):
            return stack.enter_context(nc.sbuf_tensor(name, shape, dt))

        psum = ctx.enter_context(nc.psum_tensor("psum", [P, 8, 512], F32))

        cst = sb(ctx, "cst", [P, C_END])
        pc = sb(ctx, "pc", [P, Q_END])
        pr = sb(ctx, "pr", [P, R_END])
        mhalf = sb(ctx, "mhalf", [P, NT])
        ident = cst[:, C_ID:C_ID + P]
        center = cst[:, C_CEN:C_CEN + P]
        ones = cst[:, C_ONE:C_ONE + P]
        blk_mean = cst[:, C_BLK:C_BLK + 2]
        rev = cst[:, C_REV:C_REV + NE]
        stats = sb(ctx, "stats", [P, 4, 6])
        mv = sb(ctx, "mv", [P, NT, 2])
        varr = sb(ctx, "varr", [P, NT])
        rstd = sb(ctx, "rstd", [P, NT])
        thr = sb(ctx, "thr", [P, 3])
        nthr = sb(ctx, "nthr", [P, 3])

        xts = ExitStack()
        x1t = sb(xts, "x1t", [P, KC, TOK])
        xt = x1t

        ab = ExitStack()
        xres = sb(ab, "xres", [P, NT, D])
        y = [sb(ab, f"y{s}", [P, HALF]) for s in range(2)]
        wout_sb = sb(ab, "wout_sb", [P, B, D])
        main_sb = sb(ab, "main_sb", [P, KC, D])
        ag_sb = sb(ab, "ag_sb", [P, KC, P + NG])
        lorab_sb = sb(ab, "lorab_sb", [P, D])
        gw2_sb = sb(ab, "gw2_sb", [P, 4, NE])
        sa = ExitStack()
        win_sb = sb(sa, "win_sb", [P, KC, DH])
        cos = sb(sa, "cos", [P, NL, L])
        sin = sb(sa, "sin", [P, NL, L])
        tab1 = sb(sa, "tab1", [P, NL, HALF])
        tab2 = sb(sa, "tab2", [P, NL, HALF])
        pw = sb(sa, "pw", [P, 16, NL])
        w1bd = sb(sa, "w1bd", [P, FC, P])
        w2bd = sb(sa, "w2bd", [P, FC, P])
        h = sb(sa, "h", [P, 2, HALF])
        half = lambda name, n=HALF: [sb(sa, f"{name}{s}", [P, n]) for s in range(2)]
        hc, sq, z = half("hc"), half("sq"), half("z")
        re_in, im_in, zr, zi, re_p, im_p = (half(n) for n in ("re_in", "im_in", "zr", "zi", "re_p", "im_p"))
        g = [sb(sa, f"g{s}", [P, FC, HALF]) for s in range(2)]
        var8, rstd8 = half("var8", 8), half("rstd8", 8)
        sa.close()
        sbk = ExitStack()
        lg = sb(sbk, "lg", [P, NT, P + NG])
        gh = sb(sbk, "gh", [P, NT, NG])
        gsq = sb(sbk, "gsq", [P, NT, NG])
        ght = sb(sbk, "ght", [P, 4, P])
        gs = sb(sbk, "gs", [P, 10, NT])
        ge = sb(sbk, "ge", [P, 6, NT, NE])
        oh = sb(sbk, "oh", [P, 2, NT, NE])
        cnt = sb(sbk, "cnt", [P, 2, NE])
        wexp = sb(sbk, "wexp", [P, NT, NE])
        tmpw = sb(sbk, "tmpw", [P, NT, P])
        tmpwt = sb(sbk, "tmpwt", [P, NT, P])
        sbk.close()
        ab.close()
        sq_ = ExitStack()
        parts = [sb(sq_, f"parts{i}", [P, 3, L], BF16) for i in range(2)]
        resid = [sb(sq_, f"resid{i}", [P, L]) for i in range(2)]
        vpad = [sb(sq_, f"vpad{i}", [P, NH, 2 * DK]) for i in range(2)]
        wabs = sb(sq_, "wabs", [P, 2, L])
        absum = sb(sq_, "absum", [P, 3 * 8])
        absum3 = sb(sq_, "absum3", [P, 3])
        sq_.close()
        xts.close()
        cd = ExitStack()
        tern_sb = sb(cd, "tern_sb", [P, 24, L], F32R)
        at = ExitStack()
        qst = [sb(at, f"qst{i}", [P, GH, L], BF16) for i in range(3)]
        kst = [sb(at, f"kst{i}", [P, GH, L], BF16) for i in range(3)]
        vg = [sb(at, f"vg{i}", [P, KT, GH * 2 * DK]) for i in range(3)]
        o_sb = sb(at, "o_sb", [P, L])
        wraw = sb(at, "wraw", [P, L])
        mx = [sb(at, f"mx{i}", [P, GH, KT, 2]) for i in range(2)]
        nm = sb(at, "nm", [P, GH * KT])
        nmh = sb(at, "nmh", [GH * KT, P], BF16)
        nml = sb(at, "nml", [GH * KT, P], BF16)
        pst = ExitStack()
        probs = [sb(pst, f"probs{i}", [P, L]) for i in range(2 * GH)]
        pst.close()
        pst = ExitStack()
        wqkv_sb = sb(pst, "wqkv_sb", [P, 3 * KC, D])
        pst.close()
        at.close()
        x3s = ExitStack()
        x3h = sb(x3s, "x3h", [P, KC, TOK], F32R)
        x3l = sb(x3s, "x3l", [P, KC, TOK], F32R)
        op = ExitStack()
        wo_sb = sb(op, "wo_sb", [P, KC, D])
        rb = sb(op, "rb", [P, KC, HALF])
        od = [sb(op, f"od{k}", [P, KC, P]) for k in range(4)]
        x3t = [sb(op, f"x3t{k}", [P, D]) for k in range(8)]
        den_sb = od[0]
        op.close()
        ff = ExitStack()
        hh = [sb(ff, f"hh{k}", [P, HALF], F32R) for k in range(2)]
        hl = [sb(ff, f"hl{k}", [P, HALF], F32R) for k in range(2)]
        sg = [sb(ff, f"sg{k}", [P, HALF]) for k in range(2)]
        hid = [sb(ff, f"hid{k}", [P, HALF]) for k in range(2)]
        yt = sb(ff, "yt", [P, 4, D])
        xin = sb(ff, "xin", [P, 4, D])
        ff.close()
        x3s.close()
        cd.close()

        ps_c = [psum[:, s, :] for s in range(2)]
        ps_b = [psum[:, 2 + s, :] for s in range(2)]
        ps_f = [[psum[:, 4 + 2 * s + k, :] for k in range(2)] for s in range(2)]

        ld_const, ld_x, ld_win, ld_wout = sem("ld_const"), sems("ld_x"), sem("ld_win"), sem("ld_wout")
        ld_xres = sem("ld_xres")
        zeroed, ld_w = sem("zeroed"), sem("ld_w")
        dve_chain, pool_chain, act_chain = sem("dve_chain"), sem("pool_chain"), sem("act_chain")
        mag2_ready, invm_ready, mag_ready, decay_ready = sem("mag2_ready"), sem("invm_ready"), sem("mag_ready"), sem("decay_ready")
        tables_ready = sem("tables_ready")
        inproj = sems("inproj")
        h_ready, centered, squared, hc_copied = sems("h_ready"), sems("centered"), sems("squared"), sems("hc_copied")
        var_sums, var_ready, rstd_ready = sems("var_sums"), sems("var_ready"), sems("rstd_ready")
        spread, z_ready, y_ready, yn_ready = sems("spread"), sems("z_ready"), sems("y_ready"), sems("yn_ready")
        im_in_ready, zi_ready, im_p_ready = sems("im_in_ready"), sems("zi_ready"), sems("im_p_ready")
        up_done, g_ready, down_done = sems("up_done"), sems("g_ready"), sems("down_done")
        ld_bw = sem("ld_bw")
        xres_biased = sem("xres_biased")
        proj_done, var4_ready, rstd4_ready, tile_ready = sem("proj_done"), sem("var4_ready"), sem("rstd4_ready"), sem("tile_ready")
        tr_done, xt_ready, lg_done, lg_ready = sem("tr_done"), sem("xt_ready"), sem("lg_done"), sem("lg_ready")
        gvar_ready, grstd_ready, gh_ready, ght_done, ght_ready = (sem(n) for n in ("gvar_ready", "grstd_ready", "gh_ready", "ght_done", "ght_ready"))
        gates_done, gap_ready, gexp_ready, oh_ready, cnt_done = (sem(n) for n in ("gates_done", "gap_ready", "gexp_ready", "oh_ready", "cnt_done"))
        tmpw_ready, wtr_done, tmpwt_ready = sem("tmpw_ready"), sem("wtr_done"), sem("tmpwt_ready")
        bproj_done, added = sem("bproj_done"), sem("added")
        st_x2 = sem("st_x2")
        ld_qkv, hi_ready, r1_ready, mid_ready, lo_ready, qk_done = (sem(n) for n in ("ld_qkv", "hi_ready", "r1_ready", "mid_ready", "lo_ready", "qk_done"))
        v_done, v_ready, vpad_ready = (sem(n) for n in ("v_done", "v_ready", "vpad_ready"))
        st_parts, st_v, ld_abs = sems("st_parts"), sems("st_v"), sems("ld_abs")
        abs_done, abs_sum, abs_all, thr_ready = (sem(n) for n in ("abs_done", "abs_sum", "abs_all", "thr_ready"))
        ld_stack, ld_v, ld_nm = sems("ld_stack", 3), sems("ld_v", 3), sems("ld_nm", 3)
        ones_ready, mx_done, mx_read, nm_ready, nmt_done, nmt_read = (sem(n) for n in ("ones_ready", "mx_done", "mx_read", "nm_ready", "nmt_done", "nmt_read"))
        nmh_ready = sem("nmh_ready")
        score_done, exp_done, pv_done, o_ready, st_o = (sem(n) for n in ("score_done", "exp_done", "pv_done", "o_ready", "st_o"))
        st_nm = sem("st_nm")
        ld_tern = sem("ld_tern")
        tern_chain = sem("tern_chain")
        qk_dram = nc.dram_tensor("qk_dram", [2, 3, B * D, L], BF16).ap()
        v_dram = nc.dram_tensor("v_dram", [NGRP, L, GH * 2 * DK], F32).ap()
        nm_dram = nc.dram_tensor("nm_dram", [2, GH * KT, P], BF16).ap()
        o_dram = nc.dram_tensor("o_dram", [B * D, L], F32).ap()
        den_dram = nc.dram_tensor("den_dram", [B * NH, L], F32).ap()
        x2_dram = nc.dram_tensor("x2_dram", [TOK, D], F32).ap()
        rec_dram = nc.dram_tensor("rec_dram", [B * NH, L], F32).ap()
        x3_dram = nc.dram_tensor("x3_dram", [TOK, D], F32).ap()
        ld_den, den_ready, st_rec = (sem(n) for n in ("ld_den", "den_ready", "st_rec"))
        ld_rb, normed, oproj_done = sem("ld_rb"), sem("normed"), sem("oproj_done")
        ld_od, ld_x2t, st_x3 = sems("ld_od"), sems("ld_x2t"), sem("st_x3")
        x_added, x_stats, x_mv, x_var, x_rstd, x3_ready = (sem(n) for n in ("x_added", "x_stats", "x_mv", "x_var", "x_rstd", "x3_ready"))
        x3_tr, x3h_ready, x3l_ready = sem("x3_tr"), sem("x3h_ready"), sem("x3l_ready")
        gate_up_done, silu_ready, hid_ready, hh_ready, hl_ready = (sem(n) for n in ("gate_up_done", "silu_ready", "hid_ready", "hh_ready", "hl_ready"))
        ffn_done, yt_ready, ld_xin, st_out = sem("ffn_done"), sem("yt_ready"), sem("ld_xin"), sem("st_out")
        f_added, out_ready = sem("f_added"), sem("out_ready")

        Q_PART, K_PART = (0, 0, 1, 0, 2, 1), (0, 1, 0, 2, 0, 1)
        SR = 6 * DK

        UNITS = [(b, w, c) for b in range(B) for c in range(KC) for w in range(2)]
        NU = len(UNITS)
        first_maxima = [(0, m) for m in range(64)] + ["turn"] + [(1, m) for m in range(32)]

        def first_maxima_after(kind, n):
            if kind == "v":
                at, count = 3 * (n - 2), 3
            else:
                at, count = 3 * (NT - 2) + 4 * (n - 2), 4
            return first_maxima[at:at + count] if n >= 2 else []

        score_bank = lambda c, e: (c + e) % 3
        max_bank = lambda c, m: (3, 6, 7)[(c + m) % 3]
        turn_bank = lambda c: max_bank(c + 1, 2)
        qk_banks = lambda u: slice(0, 2) if u % 2 == 0 else slice(4, 6)
        v_bank = lambda t: (2, 5)[t % 2]

        def over_groups(engine, body):
            body(0, 0)
            with engine.Fori(0, (NGRP - 4) // 3) as i:
                for c in range(1, 4):
                    body(i, c)
            for g in range(NGRP - 3, NGRP):
                body(0, g)

        def at_least(engine, semaphore, i, per, c):
            wait_for(engine, semaphore, i * per + c)

        def wait_for(engine, semaphore, count):
            if not isinstance(count, int) or count > 0:
                engine.wait_ge(semaphore, count)

        def ahead(engine):
            engine.wait_ge(ld_const, 48)

        block = ctx.enter_context(nc.Block())

        @block.sync
        def _(sp):
            sp.dma_start(pc[:, :], pcol).then_inc(ld_const, 16)
            sp.dma_start(cst[:, :], consts).then_inc(ld_const, 16)
            sp.dma_start(pr[:, :], prow).then_inc(ld_const, 16)
            sp.dma_start(win_sb[:, :, :], win.rearrange("(k p) d -> p k d", p=P)).then_inc(ld_win, 16)
            xf = x_feat.rearrange("(k p) t -> p k t", p=P)
            for s in range(2):
                for b in range(B):
                    t0 = b * L + s * HALF
                    sp.dma_start(xt[:, :, t0:t0 + HALF], xf[:, :, t0:t0 + HALF]).then_inc(ld_x[s], 16)

            def load_layer(i):
                for b in range(B):
                    r = slice(DH * b, DH * b + DH)
                    sp.dma_start(w1bd[r, :, r], w1[i].rearrange("d (c f) -> d c f", c=FC)).then_inc(ld_w, 16)
                    sp.dma_start(w2bd[r, :, r], w2[i].rearrange("(c f) d -> f c d", c=FC)).then_inc(ld_w, 16)

            sp.wait_ge(zeroed, 4)
            load_layer(0)
            for b in range(B):
                sp.dma_start(wout_sb[DH * b:DH * b + DH, b, :], wout).then_inc(ld_wout, 16)
            sp.dma_start(xres[:, :, :], x_tok.rearrange("(t p) d -> p t d", p=P)).then_inc(ld_xres, 16)
            sp.dma_start(main_sb[:, :, :], main_w.rearrange("(k p) n -> p k n", p=P)).then_inc(ld_bw, 16)
            sp.dma_start(ag_sb[:, :, :], ag_w.rearrange("(k p) n -> p k n", p=P)).then_inc(ld_bw, 16)
            sp.dma_start(lorab_sb[:, :], lora_b).then_inc(ld_bw, 16)
            for t in range(4):
                sp.dma_start(gw2_sb[NG * t:NG * t + NG, t, :], gw2).then_inc(ld_bw, 16)
            with sp.Fori(1, NL) as i:
                for s in range(2):
                    sp.wait_ge(down_done[s], i)
                for b in range(B):
                    r = slice(DH * b, DH * b + DH)
                    sp.dma_start(w1bd[r, :, r], w1[bass.ds(i, 1)].rearrange("o d (c f) -> (o d) c f", c=FC)).then_inc(ld_w, 16)
                    sp.dma_start(w2bd[r, :, r], w2[bass.ds(i, 1)].rearrange("o (c f) d -> (o f) c d", c=FC)).then_inc(ld_w, 16)
            for s in range(2):
                sp.wait_ge(yn_ready[s], NL + 1)
            sp.dma_start(wqkv_sb[:, :, :], wqkv.rearrange("w (k p) n -> p (w k) n", p=P)).then_inc(ld_qkv, 16)
            for q in range(4):
                sp.wait_ge(tile_ready, NT + 4 * q + 4)
                sp.dma_start(x2_dram.rearrange("(t p) d -> p t d", p=P)[:, 4 * q:4 * q + 4, :], xres[:, 4 * q:4 * q + 4, :]).then_inc(st_x2, 16)
            def load_stack(i, c):
                rows = lambda w, n: qk_dram[w, n].rearrange("(g j d) t -> g d j t", j=GH, d=DK)[i * 3 + c] if isinstance(i, int) else \
                    qk_dram[w, n].rearrange("(g j d) t -> g d j t", j=GH, d=DK)[bass.ds(i * 3 + c, 1)].rearrange("o d j t -> (o d) j t")
                for st, w, order in ((qst, 0, Q_PART), (kst, 1, K_PART)):
                    for m, n in enumerate(order):
                        sp.dma_start(st[c % 3][DK * m:DK * m + DK, :, :], rows(w, n)).then_inc(ld_stack[c % 3], 16)

            def load_v(i, c):
                src = v_dram[bass.ds(i * 3 + c, 1)].rearrange("o (k p) n -> p (o k) n", p=P)
                sp.dma_start(vg[c % 3][:, :, :], src).then_inc(ld_v[c % 3], 16)

            def load_nm(i, c):
                at_least(sp, nmt_read, i, 3, c + 1)
                for r, src in ((0, nmh), (1, nml)):
                    sp.dma_start(nm_dram[r], src[:, :]).then_inc(st_nm, 16)
                at_least(sp, st_nm, i, 3 * 32, 32 * (c + 1))
                sp.dma_start(qst[c % 3][SR:SR + 2, :, :].rearrange("r j t -> r (j t)"), nm_dram.rearrange("r p t -> r (p t)")).then_inc(ld_nm[c % 3], 16)

            def store_parts(u):
                b, w, c = UNITS[u]
                sp.wait_ge(lo_ready, u + 1)
                r0 = b * D + P * c
                sp.dma_start(qk_dram[w, :, r0:r0 + P, :].rearrange("n p t -> p n t"), parts[u % 2][:, :, :]).then_inc(st_parts[u % 2], 16)

            def store_v(t):
                sp.wait_ge(v_ready, t + 1)
                b, t0 = t // KT, t % KT * P
                dst = v_dram[b * NGRP // B:(b + 1) * NGRP // B, t0:t0 + P, :].rearrange("g p n -> p g n")
                sp.dma_start(dst, vpad[t % 2][:, :, :].rearrange("p (g j) e -> p g (j e)", j=GH)).then_inc(st_v[t % 2], 16)

            for u in range(2):
                store_parts(u)
            for k in range(2):
                sp.wait_ge(st_parts[k], 16)
            load_stack(0, 0)
            for t in range(NT):
                store_v(t)
            for k in range(2):
                sp.wait_ge(st_v[k], 128)
            load_stack(0, 1)
            for u in range(2, NU):
                store_parts(u)
                if u == 4:
                    for c in range(2):
                        load_v(0, c)
                if u == 10:
                    load_nm(0, 0)
            for k in range(2):
                sp.wait_ge(st_parts[k], 128)

            def store_o(i, c):
                at_least(sp, o_ready, i, 3, c + 1)
                for j in range(GH):
                    r0 = (i * 3 + c) * (GH * DK) + DK * j
                    sp.dma_start(o_dram[bass.ds(r0, DK), :], o_sb[2 * DK * j:2 * DK * j + DK, :]).then_inc(st_o, 16)
                    sp.dma_start(den_dram[bass.ds((i * 3 + c) * GH + j, 1), :], o_sb[2 * DK * j + DK:2 * DK * j + DK + 1, :]).then_inc(st_o, 16)

            def group(i, c):
                last = isinstance(i, int) and 3 * i + c + 2 >= NGRP
                if not last:
                    at_least(sp, score_done, i, 192, 64 * c)
                    load_stack(i, c + 2)
                if not (isinstance(i, int) and 3 * i + c == 0):
                    store_o(i, c - 1)
                if not last:
                    at_least(sp, pv_done, i, 48, 16 * c)
                    load_v(i, c + 2)
                if not (isinstance(i, int) and 3 * i + c + 1 >= NGRP):
                    load_nm(i, c + 1)

            over_groups(sp, group)
            store_o(0, NGRP - 1)
            sp.wait_ge(st_o, 128 * NGRP)
            sp.wait_ge(score_done, 64 * NGRP)
            sp.wait_ge(exp_done, 64 * NGRP)
            sp.wait_ge(pv_done, 2 * KT * NGRP)
            sp.wait_ge(tern_chain, 72)
            sp.wait_ge(nmt_read, NGRP)
            sp.dma_start(den_sb[:, :, :].rearrange("p k t -> p (k t)"), den_dram.rearrange("n (a t) -> (n a) t", a=2)).then_inc(ld_den, 16)
            sp.dma_start(wo_sb[:, :, :], wo.rearrange("(k p) n -> p k n", p=P)).then_inc(ld_qkv, 16)
            sp.wait_ge(den_ready, 1)
            sp.dma_start(rec_dram.rearrange("n (a t) -> (n a) t", a=2), den_sb[:, :, :].rearrange("p k t -> p (k t)")).then_inc(st_rec, 16)

            def load_attn(q):
                b, a = q // 2, q % 2
                for k in range(4):
                    if q == 0 and k == 0:
                        sp.wait_ge(st_rec, 16)
                    elif q > 0:
                        sp.wait_ge(oproj_done, 4 * q - 4 + k + 1)
                    t0 = a * HALF + k * P
                    sp.dma_start(od[k][:, :, :], o_dram[b * D:b * D + D, t0:t0 + P].rearrange("(k p) t -> p k t", p=P)).then_inc(ld_od[q % 2], 16)
                if q > 0:
                    sp.wait_ge(normed, 4 * q)
                for k in range(KC):
                    h0, n = b * NH + k * (NH // KC), NH // KC
                    sp.dma_start(rb[:, k, :], rec_dram[h0:h0 + n, a * HALF:a * HALF + HALF].unsqueeze(1).to_broadcast([n, DK, HALF])).then_inc(ld_rb, 16)
                if q >= 2:
                    sp.wait_ge(st_x3, 64 * (q - 1))
                for k in range(4):
                    t, slot = 4 * q + k, 4 * (q % 2) + k
                    if q >= 2:
                        sp.wait_ge(x3_tr, t - 8 + 1)
                    sp.dma_start(x3t[slot][:, :], x2_dram[P * t:P * t + P, :]).then_inc(ld_x2t[q % 2], 16)

            def store_x3(q):
                for k in range(4):
                    t, slot = 4 * q + k, 4 * (q % 2) + k
                    sp.wait_ge(x3_ready, t + 1)
                    sp.dma_start(x3_dram[P * t:P * t + P, :], x3t[slot][:, :]).then_inc(st_x3, 16)

            load_attn(0)
            load_attn(1)
            for q in range(4):
                store_x3(q)
                if q < 2:
                    load_attn(q + 2)
            sp.wait_ge(st_x3, 16 * NT)
            sp.wait_ge(x3_tr, NT)

            def write_out(n):
                wait_for(sp, f_added, n * 4)
                sp.dma_start(xin[:, :, :], x3_dram.rearrange("(n k p) d -> p n k d", p=P, k=4)[:, bass.ds(n, 1)].rearrange("p o k d -> p (o k) d")).then_inc(ld_xin, 16)
                for k in range(4):
                    sp.wait_ge(out_ready, n * 4 + k + 1)
                    sp.dma_start(out[bass.ds(n * HALF + k * P, P), :], yt[:, k, :]).then_inc(st_out, 16)

            write_out(0)
            with sp.Fori(1, 4) as n:
                write_out(n)
            sp.wait_ge(st_out, 16 * NT)

        @block.gpsimd
        def _(pool):
            nc.gpsimd.memset(mhalf[:, :], -0.5).then_inc(pool_chain, 1)
            pool.wait_ge(pool_chain, 1)
            pool.wait_ge(mag2_ready, 1)
            nc.gpsimd.tensor_tensor(pw[:, 3, :], pw[:, 2, :], mhalf[:, 0:NL], ALU.pow).then_inc(invm_ready, 1)

            def ln_rstd(n, s):
                pool.wait_ge(var_ready[s], n + 1)
                nc.gpsimd.tensor_tensor(rstd8[s][:, :], var8[s][:, :], mhalf[:, 0:8], ALU.pow).then_inc(rstd_ready[s], 1)

            pool.wait_ge(ld_const, 48)
            pool.wait_ge(ld_xres, 16)
            nc.gpsimd.tensor_tensor(xres[:, :, :], xres[:, :, :], pr[:, R_BOUT:R_BOUT + D].unsqueeze(1).to_broadcast([P, NT, D]), ALU.add).then_inc(xres_biased, 1)
            with pool.Fori(0, NL) as i:
                for s in range(2):
                    ln_rstd(i * 2, s)
                for s in range(2):
                    sl = slice(s * HALF, s * HALF + HALF)
                    ahead(pool)
                    pool.wait_ge(y_ready[s], i + 1)
                    nc.gpsimd.tensor_tensor(im_in[s][:, :], sin[:, bass.ds(i, 1), sl].rearrange("p o t -> p (o t)"), y[s][:, :], ALU.mult).then_inc(im_in_ready[s], 1)
                for s in range(2):
                    sl = slice(s * HALF, s * HALF + HALF)
                    ahead(pool)
                    pool.wait_ge(zi_ready[s], i + 1)
                    nc.gpsimd.tensor_tensor(im_p[s][:, :], sin[:, bass.ds(i, 1), sl].rearrange("p o t -> p (o t)"), zi[s][:, :], ALU.mult).then_inc(im_p_ready[s], 1)
                for s in range(2):
                    ln_rstd(i * 2 + 1, s)
            for s in range(2):
                ln_rstd(2 * NL, s)

            def rstd_tiles(r):
                for q in range(4):
                    sl = slice(4 * q, 4 * q + 4)
                    pool.wait_ge(var4_ready, 4 * r + q + 1)
                    nc.gpsimd.tensor_tensor(rstd[:, sl], varr[:, sl], mhalf[:, sl], ALU.pow).then_inc(rstd4_ready, 1)

            rstd_tiles(0)
            pool.wait_ge(gvar_ready, 1)
            nc.gpsimd.tensor_tensor(gs[:, 2, :], gs[:, 1, :], mhalf[:, :], ALU.pow).then_inc(grstd_ready, 1)
            rstd_tiles(1)

            for c in range(24):
                if c >= 2:
                    pool.wait_ge(abs_done, c - 1)
                elif c == 0:
                    pool.wait_ge(tile_ready, 2 * NT)
                    pool.wait_ge(tmpwt_ready, 4)
                    pool.wait_ge(tr_done, 2 * NT)
                    pool.wait_ge(st_x2, 64)
                pool.dma_start(wabs[:, c % 2, :], tern[c]).then_inc(ld_abs[c % 2], 16)
            pool.wait_ge(thr_ready, 1)
            pool.wait_ge(qk_done, NU)
            for k in range(2):
                pool.wait_ge(st_parts[k], 128)
            pch = Chain(pool, tern_chain)
            for c in range(24):
                w = c // 8
                pool.dma_start(wraw[:, :], tern[c]).then_inc(ld_tern, 16)
                pool.wait_ge(ld_tern, 16 * c + 16)
                pch.step(nc.gpsimd.tensor_scalar(tern_sb[:, c, :], wraw[:, :], thr[:, w:w + 1], None, ALU.is_gt))
                pch.step(nc.gpsimd.tensor_scalar(wraw[:, :], wraw[:, :], nthr[:, w:w + 1], None, ALU.is_lt))
                pch.step(nc.gpsimd.tensor_tensor(tern_sb[:, c, :], tern_sb[:, c, :].bitcast(F32), wraw[:, :], ALU.subtract))
            for r, applied in ((0, x3_ready), (4, out_ready)):
                for q in range(4):
                    pool.wait_ge(x_var, q + r + 1)
                    wait_for(pool, applied, q * 4)
                    nc.gpsimd.tensor_tensor(rstd[:, 0:4], varr[:, 0:4], mhalf[:, 0:4], ALU.pow).then_inc(x_rstd, 1)

        @block.scalar
        def _(act):
            act.wait_ge(ld_const, 48)
            act.wait_ge(mag_ready, 1)
            nc.scalar.activation(pw[:, 5, :], pw[:, 4, :], ACT.Tanh).then_inc(decay_ready, 1)
            for s in range(2):
                act.wait_ge(inproj[s], 1)
                nc.scalar.activation(h[:, s, :], ps_c[s], ACT.Identity, bias=pc[:, Q_BIN:Q_BIN + 1]).then_inc(h_ready[s], 1)

            def ln_square(n, s):
                act.wait_ge(centered[s], n + 1)
                nc.scalar.activation(sq[s][:, :], ps_c[s], ACT.Square).then_inc(squared[s], 1)
                nc.scalar.activation(hc[s][:, :], ps_c[s], ACT.Copy).then_inc(hc_copied[s], 1)

            col = lambda base, i: pc[:, bass.ds(base + i, 1)]
            with act.Fori(0, NL) as i:
                for s in range(2):
                    ln_square(2 * i, s)
                for s in range(2):
                    ahead(act)
                    act.wait_ge(z_ready[s], 2 * i + 1)
                    nc.scalar.activation(y[s][:, :], z[s][:, :], ACT.Silu, bias=col(Q_L1B, i), scale=col(Q_L1W, i)).then_inc(y_ready[s], 1)
                for s in range(2):
                    ln_square(2 * i + 1, s)
                for s in range(2):
                    ahead(act)
                    act.wait_ge(z_ready[s], 2 * i + 2)
                    nc.scalar.activation(y[s][:, :], z[s][:, :], ACT.Identity, bias=col(Q_L2B, i), scale=col(Q_L2W, i)).then_inc(yn_ready[s], 1)
                for c in range(FC):
                    for s in range(2):
                        ahead(act)
                        act.wait_ge(up_done[s], FC * i + c + 1)
                        nc.scalar.activation(g[s][:, c, :], ps_f[s][c % 2], ACT.Silu, bias=pc[:, bass.ds(Q_B1 + i * FC + c, 1)]).then_inc(g_ready[s], 1)

            for s in range(2):
                ln_square(2 * NL, s)
            for s in range(2):
                act.wait_ge(z_ready[s], 2 * NL + 1)
                nc.scalar.activation(y[s][:, :], z[s][:, :], ACT.Identity, bias=pc[:, Q_LNB:Q_LNB + 1], scale=pc[:, Q_LNW:Q_LNW + 1]).then_inc(yn_ready[s], 1)

            def evac_x(n, t):
                act.wait_ge(tr_done, n + 1)
                nc.scalar.activation(x1t[:, :, P * t:P * t + P], psum[:, 4 + n % 2, :].rearrange("p (k t) -> p k t", k=KC), ACT.Copy).then_inc(xt_ready, 1)

            for t in range(NT):
                evac_x(t, t)
                if t >= 1:
                    act.wait_ge(lg_done, t)
                    nc.scalar.activation(lg[:, t - 1, :], psum[:, 6 + (t - 1) % 2, 0:P + NG], ACT.Copy).then_inc(lg_ready, 1)
            act.wait_ge(lg_done, NT)
            nc.scalar.activation(lg[:, NT - 1, :], psum[:, 6 + (NT - 1) % 2, 0:P + NG], ACT.Copy).then_inc(lg_ready, 1)
            act.wait_ge(ght_done, 1)
            nc.scalar.activation(ght[:, :, :], psum[:, 4, :].rearrange("p (q t) -> p q t", q=4), ACT.Copy).then_inc(ght_ready, 1)
            act.wait_ge(gap_ready, 1)
            nc.scalar.activation(gs[:, 5, :], gs[:, 4, :], ACT.Exp).then_inc(gexp_ready, 1)
            for q in range(4):
                act.wait_ge(wtr_done, q + 1)
                nc.scalar.activation(tmpwt[:, 4 * q:4 * q + 4, :], psum[:, 6 + q % 2, :].rearrange("p (t n) -> p t n", t=4), ACT.Copy).then_inc(tmpwt_ready, 1)
                if q >= 1:
                    for t in range(4 * q - 4, 4 * q):
                        evac_x(NT + t, t)
            for t in range(NT - 4, NT):
                evac_x(NT + t, t)

            def abs_chunk(c):
                act.wait_ge(ld_abs[c % 2], 16 * (c // 2) + 16)
                nc.scalar.activation(wabs[:, c % 2, :], wabs[:, c % 2, :], ACT.Abs, accum_out=absum[:, c:c + 1]).then_inc(abs_done, 1)

            def hi_part(u):
                act.wait_ge(qk_done, u + 1)
                if u >= 2:
                    act.wait_ge(st_parts[u % 2], 16 * (u // 2))
                nc.scalar.activation(parts[u % 2][:, 0, :], psum[:, qk_banks(u), :].rearrange("p a t -> p (a t)"), ACT.Copy).then_inc(hi_ready, 1)

            def mid_part(u):
                act.wait_ge(r1_ready, u + 1)
                nc.scalar.activation(parts[u % 2][:, 1, :], resid[u % 2][:, :], ACT.Copy).then_inc(mid_ready, 1)

            act.wait_ge(st_x2, 64)
            for f, u in ((hi_part, 0), (hi_part, 1), (mid_part, 0), (mid_part, 1)):
                f(u)
            act.wait_ge(vpad_ready, 4)
            for t in range(NT):
                act.wait_ge(v_done, t + 1)
                if t >= 2:
                    act.wait_ge(st_v[t % 2], 16 * (t // 2))
                nc.scalar.activation(vpad[t % 2][:, :, 0:DK], psum[:, v_bank(t), :].rearrange("p (h d) -> p h d", d=DK), ACT.Copy).then_inc(v_ready, 1)
                abs_chunk(t)
            for u in range(2, NU):
                hi_part(u)
                if u >= 3:
                    mid_part(u - 1)
                if u < 10:
                    abs_chunk(NT + u - 2)
            mid_part(NU - 1)

            def group(i, c):
                first = isinstance(i, int) and 3 * i + c == 0
                for e in range(2 * GH * KT):
                    n, a = e // 2, e % 2
                    at_least(act, score_done, i, 192, 64 * c + e + 1)
                    if e % (2 * GH) == 0:
                        at_least(act, pv_done, i, 48, 16 * c + 2 * (n // GH) - 2)
                    nc.scalar.activation(probs[n % (2 * GH)][:, a * HALF:a * HALF + HALF], psum[:, score_bank(c, e), :], ACT.Exp, scale=DK ** -0.5).then_inc(exp_done, 1)
                    if e == 2 * GH - 1 and not first:
                        copy_o(i, c - 1)

            def copy_o(i, c):
                at_least(act, pv_done, i, 48, 16 * c + 16)
                at_least(act, st_o, i, 3 * 128, 128 * c)
                nc.scalar.activation(o_sb[:, :], psum[:, 4:6, :].rearrange("p a t -> p (a t)"), ACT.Copy).then_inc(o_ready, 1)

            over_groups(act, group)
            copy_o(0, NGRP - 1)
            for t in range(NT):
                act.wait_ge(x3_tr, t + 1)
                nc.scalar.activation(x3h[:, :, P * t:P * t + P], psum[:, 4 + t % 4, :].rearrange("p (k t) -> p k t", k=KC), ACT.Copy).then_inc(x3h_ready, 1)
            act.wait_ge(x3l_ready, NT)

            def ffn_block(n):
                for f in range(HC):
                    act.wait_ge(gate_up_done, n * HC + f + 1)
                    wait_for(act, hid_ready, n * HC + f - 1)
                    nc.scalar.activation(sg[f % 2][:, :], psum[:, 4 + 2 * (f % 2), :], ACT.Silu, scale=pc[:, Q_GS + f:Q_GS + f + 1]).then_inc(silu_ready, 1)
                    act.wait_ge(hid_ready, n * HC + f + 1)
                    wait_for(act, ffn_done, n * HC + f - 1)
                    nc.scalar.activation(hh[f % 2][:, :], hid[f % 2][:, :], ACT.Copy).then_inc(hh_ready, 1)

            ffn_block(0)
            with act.Fori(1, 4) as n:
                ffn_block(n)

        @block.vector
        def _(dve):
            ch = Chain(dve, dve_chain)
            nc.vector.memset(w1bd[:, :, :], 0.0).then_inc(zeroed, 1)
            nc.vector.memset(w2bd[:, :, :], 0.0).then_inc(zeroed, 1)
            nc.vector.memset(wout_sb[:, :, :], 0.0).then_inc(zeroed, 1)
            nc.vector.memset(gw2_sb[:, :, :], 0.0).then_inc(zeroed, 1)
            nc.vector.memset(cos[:, :, 0:1], 1.0)
            nc.vector.memset(sin[:, :, 0:1], 0.0)
            dve.wait_ge(ld_const, 48)
            tt = lambda o, a, b_, op: ch.step(nc.vector.tensor_tensor(o, a, b_, op))
            ts = lambda o, a, s1, s2, o0, o1: ch.step(nc.vector.tensor_scalar(o, a, s1, s2, o0, o1))
            q = lambda base: pc[:, base:base + NL]
            w = lambda k: pw[:, k, :]
            tt(w(0), q(Q_RE), q(Q_RE), ALU.mult)
            tt(w(1), q(Q_IM), q(Q_IM), ALU.mult)
            tt(w(0), w(0), w(1), ALU.add)
            ts(w(8), w(0), 1e-30, None, ALU.is_ge, ALU.bypass)
            nc.vector.tensor_scalar(w(2), w(0), 1e-30, None, ALU.max).then_inc(mag2_ready, 1)
            dve.wait_ge(invm_ready, 1)
            nc.vector.tensor_tensor(w(4), w(2), w(3), ALU.mult).then_inc(mag_ready, 1)
            tt(w(9), w(3), w(8), ALU.mult)
            ts(w(10), w(8), -1.0, 1.0, ALU.mult, ALU.add)
            tt(w(6), q(Q_RE), w(9), ALU.mult)
            tt(w(6), w(6), w(10), ALU.add)
            tt(w(7), q(Q_IM), w(9), ALU.mult)
            tt(w(0), w(6), q(Q_LR), ALU.mult)
            tt(w(1), w(7), q(Q_LI), ALU.mult)
            tt(w(11), w(0), w(1), ALU.subtract)
            tt(w(0), w(6), q(Q_LI), ALU.mult)
            tt(w(1), w(7), q(Q_LR), ALU.mult)
            tt(w(0), w(0), w(1), ALU.add)
            ts(w(12), w(0), -1.0, None, ALU.mult, ALU.bypass)
            n = 1
            while n < L:
                bc = lambda k: w(k).unsqueeze(2).to_broadcast([P, NL, n])
                c0, s0, a, b_ = cos[:, :, 0:n], sin[:, :, 0:n], tab1[:, :, 0:n], tab2[:, :, 0:n]
                nc.vector.tensor_tensor(a, c0, bc(6), ALU.mult)
                tt(b_, s0, bc(7), ALU.mult)
                tt(cos[:, :, n:2 * n], a, b_, ALU.subtract)
                nc.vector.tensor_tensor(a, c0, bc(7), ALU.mult)
                tt(b_, s0, bc(6), ALU.mult)
                tt(sin[:, :, n:2 * n], a, b_, ALU.add)
                n *= 2
                if n < L:
                    tt(w(0), w(6), w(6), ALU.mult)
                    tt(w(1), w(7), w(7), ALU.mult)
                    tt(w(9), w(6), w(7), ALU.mult)
                    tt(w(6), w(0), w(1), ALU.subtract)
                    ts(w(7), w(9), 2.0, None, ALU.mult, ALU.bypass)
                    tt(w(0), w(6), w(6), ALU.mult)
                    tt(w(1), w(7), w(7), ALU.mult)
                    tt(w(0), w(0), w(1), ALU.add)
                    ts(w(0), w(0), -0.5, 1.5, ALU.mult, ALU.add)
                    tt(w(6), w(6), w(0), ALU.mult)
                    tt(w(7), w(7), w(0), ALU.mult)
            dve.wait_ge(decay_ready, 1)
            nc.vector.tensor_copy(w(13), w(5)).then_inc(tables_ready, 1)
            dve.wait_ge(tables_ready, 1)

            def ln_var(n, s):
                dve.wait_ge(var_sums[s], n + 1)
                nc.vector.tensor_scalar(var8[s][:, :], ps_b[s][:, 0:8], EPS, None, ALU.add).then_inc(var_ready[s], 1)

            def ln_scale(n, s):
                dve.wait_ge(spread[s], n + 1)
                dve.wait_ge(hc_copied[s], n + 1)
                nc.vector.tensor_tensor(z[s][:, :], ps_b[s], hc[s][:, :], ALU.mult).then_inc(z_ready[s], 1)

            start, PER = ch.n, 8
            with dve.Fori(0, NL) as i:
                ch.base, ch.n = start + i * PER, 0
                wcol = lambda k: pw[:, k, bass.ds(i, 1)]
                for s in range(2):
                    ln_var(2 * i, s)
                for s in range(2):
                    ln_scale(2 * i, s)
                for s in range(2):
                    sl = slice(s * HALF, s * HALF + HALF)
                    dve.wait_ge(y_ready[s], i + 1)
                    tt(re_in[s][:, :], cos[:, bass.ds(i, 1), sl].rearrange("p o t -> p (o t)"), y[s][:, :], ALU.mult)
                    first = wcol(11) if s == 0 else zr[0][:, HALF - 1:HALF]
                    ch.step(nc.vector.tensor_tensor_scan(zr[s][:, :], wcol(13).to_broadcast([P, HALF]), re_in[s][:, :], first, ALU.mult, ALU.add))
                    dve.wait_ge(im_in_ready[s], i + 1)
                    first = wcol(12) if s == 0 else zi[0][:, HALF - 1:HALF]
                    nc.vector.tensor_tensor_scan(zi[s][:, :], wcol(13).to_broadcast([P, HALF]), im_in[s][:, :], first, ALU.mult, ALU.add).then_inc(zi_ready[s], 1)
                    tt(re_p[s][:, :], cos[:, bass.ds(i, 1), sl].rearrange("p o t -> p (o t)"), zr[s][:, :], ALU.mult)
                    if s == 0:
                        dve.wait_ge(zi_ready[0], i + 1)
                for s in range(2):
                    dve.wait_ge(im_p_ready[s], i + 1)
                    tt(re_p[s][:, :], re_p[s][:, :], im_p[s][:, :], ALU.add)
                    nc.vector.scalar_tensor_tensor(h[:, s, :], re_p[s][:, :], pc[:, bass.ds(Q_SCL + i, 1)], h[:, s, :], ALU.mult, ALU.add).then_inc(h_ready[s], 1)
                for s in range(2):
                    ln_var(2 * i + 1, s)
                for s in range(2):
                    ln_scale(2 * i + 1, s)
                for s in range(2):
                    dve.wait_ge(down_done[s], i + 1)
                    nc.vector.scalar_tensor_tensor(h[:, s, :], ps_c[s], pc[:, bass.ds(Q_B2 + i, 1)], h[:, s, :], ALU.add, ALU.add).then_inc(h_ready[s], 1)
                assert ch.n == PER
            ch.base, ch.n = 0, start + NL * PER
            for s in range(2):
                ln_var(2 * NL, s)
            for s in range(2):
                ln_scale(2 * NL, s)

            def ln_tiles(r, q, projected):
                for t in range(4 * q, 4 * q + 4):
                    dve.wait_ge(projected, t + 1)
                    nc.vector.tensor_tensor(xres[:, t, :], psum[:, t % 4, :], xres[:, t, :], ALU.add).then_inc(added, 1)
                for t in range(4 * q, 4 * q + 4):
                    dve.wait_ge(added, NT * r + t + 1)
                    nc.vector.bn_stats(stats[:, t % 4, :], xres[:, t, :]).then_inc(dve_chain, 1)
                    ch.n += 1
                for t in range(4 * q, 4 * q + 4):
                    dve.wait_ge(dve_chain, ch.n - 3 if t % 4 == 0 else ch.n - 3)
                    ch.step(nc.vector.bn_aggr(mv[:, t, :], stats[:, t % 4, :]))
                sl = slice(4 * q, 4 * q + 4)
                nc.vector.tensor_scalar(varr[:, sl], mv[:, sl, 1], EPS, None, ALU.add).then_inc(var4_ready, 1)
                dve.wait_ge(rstd4_ready, 4 * r + q + 1)
                for t in range(4 * q, 4 * q + 4):
                    nc.vector.tensor_scalar(xres[:, t, :], xres[:, t, :], mv[:, t, 0:1], rstd[:, t:t + 1], ALU.subtract, ALU.mult).then_inc(tile_ready, 1)

            dve.wait_ge(xres_biased, 1)
            for q in range(4):
                ln_tiles(0, q, proj_done)

            row = lambda r0, n, t: pr[:, r0:r0 + n].unsqueeze(1).to_broadcast([P, t, n])
            over = lambda a, n: a.unsqueeze(2).to_broadcast([P, NT, n])
            G = lambda k: gs[:, k, :]
            red = lambda o, a, op: ch.step(nc.vector.tensor_reduce(o, a, AX.X, op))
            dve.wait_ge(lg_ready, NT)
            tt(gh[:, :, :], lg[:, :, P:P + NG], row(R_GB1, NG, NT), ALU.add)
            red(G(0), gh[:, :, :], ALU.add)
            ts(G(0), G(0), 1.0 / NG, None, ALU.mult, ALU.bypass)
            tt(gh[:, :, :], gh[:, :, :], over(G(0), NG), ALU.subtract)
            tt(gsq[:, :, :], gh[:, :, :], gh[:, :, :], ALU.mult)
            red(G(1), gsq[:, :, :], ALU.add)
            nc.vector.tensor_scalar(G(1), G(1), 1.0 / NG, EPS, ALU.mult, ALU.add).then_inc(gvar_ready, 1)
            dve.wait_ge(grstd_ready, 1)
            tt(gh[:, :, :], gh[:, :, :], over(G(2), NG), ALU.mult)
            tt(gh[:, :, :], gh[:, :, :], row(R_GAM, NG, NT), ALU.mult)
            tt(gh[:, :, :], gh[:, :, :], row(R_BET, NG, NT), ALU.add)
            nc.vector.tensor_scalar(gh[:, :, :], gh[:, :, :], 0.0, None, ALU.max).then_inc(gh_ready, 1)
            E_ = lambda k: ge[:, k, :, :]
            revb = rev.unsqueeze(1).to_broadcast([P, NT, NE])
            dve.wait_ge(gates_done, 1)
            tt(E_(0), psum[:, 5, 0:P].rearrange("p (t e) -> p t e", t=NT), row(R_GB2, NE, NT), ALU.add)

            def top(k, gates, best):
                red(best, gates, ALU.max)
                tt(E_(2), gates, over(best, NE), ALU.is_equal)
                tt(E_(2), E_(2), revb, ALU.mult)
                red(G(6), E_(2), ALU.max)
                tt(oh[:, k, :, :], E_(2), over(G(6), NE), ALU.is_equal)

            top(0, E_(0), G(3))
            ts(E_(3), oh[:, 0, :, :], -3e38, None, ALU.mult, ALU.bypass)
            tt(E_(1), E_(0), E_(3), ALU.add)
            top(1, E_(1), G(7))
            nc.vector.tensor_tensor(G(4), G(7), G(3), ALU.subtract).then_inc(gap_ready, 1)
            nc.vector.tensor_copy(E_(4), oh[:, 0, :, :]).then_inc(oh_ready, 1)
            dve.wait_ge(gexp_ready, 1)
            ts(G(8), G(5), 1.0, None, ALU.add, ALU.bypass)
            ch.step(nc.vector.reciprocal(G(8), G(8)))
            tt(G(9), G(5), G(8), ALU.mult)
            dve.wait_ge(cnt_done, 1)
            red(cnt[:, :, :], psum[:, 4, 0:2 * P].rearrange("p (k t e) -> p k e t", k=2, t=NT), ALU.add)
            ts(cnt[:, :, :], cnt[:, :, :], float(CAPACITY), 1.0 / ER, ALU.is_le, ALU.mult)
            for k in range(2):
                tt(E_(k), oh[:, k, :, :], over(G(8 + k), NE), ALU.mult)
                tt(E_(k), E_(k), cnt[:, k, :].unsqueeze(1).to_broadcast([P, NT, NE]), ALU.mult)
            tt(wexp[:, :, :], E_(0), E_(1), ALU.add)
            for q in range(4):
                sl = slice(4 * q, 4 * q + 4)
                nc.vector.tensor_tensor(tmpw[:, sl, :].rearrange("p t (e r) -> p t e r", e=NE), lg[:, sl, 0:P].rearrange("p t (e r) -> p t e r", e=NE),
                                        wexp[:, sl, :].unsqueeze(3).to_broadcast([P, 4, NE, ER]), ALU.mult).then_inc(tmpw_ready, 1)
            for q in range(4):
                ln_tiles(1, q, bproj_done)

            def first_part(u):
                dve.wait_ge(hi_ready, u + 1)
                if u >= 2:
                    dve.wait_ge(lo_ready, u - 1)
                nc.vector.tensor_tensor(resid[u % 2][:, :], psum[:, qk_banks(u), :].rearrange("p a t -> p (a t)"), parts[u % 2][:, 0, :], ALU.subtract).then_inc(r1_ready, 1)

            def last_part(u):
                dve.wait_ge(mid_ready, u + 1)
                nc.vector.tensor_tensor(parts[u % 2][:, 2, :], resid[u % 2][:, :], parts[u % 2][:, 1, :], ALU.subtract).then_inc(lo_ready, 1)

            def maximum(i, c, m):
                qt, j, a = m // (2 * GH), m // 2 % GH, m % 2
                at_least(dve, mx_done, i, 192, 64 * c + m + 1)
                nc.vector.tensor_reduce(mx[c % 2][:, j, qt, a:a + 1], psum[:, max_bank(c, m), :], AX.X, ALU.max).then_inc(mx_read, 2)

            def finish_maxima(i, c):
                at_least(dve, mx_read, i, 2 * 192, 2 * (64 * c + 64))
                at_least(dve, nmt_done, i, 3, c)
                nc.vector.tensor_reduce(nm[:, :].rearrange("p (j q) -> p j q", j=GH), mx[c % 2][:, :, :, :], AX.X, ALU.max, negate=True).then_inc(nm_ready, 1)
                at_least(dve, nmt_done, i, 3, c + 1)
                if not (isinstance(i, int) and 3 * i + c == 0):
                    dve.wait_ge(ld_nm[(c - 1) % 3], ((i + (c - 1) // 3) + 1) * 16)
                ch2.step(nc.vector.tensor_copy(nmh[:, :], psum[0:GH * KT, turn_bank(c), 0:P]))
                nc.vector.tensor_tensor(nml[:, :], psum[0:GH * KT, turn_bank(c), 0:P], nmh[:, :], ALU.subtract).then_inc(nmt_read, 1)

            def first_maxima_of(kind, n):
                for what in first_maxima_after(kind, n):
                    if what == "turn":
                        finish_maxima(0, 0)
                    else:
                        maximum(0, *what)

            ch2 = Chain(dve, nmh_ready)
            dve.wait_ge(tmpwt_ready, 4)
            dve.wait_ge(bproj_done, NT)
            dve.wait_ge(tr_done, 2 * NT)
            dve.wait_ge(st_x2, 64)
            for k in range(2):
                nc.vector.memset(vpad[k][:, :, DK:DK + 1], 1.0).then_inc(vpad_ready, 1)
                nc.vector.memset(vpad[k][:, :, DK + 1:], 0.0).then_inc(vpad_ready, 1)
            for k in range(3):
                nc.vector.memset(kst[k][SR:SR + 2, :, :], 1.0).then_inc(ones_ready, 1)
            for f, u in ((first_part, 0), (first_part, 1), (last_part, 0), (last_part, 1)):
                f(u)
            for t in range(NT):
                first_maxima_of("v", t)
            for u in range(2, NU):
                first_maxima_of("u", u)
                first_part(u)
                if u >= 3:
                    last_part(u - 1)
                if u == 12:
                    dve.wait_ge(abs_done, 24)
                    nc.vector.tensor_reduce(absum3[:, :], absum[:, :].rearrange("p (w c) -> p w c", w=3), AX.X, ALU.add).then_inc(abs_sum, 1)
                if u == 13:
                    dve.wait_ge(abs_all, 1)
                    ts(thr[:, :], psum[:, 2, 0:3], 1.0 / (D * HID), THRESH, ALU.mult, ALU.mult)
                    nc.vector.tensor_scalar(nthr[:, :], thr[:, :], -1.0, None, ALU.mult).then_inc(thr_ready, 1)
            last_part(NU - 1)

            def group(i, c):
                ch2.base, ch2.n = i * 3 + c + 1, 0
                g = 3 * i + c if isinstance(i, int) else 1
                if g + 1 < NGRP:
                    for m in range(32, 64):
                        maximum(i, c + 1, m)
                    finish_maxima(i, c + 1)
                if g + 2 < NGRP:
                    for m in range(32):
                        maximum(i, c + 2, m)

            over_groups(dve, group)
            dve.wait_ge(ld_den, 16)
            nc.vector.reciprocal(den_sb[:, :, :], den_sb[:, :, :]).then_inc(den_ready, 1)

            def normalise(q):
                dve.wait_ge(ld_rb, 64 * q + 64)
                dve.wait_ge(ld_od[q % 2], 64 * (q // 2) + 64)
                for k in range(4):
                    nc.vector.tensor_tensor(od[k][:, :, :], od[k][:, :, :], rb[:, :, P * k:P * k + P], ALU.mult).then_inc(normed, 1)

            def ln_stats(r, q, x, added):
                for k in range(4):
                    dve.wait_ge(added, q * 4 + k + 1)
                    nc.vector.bn_stats(stats[:, k, :], x(k)).then_inc(x_stats, 1)
                dve.wait_ge(x_stats, q * 4 + 4 * r + 4)
                nc.vector.memset(varr[:, 0:4], EPS).then_inc(x_mv, 1)
                for k in range(4):
                    nc.vector.bn_aggr(mv[:, k, :], stats[:, k, :]).then_inc(x_mv, 1)
                dve.wait_ge(x_mv, q * 5 + 5 * r + 5)
                nc.vector.tensor_tensor(varr[:, 0:4], mv[:, 0:4, 1], varr[:, 0:4], ALU.add).then_inc(x_var, 1)

            def ln_apply(r, q, x, ready):
                dve.wait_ge(x_rstd, q + r + 1)
                for k in range(4):
                    nc.vector.tensor_scalar(x(k), x(k), mv[:, k, 0:1], rstd[:, k:k + 1], ALU.subtract, ALU.mult).then_inc(ready, 1)

            normalise(0)
            for q in range(4):
                x = lambda k: x3t[4 * (q % 2) + k][:, :]
                dve.wait_ge(ld_x2t[q % 2], 64 * (q // 2) + 64)
                for k in range(4):
                    dve.wait_ge(oproj_done, 4 * q + k + 1)
                    nc.vector.tensor_tensor(x(k), psum[:, k, :], x(k), ALU.add).then_inc(x_added, 1)
                ln_stats(0, q, x, x_added)
                if q < 3:
                    normalise(q + 1)
                ln_apply(0, q, x, x3_ready)
                for t in range(4 * q, 4 * q + 4):
                    dve.wait_ge(x3h_ready, t + 1)
                    nc.vector.tensor_tensor(x3l[:, :, P * t:P * t + P], psum[:, 4 + t % 4, :].rearrange("p (k t) -> p k t", k=KC), x3h[:, :, P * t:P * t + P].bitcast(F32), ALU.subtract).then_inc(x3l_ready, 1)
            yk = lambda k: yt[:, k, :]

            def hidden(n, f):
                dve.wait_ge(silu_ready, n * HC + f + 1)
                wait_for(dve, hl_ready, n * HC + f - 1)
                nc.vector.scalar_tensor_tensor(hid[f % 2][:, :], psum[:, 5 + 2 * (f % 2), :], pc[:, Q_US + f:Q_US + f + 1], sg[f % 2][:, :], ALU.mult, ALU.mult).then_inc(hid_ready, 1)
                dve.wait_ge(hh_ready, n * HC + f + 1)
                wait_for(dve, ffn_done, n * HC + f - 1)
                nc.vector.tensor_tensor(hl[f % 2][:, :], hid[f % 2][:, :], hh[f % 2][:, :].bitcast(F32), ALU.subtract).then_inc(hl_ready, 1)

            def finish(n):
                dve.wait_ge(ld_xin, n * 16 + 16)
                for k in range(4):
                    dve.wait_ge(yt_ready, n * 4 + k + 1)
                    nc.vector.tensor_tensor(yk(k), yk(k), xin[:, k, :], ALU.add).then_inc(f_added, 1)
                ln_stats(4, n, yk, f_added)
                ln_apply(4, n, yk, out_ready)

            def block_of_tokens(n, first):
                for f in range(HC):
                    hidden(n, f)
                    if f == 0 and not first:
                        finish(n - 1)
                dve.wait_ge(ffn_done, n * HC + HC)
                wait_for(dve, st_out, n * 64)
                for k in range(4):
                    nc.vector.tensor_tensor(yk(k), psum[:, k, :], pr[:, R_DS:R_DS + D], ALU.mult).then_inc(yt_ready, 1)

            dve.wait_ge(x3_tr, NT)
            dve.wait_ge(x3l_ready, NT)
            dve.wait_ge(st_x3, 16 * NT)
            block_of_tokens(0, True)
            with dve.Fori(1, 4) as n:
                block_of_tokens(n, False)
            finish(3)

        @block.tensor
        def _(pe):
            mm = nc.tensor.matmul
            pe.wait_ge(ld_win, 16)
            for s in range(2):
                pe.wait_ge(ld_x[s], 32)
                for k in range(KC):
                    for b in range(B):
                        t0 = b * L + s * HALF
                        last = mm(ps_c[s][DH * b:DH * b + DH, :], win_sb[:, k, :], xt[:, k, t0:t0 + HALF], start=(k == 0), stop=(k == KC - 1))
                last.then_inc(inproj[s], 1)
            pe.wait_ge(ld_const, 48)

            def ln_center(n, s):
                pe.wait_ge(h_ready[s], n + 1)
                mm(ps_c[s], center, h[:, s, :], start=True, stop=True).then_inc(centered[s], 1)

            def ln_sums(n, s):
                pe.wait_ge(squared[s], n + 1)
                for t in range(4):
                    last = mm(ps_b[s][:, 2 * t:2 * t + 2], sq[s][:, P * t:P * t + P], blk_mean, start=True, stop=True)
                last.then_inc(var_sums[s], 1)

            def ln_spread(n, s):
                pe.wait_ge(rstd_ready[s], n + 1)
                for t in range(4):
                    for b in range(B):
                        last = mm(ps_b[s][DH * b:DH * b + DH, P * t:P * t + P], rstd8[s][:, 2 * t + b:2 * t + b + 1].to_broadcast([P, DH]), ident, start=True, stop=True)
                last.then_inc(spread[s], 1)

            with pe.Fori(0, NL) as i:
                for j in range(2):
                    for f in (ln_center, ln_sums, ln_spread):
                        for s in range(2):
                            f(2 * i + j, s)
                pe.wait_ge(ld_w, 64 * (i + 1))
                for c in range(FC + 2):
                    for s in range(2):
                        if c == 0:
                            pe.wait_ge(yn_ready[s], i + 1)
                        if c < FC:
                            if c >= 2:
                                pe.wait_ge(g_ready[s], FC * i + c - 1)
                            mm(ps_f[s][c % 2], w1bd[:, c, :], y[s][:, :], start=True, stop=True).then_inc(up_done[s], 1)
                        if c >= 2:
                            pe.wait_ge(g_ready[s], FC * i + c - 1)
                            last = mm(ps_c[s], w2bd[:, c - 2, :], g[s][:, c - 2, :], start=(c == 2), stop=(c == FC + 1))
                            if c == FC + 1:
                                last.then_inc(down_done[s], 1)

            for f in (ln_center, ln_sums, ln_spread):
                for s in range(2):
                    f(2 * NL, s)

            def out_proj(q):
                for t in range(4 * q, 4 * q + 4):
                    b, s = t // (NT // B), (t // 4) % 2
                    if t < 4:
                        pe.wait_ge(yn_ready[0], NL + 1)
                        pe.wait_ge(yn_ready[1], NL + 1)
                        pe.wait_ge(ld_wout, 32)
                    else:
                        pe.wait_ge(added, t - 3)
                    mm(psum[:, t % 4, :], y[s][:, P * (t % 4):P * (t % 4) + P], wout_sb[:, b, :], start=True, stop=True).then_inc(proj_done, 1)

            def transpose_x(n, t):
                pe.wait_ge(tile_ready, n + 1)
                if n >= 2:
                    pe.wait_ge(xt_ready, n - 1)
                if n == NT:
                    pe.wait_ge(ght_ready, 1)
                for k in range(KC):
                    last = nc.tensor.transpose(psum[:, 4 + n % 2, P * k:P * k + P], xres[:, t, P * k:P * k + P], ident)
                last.then_inc(tr_done, 1)

            def lora_gate(t):
                pe.wait_ge(xt_ready, t + 1)
                if t >= 2:
                    pe.wait_ge(lg_ready, t - 1)
                for k in range(KC):
                    last = mm(psum[:, 6 + t % 2, 0:P + NG], x1t[:, k, P * t:P * t + P], ag_sb[:, k, :], start=(k == 0), stop=(k == KC - 1))
                last.then_inc(lg_done, 1)

            def main_proj(q):
                for t in range(4 * q, 4 * q + 4):
                    pe.wait_ge(added, NT + t - 3)
                    for k in range(KC):
                        mm(psum[:, t % 4, :], x1t[:, k, P * t:P * t + P], main_sb[:, k, :], start=(k == 0), stop=False)

            out_proj(0)
            pe.wait_ge(ld_bw, 16 * 7)
            for q in range(4):
                if q < 3:
                    out_proj(q + 1)
                for t in range(4 * q, 4 * q + 4):
                    transpose_x(t, t)
                    if t >= 1:
                        lora_gate(t - 1)
            lora_gate(NT - 1)
            main_proj(0)
            pe.wait_ge(gh_ready, 1)
            for q in range(4):
                last = nc.tensor.transpose(psum[:, 4, P * q:P * q + P], gh[:, 4 * q:4 * q + 4, :].rearrange("p t n -> p (t n)"), ident)
            last.then_inc(ght_done, 1)
            pe.wait_ge(ght_ready, 1)
            for q in range(4):
                last = mm(psum[:, 5, 4 * NE * q:4 * NE * q + 4 * NE], ght[:, q, :], gw2_sb[:, :, :].rearrange("p t e -> p (t e)"), start=True, stop=True)
            last.then_inc(gates_done, 1)
            pe.wait_ge(oh_ready, 1)
            mm(psum[:, 4, 0:2 * P], ones, oh[:, :, :, :].rearrange("p k t e -> p (k t e)"), start=True, stop=True).then_inc(cnt_done, 1)
            for q in range(4):
                if q >= 1:
                    main_proj(q)
                pe.wait_ge(tmpw_ready, q + 1)
                if q == 0:
                    pe.wait_ge(lg_ready, NT)
                if q >= 2:
                    pe.wait_ge(tmpwt_ready, q - 1)
                for t in range(4):
                    last = nc.tensor.transpose(psum[:, 6 + q % 2, P * t:P * t + P], tmpw[:, 4 * q + t, :], ident)
                last.then_inc(wtr_done, 1)
                pe.wait_ge(tmpwt_ready, q + 1)
                for t in range(4 * q, 4 * q + 4):
                    mm(psum[:, t % 4, :], tmpwt[:, t, :], lorab_sb[:, :], start=False, stop=True).then_inc(bproj_done, 1)
                if q >= 1:
                    for t in range(4 * q - 4, 4 * q):
                        transpose_x(NT + t, t)
            for t in range(NT - 4, NT):
                transpose_x(NT + t, t)

            def maximum(i, c, m):
                qt, j, a = m // (2 * GH), m // 2 % GH, m % 2
                if m == 0:
                    pe.wait_ge(ld_stack[c % 3], ((i + c // 3) + 1) * 192)
                if m == 2:
                    at_least(pe, nmt_read, i, 3, c)
                at_least(pe, mx_read, i, 2 * 192, 2 * (64 * c + m - 2))
                mm(psum[:, max_bank(c, m), :], qst[c % 3][0:SR, j, P * qt:P * qt + P], kst[c % 3][0:SR, j, a * HALF:a * HALF + HALF], start=True, stop=True).then_inc(mx_done, 1)

            def turn_maxima(i, c):
                at_least(pe, nm_ready, i, 3, c + 1)
                nc.tensor.transpose(psum[0:GH * KT, turn_bank(c), 0:P], nm[:, :], ident).then_inc(nmt_done, 1)

            def first_maxima_of(kind, n, start=0, end=None):
                for what in first_maxima_after(kind, n)[start:end]:
                    if what == "turn":
                        turn_maxima(0, 0)
                    else:
                        maximum(0, *what)

            def project_unit(u):
                b, w, c = UNITS[u]
                if u >= 2:
                    pe.wait_ge(r1_ready, u - 1)
                if u == 3:
                    pe.wait_ge(v_ready, NT)
                for a in range(2):
                    first_maxima_of("u", u, 2 * a, 2 * a + 2)
                    for k in range(KC):
                        last = mm(psum[:, qk_banks(u), :][:, a, :], wqkv_sb[:, w * KC + k, P * c:P * c + P], x1t[:, k, b * L + a * HALF:b * L + a * HALF + HALF], start=(k == 0), stop=(k == KC - 1))
                last.then_inc(qk_done, 1)

            def project_v(t):
                if t == 1:
                    pe.wait_ge(r1_ready, 2)
                if t >= 2:
                    pe.wait_ge(v_ready, t - 1)
                for k in range(KC):
                    last = mm(psum[:, v_bank(t), :], x1t[:, k, P * t:P * t + P], wqkv_sb[:, 2 * KC + k, :], start=(k == 0), stop=(k == KC - 1))
                last.then_inc(v_done, 1)

            pe.wait_ge(ld_qkv, 16)
            pe.wait_ge(xt_ready, 2 * NT)
            pe.wait_ge(added, 2 * NT)
            for u in range(2):
                project_unit(u)
            for t in range(NT):
                project_v(t)
                first_maxima_of("v", t)
            for u in range(2, NU):
                if u == 13:
                    pe.wait_ge(abs_sum, 1)
                    mm(psum[:, 2, 0:3], ones, absum3[:, :], start=True, stop=True).then_inc(abs_all, 1)
                project_unit(u)
            pe.wait_ge(ones_ready, 3)
            pe.wait_ge(thr_ready, 1)

            def scores(i, c, e):
                n, a = e // 2, e % 2
                kt, j = n // GH, n % GH
                at_least(pe, exp_done, i, 192, 64 * c + e - 2)
                mm(psum[:, score_bank(c, e), :], kst[c % 3][0:SR + 2, j, P * kt:P * kt + P], qst[c % 3][0:SR + 2, j, a * HALF:a * HALF + HALF], start=True, stop=True).then_inc(score_done, 1)

            def gather(i, c, kt, a):
                at_least(pe, exp_done, i, 192, 64 * c + 2 * GH * kt + 2 * GH)
                if kt == 0 and a == 0:
                    at_least(pe, o_ready, i, 3, c)
                    pe.wait_ge(ld_v[c % 3], ((i + c // 3) + 1) * 16)
                for j in range(GH):
                    r = slice(2 * DK * j, 2 * DK * j + 2 * DK)
                    last = mm(psum[r, 4 + a, :], vg[c % 3][:, kt, r], probs[(GH * kt + j) % (2 * GH)][:, a * HALF:a * HALF + HALF], start=(kt == 0), stop=(kt == KT - 1))
                last.then_inc(pv_done, 1)

            def group(i, c):
                g = 3 * i + c if isinstance(i, int) else 1
                if g == 0:
                    pe.wait_ge(r1_ready, NU)
                pe.wait_ge(ld_nm[c % 3], ((i + c // 3) + 1) * 16)
                for h in range(2 * KT):
                    kt, a = h // 2, h % 2
                    ahead_by = 1 if h < KT else 2
                    for k in range(4):
                        if g + ahead_by < NGRP:
                            maximum(i, c + ahead_by, 4 * ((h + KT) % (2 * KT)) + k)
                        scores(i, c, 4 * h + k)
                        if h == KT and k == 0 and g + 1 < NGRP:
                            turn_maxima(i, c + 1)
                    if kt > 0:
                        gather(i, c, kt - 1, a)
                    elif g > 0:
                        gather(i, c - 1, KT - 1, a)

            over_groups(pe, group)
            for a in range(2):
                gather(0, NGRP - 1, KT - 1, a)

            def out_projection(q):
                if q == 0:
                    pe.wait_ge(ld_qkv, 32)
                    pe.wait_ge(o_ready, NGRP)
                for k in range(4):
                    pe.wait_ge(normed, 4 * q + k + 1)
                    if q > 0:
                        pe.wait_ge(x_added, 4 * q - 4 + k + 1)
                    for c in range(KC):
                        last = mm(psum[:, k, :], od[k][:, c, :], wo_sb[:, c, :], start=(c == 0), stop=(c == KC - 1))
                    last.then_inc(oproj_done, 1)

            out_projection(0)
            for q in range(4):
                if q < 3:
                    out_projection(q + 1)
                for k in range(4):
                    t = 4 * q + k
                    pe.wait_ge(x3_ready, t + 1)
                    if q > 0:
                        pe.wait_ge(x3l_ready, t - 3)
                    for c in range(KC):
                        last = nc.tensor.transpose(psum[:, 4 + k, P * c:P * c + P], x3t[4 * (q % 2) + k][:, P * c:P * c + P], ident)
                    last.then_inc(x3_tr, 1)
            def gate_up(n, f):
                wait_for(pe, hid_ready, n * HC + f - 1)
                cols = slice(P * (f % 8), P * (f % 8) + P)
                for w in range(2):
                    for k in range(KC):
                        for x in (x3h, x3l):
                            last = mm(psum[:, 4 + 2 * (f % 2) + w, :], tern_sb[:, 8 * w + 2 * k + f // 8, cols], x[:, k, bass.ds(n * HALF, HALF)],
                                      start=(k == 0 and x is x3h), stop=(k == KC - 1 and x is x3l))
                last.then_inc(gate_up_done, 1)

            def down(n, f):
                pe.wait_ge(hl_ready, n * HC + f + 1)
                if f == 0:
                    wait_for(pe, yt_ready, n * 4)
                cols = slice(D * (f % 2), D * (f % 2) + D)
                for k in range(4):
                    for x in (hh, hl):
                        last = mm(psum[:, k, :], x[f % 2][:, P * k:P * k + P], tern_sb[:, 16 + f // 2, cols], start=(f == 0 and x is hh), stop=(f == HC - 1 and x is hl))
                last.then_inc(ffn_done, 1)

            pe.wait_ge(x3l_ready, NT)
            pe.wait_ge(x_added, NT)
            gate_up(0, 0)
            gate_up(0, 1)

            def ffn_block(n, last):
                for f in range(HC):
                    down(n, f)
                    if f + 2 < HC:
                        gate_up(n, f + 2)
                    elif not last:
                        gate_up(n + 1, f + 2 - HC)

            ffn_block(0, False)
            with pe.Fori(1, 3) as n:
                ffn_block(n, False)
            ffn_block(3, True)


def kernel(**inputs):
    import numpy as np
    import concourse.bacc as bacc
    from concourse import mybir
    from concourse.bass_utils import run_bass_kernel_spmd

    a = {name: np.asarray(value) for name, value in inputs.items()}
    attn = lambda name: a["L0_attn_" + name]
    ffn = lambda name: a["L0_ffn_" + name]
    tf = lambda name: a["L1_ffn_" + name]
    x = attn("x").reshape(TOK, D)
    by_half = lambda w: w.T.reshape(KC, P, 2, L).transpose(0, 2, 1, 3).reshape(2 * KC, P, L)
    by_pair = lambda w: w.T.reshape(HC // 2, 2, P, D).transpose(0, 2, 1, 3).reshape(HC // 2, P, L)
    both = lambda v: np.concatenate([v, v], -1)
    consts = np.zeros((P, C_END), np.float32)
    consts[:, C_ID:C_ID + P] = np.eye(P)
    consts[:, C_CEN:C_CEN + P] = np.kron(np.eye(B), np.eye(DH) - 1 / DH)
    consts[:, C_ONE:C_ONE + P] = 1
    consts[:, C_BLK:C_BLK + B] = np.kron(np.eye(B), np.ones((DH, 1))) / DH
    consts[:, C_REV:] = NE - np.arange(NE)
    columns = [both(attn(n)).T for n in ("ln1_w", "ln1_b", "phz_re", "phz_im", "lc_re", "lc_im", "sc_lin", "ln2_w", "ln2_b", "b2")]
    columns += [np.broadcast_to(both(attn(n))[:, None], (P, 4)) for n in ("bin", "lnl_w", "lnl_b")]
    columns += [both(attn("b1").reshape(NL, FC, DH)).reshape(NL * FC, P).T]
    columns += [tf(n).reshape(HC, P).T for n in ("gate_scale", "up_scale")]
    row = np.concatenate([attn("bout"), tf("down_scale").ravel(), ffn("gb1"), ffn("ln_gamma"), ffn("ln_beta"), ffn("gb2")])
    arrays = {
        "x_tok": x,
        "x_feat": x.T,
        "win": attn("Win").T,
        "w1": attn("W1").transpose(0, 2, 1),
        "w2": attn("W2").transpose(0, 2, 1),
        "wout": attn("Wout").T,
        "main_w": ffn("weight").T,
        "ag_w": np.concatenate([ffn("lora_A").transpose(1, 0, 2).reshape(D, NE * ER), ffn("gw1").T], 1),
        "lora_b": ffn("lora_B").reshape(NE * ER, D),
        "gw2": ffn("gw2").T,
        "wqkv": np.stack([a["L1_attn_w_" + c].T for c in "qkv"]),
        "wo": a["L1_attn_w_o"].T,
        "tern": np.concatenate([by_half(tf("gate_w")), by_half(tf("up_w")), by_pair(tf("down_w"))]),
        "consts": consts,
        "pcol": np.concatenate(columns, 1),
        "prow": np.broadcast_to(row, (P, row.size)),
    }
    arrays = {name: np.ascontiguousarray(value) for name, value in arrays.items()}
    nc = bacc.Bacc("TRN2", target_bir_lowering=False, num_devices=1)
    args = [nc.dram_tensor(name, value.shape, mybir.dt.from_np(value.dtype), kind="ExternalInput").ap() for name, value in arrays.items()]
    out = nc.dram_tensor("out", [TOK, D], F32, kind="ExternalOutput").ap()
    build(nc, *args, out)
    result = run_bass_kernel_spmd(nc, [arrays], core_ids=[0])
    return result.results[0]["out"].reshape(B, L, D)
```

```python
import numpy as np
from contextlib import ExitStack

import concourse.bass as bass
from concourse import mybir
from concourse.alu_op_type import AluOpType as ALU

ACT = mybir.ActivationFunctionType
AX = mybir.AxisListType
F32 = mybir.dt.float32
F32R = mybir.dt.float32r
BF16 = mybir.dt.bfloat16

P = 128
B, L, D = 2, 1024, 512
TOK = B * L
KC = D // P
NT = TOK // P
HALF = L // 2
NL, DH, DFF = 4, 64, 256
FC = DFF // DH
NE, ER = 8, 16
NG = 4 * NE
CAPACITY = int(3.0 * TOK / NE)
NH, DK = 32, 16
GH = 4
NGRP = B * NH // GH
KT = L // P
HID = 2048
HC = HID // P
EPS = 1e-5
THRESH = 0.7

C_ID, C_CEN, C_ONE, C_BLK, C_REV = 0, P, 2 * P, 3 * P, 3 * P + 2
C_END = C_REV + NE
(Q_L1W, Q_L1B, Q_RE, Q_IM, Q_LR, Q_LI, Q_SCL, Q_L2W, Q_L2B, Q_B2, Q_BIN, Q_LNW, Q_LNB) = range(0, 52, 4)
Q_B1 = 52
Q_GS = Q_B1 + NL * FC
Q_US = Q_GS + HC
Q_END = Q_US + HC
R_BOUT, R_DS = 0, D
R_GB1 = 2 * D
R_GAM, R_BET, R_GB2 = R_GB1 + NG, R_GB1 + 2 * NG, R_GB1 + 3 * NG
R_END = R_GB2 + NE


class Chain:

    def __init__(self, engine, sem):
        self.engine, self.sem, self.base, self.n = engine, sem, 0, 0

    def step(self, instruction):
        instruction.then_inc(self.sem, 1)
        self.n += 1
        self.engine.wait_ge(self.sem, self.base + self.n)


def build(nc, x_tok, x_feat, win, w1, w2, wout, main_w, ag_w, lora_b, gw2, wqkv, wo, tern, consts, pcol, prow, out):
    ctx = ExitStack()
    with ctx:
        sem = lambda name: ctx.enter_context(nc.semaphore(name))
        sems = lambda name, n=2: [sem(f"{name}{i}") for i in range(n)]

        def sb(stack, name, shape, dt=F32):
            return stack.enter_context(nc.sbuf_tensor(name, shape, dt))

        psum = ctx.enter_context(nc.psum_tensor("psum", [P, 8, 512], F32))

        cst = sb(ctx, "cst", [P, C_END])
        pc = sb(ctx, "pc", [P, Q_END])
        pr = sb(ctx, "pr", [P, R_END])
        mhalf = sb(ctx, "mhalf", [P, NT])
        ident = cst[:, C_ID:C_ID + P]
        center = cst[:, C_CEN:C_CEN + P]
        ones = cst[:, C_ONE:C_ONE + P]
        blk_mean = cst[:, C_BLK:C_BLK + 2]
        rev = cst[:, C_REV:C_REV + NE]
        stats = sb(ctx, "stats", [P, 4, 6])
        mv = sb(ctx, "mv", [P, NT, 2])
        varr = sb(ctx, "varr", [P, NT])
        rstd = sb(ctx, "rstd", [P, NT])
        thr = sb(ctx, "thr", [P, 3])
        nthr = sb(ctx, "nthr", [P, 3])

        xts = ExitStack()
        x2l = sb(xts, "x2l", [P, KC, TOK], F32R)
        xts.close()
        xts = ExitStack()
        x1t = sb(xts, "x1t", [P, KC, TOK])
        xt = x1t

        ab = ExitStack()
        y = [sb(ab, f"y{s}", [P, HALF]) for s in range(2)]
        wout_sb = sb(ab, "wout_sb", [P, B, D])
        main_sb = sb(ab, "main_sb", [P, KC, D])
        ag_sb = sb(ab, "ag_sb", [P, KC, P + NG])
        lorab_sb = sb(ab, "lorab_sb", [P, D])
        gw2_sb = sb(ab, "gw2_sb", [P, 4, NE])
        xres = sb(ab, "xres", [P, NT, D])
        sa = ExitStack()
        win_sb = sb(sa, "win_sb", [P, KC, DH])
        cos = sb(sa, "cos", [P, NL, L])
        sin = sb(sa, "sin", [P, NL, L])
        tab1 = sb(sa, "tab1", [P, NL, HALF])
        tab2 = sb(sa, "tab2", [P, NL, HALF])
        pw = sb(sa, "pw", [P, 16, NL])
        unit = sb(sa, "unit", [P, 2, 10, NL])
        cscl = sb(sa, "cscl", [P, P])
        w1bd = sb(sa, "w1bd", [P, FC, P])
        w2bd = sb(sa, "w2bd", [P, FC, P])
        h = sb(sa, "h", [P, 2, HALF])
        half = lambda name, n=HALF: [sb(sa, f"{name}{s}", [P, n]) for s in range(2)]
        hc, sq, z = half("hc"), half("sq"), half("z")
        re_in, im_in, zr, zi, re_p, im_p = (half(n) for n in ("re_in", "im_in", "zr", "zi", "re_p", "im_p"))
        g = [sb(sa, f"g{s}", [P, FC, HALF]) for s in range(2)]
        var8, rstd8 = half("var8", 8), half("rstd8", 8)
        sa.close()
        sbk = ExitStack()
        lg = sb(sbk, "lg", [P, NT, P + NG])
        gh = sb(sbk, "gh", [P, NT, NG])
        gsq = sb(sbk, "gsq", [P, NT, NG])
        ght = sb(sbk, "ght", [P, 4, P])
        gs = sb(sbk, "gs", [P, 10, NT])
        ge = sb(sbk, "ge", [P, 6, NT, NE])
        oh = sb(sbk, "oh", [P, 2, NT, NE])
        cnt = sb(sbk, "cnt", [P, 2, NE])
        wexp = sb(sbk, "wexp", [P, NT, NE])
        tmpw = sb(sbk, "tmpw", [P, NT, P])
        tmpwt = sb(sbk, "tmpwt", [P, NT, P])
        sbk.close()
        ab.close()
        sq_ = ExitStack()
        parts = [sb(sq_, f"parts{i}", [P, 3, L], BF16) for i in range(2)]
        resid = [sb(sq_, f"resid{i}", [P, L]) for i in range(2)]
        vpad = [sb(sq_, f"vpad{i}", [P, NH, 2 * DK]) for i in range(2)]
        wabs = sb(sq_, "wabs", [P, 2, L])
        absum = sb(sq_, "absum", [P, 3 * 8])
        absum3 = sb(sq_, "absum3", [P, 3])
        x2h = [None, sb(sq_, "x2h1", [P, KC, L], F32R)]
        wh = [sb(sq_, f"wh{i}", [P, KC, P], F32R) for i in range(2)]
        wl = [sb(sq_, f"wl{i}", [P, KC, P], F32R) for i in range(2)]
        sq_.close()
        xts.close()
        cd = ExitStack()
        tern_sb = sb(cd, "tern_sb", [P, 24, L], F32R)
        at = ExitStack()
        qst, kst = ([None] * 3 for _ in range(2))
        for i in (1, 2, 0):
            if i == 2:
                early = ExitStack()
                x2h[0] = sb(early, "x2h0", [P, KC, L], F32R)
                early.close()
            qst[i], kst[i] = sb(at, f"qst{i}", [P, GH, L], BF16), sb(at, f"kst{i}", [P, GH, L], BF16)
        vg = [sb(at, f"vg{i}", [P, KT, GH * 2 * DK]) for i in range(3)]
        o_sb = sb(at, "o_sb", [P, L])
        wraw = sb(at, "wraw", [P, L])
        mx = [sb(at, f"mx{i}", [P, GH, KT, 2]) for i in range(2)]
        nm = sb(at, "nm", [P, GH * KT])
        nmh = sb(at, "nmh", [GH * KT, P], BF16)
        nml = sb(at, "nml", [GH * KT, P], BF16)
        pst = ExitStack()
        probs = [sb(pst, f"probs{i}", [P, L]) for i in range(2 * GH)]
        pst.close()
        pst = ExitStack()
        wqkv_sb = sb(pst, "wqkv_sb", [P, 3 * KC, D])
        pst.close()
        at.close()
        op = ExitStack()
        wo_sb = sb(op, "wo_sb", [P, KC, D])
        rb_sb = sb(op, "rb", [P, KC, HALF])
        od = [sb(op, f"od{k}", [P, KC, P]) for k in range(4)]
        x3t = [sb(op, f"x3t{k}", [P, D]) for k in range(8)]
        den_sb = [x3t[3][0:2 * NH, :], x3t[7][0:2 * NH, :]]
        x3h = sb(op, "x3h", [P, KC, TOK], F32R)
        x3l = sb(op, "x3l", [P, KC, TOK], F32R)
        rb = [rb_sb, rb_sb, x3l[:, :, 3 * HALF:4 * HALF].bitcast(F32), rb_sb]
        op.close()
        ff = ExitStack()
        hh = [sb(ff, f"hh{k}", [P, HALF], F32R) for k in range(2)]
        hl = [sb(ff, f"hl{k}", [P, HALF], F32R) for k in range(2)]
        sg = [sb(ff, f"sg{k}", [P, HALF]) for k in range(2)]
        hid = [sb(ff, f"hid{k}", [P, HALF]) for k in range(2)]
        yt = sb(ff, "yt", [P, 4, D])
        xin = sb(ff, "xin", [P, 4, D])
        ff.close()
        cd.close()

        ps_c = [psum[:, s, :] for s in range(2)]
        ps_b = [psum[:, 2 + s, :] for s in range(2)]
        ps_f = [[psum[:, 4 + 2 * s + k, :] for k in range(2)] for s in range(2)]

        ld_const, ld_x, ld_win = sem("ld_const"), sems("ld_x"), sem("ld_win")
        ld_xres = sem("ld_xres")
        zeroed, ld_w = sem("zeroed"), sem("ld_w")
        dve_chain = sem("dve_chain")
        pow_in_ready, pow_ready, func_in_ready, func_ready = sem("pow_in_ready"), sem("pow_ready"), sem("func_in_ready"), sem("func_ready")
        unit_ready, power_chain = sem("unit_ready"), sem("power_chain")
        inproj = sems("inproj")
        h_ready, centered, squared, hc_copied = sems("h_ready"), sems("centered"), sems("squared"), sems("hc_copied")
        var_sums, var_ready, rstd_ready = sems("var_sums"), sems("var_ready"), sems("rstd_ready")
        spread, z_ready, y_ready, yn_ready = sems("spread"), sems("z_ready"), sems("y_ready"), sems("yn_ready")
        re_p_ready, cscl_ready = sems("re_p_ready"), sem("cscl_ready")
        im_in_ready, zi_ready, im_p_ready = sems("im_in_ready"), sems("zi_ready"), sems("im_p_ready")
        up_done, g_ready, down_done = sems("up_done"), sems("g_ready"), sems("down_done")
        ld_bw = sem("ld_bw")
        xres_biased = sem("xres_biased")
        proj_done, var4_ready, rstd4_ready, tile_ready = sem("proj_done"), sem("var4_ready"), sem("rstd4_ready"), sem("tile_ready")
        tr_done, xt_ready, lg_done, lg_ready = sem("tr_done"), sem("xt_ready"), sem("lg_done"), sem("lg_ready")
        gh_ready, ght_done, ght_ready = (sem(n) for n in ("gh_ready", "ght_done", "ght_ready"))
        gates_done, oh_ready, cnt_done = (sem(n) for n in ("gates_done", "oh_ready", "cnt_done"))
        tmpw_ready, wtr_done, tmpwt_ready = sem("tmpw_ready"), sem("wtr_done"), sem("tmpwt_ready")
        bproj_done, added = sem("bproj_done"), sem("added")
        st_x2 = sem("st_x2")
        ld_qkv, hi_ready, r1_ready, mid_ready, lo_ready, qk_done = (sem(n) for n in ("ld_qkv", "hi_ready", "r1_ready", "mid_ready", "lo_ready", "qk_done"))
        xh_ready, xl_ready, wh_ready, wl_ready = (sem(n) for n in ("xh_ready", "xl_ready", "wh_ready", "wl_ready"))
        v_done, v_ready, vpad_ready = (sem(n) for n in ("v_done", "v_ready", "vpad_ready"))
        st_parts, st_v, ld_abs = sems("st_parts"), sems("st_v"), sems("ld_abs")
        abs_done, abs_sum, abs_all, thr_ready = (sem(n) for n in ("abs_done", "abs_sum", "abs_all", "thr_ready"))
        ld_stack, ld_v, ld_nm = sems("ld_stack", 3), sems("ld_v", 3), sems("ld_nm", 3)
        ones_ready, mx_done, mx_read, nm_ready, nmt_done, nmt_read = (sem(n) for n in ("ones_ready", "mx_done", "mx_read", "nm_ready", "nmt_done", "nmt_read"))
        nmh_ready = sem("nmh_ready")
        score_done, exp_done, pv_done, o_ready, st_o = (sem(n) for n in ("score_done", "exp_done", "pv_done", "o_ready", "st_o"))
        st_nm = sem("st_nm")
        ld_tern = sem("ld_tern")
        tern_chain = sem("tern_chain")
        qk_dram = nc.dram_tensor("qk_dram", [2, 3, B * D, L], BF16).ap()
        v_dram = nc.dram_tensor("v_dram", [NGRP, L, GH * 2 * DK], F32).ap()
        nm_dram = nc.dram_tensor("nm_dram", [2, GH * KT, P], BF16).ap()
        o_dram = nc.dram_tensor("o_dram", [B * D, L], F32).ap()
        den_dram = nc.dram_tensor("den_dram", [B * NH, L], F32).ap()
        x2_dram = nc.dram_tensor("x2_dram", [TOK, D], F32).ap()
        rec_dram = nc.dram_tensor("rec_dram", [B * NH, L], F32).ap()
        x3_dram = nc.dram_tensor("x3_dram", [TOK, D], F32).ap()
        ld_den, den_ready, st_rec = (sem(n) for n in ("ld_den", "den_ready", "st_rec"))
        ld_rb, normed, oproj_done = sem("ld_rb"), sem("normed"), sem("oproj_done")
        ld_od, ld_x2t, st_x3 = sems("ld_od", 4), sems("ld_x2t", 3), sem("st_x3")
        x_added, x_stats, x_mv, x_var, x_rstd, x3_ready = (sem(n) for n in ("x_added", "x_stats", "x_mv", "x_var", "x_rstd", "x3_ready"))
        x3_tr, x3h_ready, x3l_ready = sem("x3_tr"), sem("x3h_ready"), sem("x3l_ready")
        gate_up_done, silu_ready, hid_ready, hh_ready, hl_ready = (sem(n) for n in ("gate_up_done", "silu_ready", "hid_ready", "hh_ready", "hl_ready"))
        ffn_done, yt_ready, ld_xin, st_out = sem("ffn_done"), sem("yt_ready"), sem("ld_xin"), sem("st_out")
        f_added, out_ready = sem("f_added"), sem("out_ready")

        Q_PART, K_PART = (0, 0, 1, 0, 2, 1), (0, 1, 0, 2, 0, 1)
        SR = 6 * DK

        UNITS = [(b, w, c) for b in range(B) for c in range(KC) for w in range(2)]
        NU = len(UNITS)
        first_maxima = [(0, m) for m in range(64)] + ["reduce", (1, 0), (1, 1), "turn"] + [(1, m) for m in range(2, 32)]

        def first_maxima_after(kind, n):
            if kind == "v":
                at, count = 4 * (n - 5), 4
            else:
                at, count = 4 * (NT - 5) + 4 * (n - 2), 4
            return first_maxima[at:at + count] if n >= (5 if kind == "v" else 2) else []

        score_bank = lambda c, e: (c + e) % 3
        max_bank = lambda c, m: (3, 6, 7)[(c + m) % 3]
        turn_bank = lambda c: max_bank(c + 1, 2)
        qk_banks = lambda u: slice(0, 2) if u % 2 == 0 else slice(4, 6)
        v_bank = lambda t: (2, 5)[t % 2]
        x3_bank = lambda t: t % 4 if t >= NT - 4 else 4 + t % 4

        def over_groups(engine, body):
            body(0, 0)
            with engine.Fori(0, (NGRP - 4) // 3) as i:
                for c in range(1, 4):
                    body(i, c)
            for g in range(NGRP - 3, NGRP):
                body(0, g)

        def at_least(engine, semaphore, i, per, c):
            wait_for(engine, semaphore, i * per + c)

        def wait_for(engine, semaphore, count):
            if not isinstance(count, int) or count > 0:
                engine.wait_ge(semaphore, count)

        def ahead(engine):
            engine.wait_ge(ld_const, 48)

        block = ctx.enter_context(nc.Block())

        @block.sync
        def _(sp):
            sp.dma_start(pc[:, :], pcol).then_inc(ld_const, 16)
            sp.dma_start(cst[:, :], consts).then_inc(ld_const, 16)
            sp.dma_start(pr[:, :], prow).then_inc(ld_const, 16)
            sp.dma_start(win_sb[:, :, :], win.rearrange("(k p) d -> p k d", p=P)).then_inc(ld_win, 16)
            xf = x_feat.rearrange("(k p) t -> p k t", p=P)
            for s in range(2):
                for b in range(B):
                    t0 = b * L + s * HALF
                    sp.dma_start(xt[:, :, t0:t0 + HALF], xf[:, :, t0:t0 + HALF]).then_inc(ld_x[s], 16)

            def load_layer(i):
                for b in range(B):
                    r = slice(DH * b, DH * b + DH)
                    sp.dma_start(w1bd[r, :, r], w1[i].rearrange("d (c f) -> d c f", c=FC)).then_inc(ld_w, 16)
                    sp.dma_start(w2bd[r, :, r], w2[i].rearrange("(c f) d -> f c d", c=FC)).then_inc(ld_w, 16)

            sp.wait_ge(zeroed, 4)
            load_layer(0)
            for b in range(B):
                sp.dma_start(wout_sb[DH * b:DH * b + DH, b, :], wout).then_inc(ld_bw, 16)
            sp.dma_start(xres[:, :, :], x_tok.rearrange("(t p) d -> p t d", p=P)).then_inc(ld_xres, 16)
            sp.dma_start(main_sb[:, :, :], main_w.rearrange("(k p) n -> p k n", p=P)).then_inc(ld_bw, 16)
            sp.dma_start(ag_sb[:, :, :], ag_w.rearrange("(k p) n -> p k n", p=P)).then_inc(ld_bw, 16)
            sp.dma_start(lorab_sb[:, :], lora_b).then_inc(ld_bw, 16)
            for t in range(4):
                sp.dma_start(gw2_sb[NG * t:NG * t + NG, t, :], gw2).then_inc(ld_bw, 16)
            with sp.Fori(1, NL) as i:
                for s in range(2):
                    sp.wait_ge(down_done[s], i)
                for b in range(B):
                    r = slice(DH * b, DH * b + DH)
                    sp.dma_start(w1bd[r, :, r], w1[bass.ds(i, 1)].rearrange("o d (c f) -> (o d) c f", c=FC)).then_inc(ld_w, 16)
                    sp.dma_start(w2bd[r, :, r], w2[bass.ds(i, 1)].rearrange("o (c f) d -> (o f) c d", c=FC)).then_inc(ld_w, 16)
            for s in range(2):
                sp.wait_ge(yn_ready[s], NL + 1)
            sp.dma_start(wqkv_sb[:, :, :], wqkv.rearrange("w (k p) n -> p (w k) n", p=P)).then_inc(ld_qkv, 16)
            for q in range(4):
                sp.wait_ge(tile_ready, NT + 4 * q + 4)
                sp.dma_start(x2_dram.rearrange("(t p) d -> p t d", p=P)[:, 4 * q:4 * q + 4, :], xres[:, 4 * q:4 * q + 4, :]).then_inc(st_x2, 16)
            def load_stack(i, c, which=(0, 1)):
                rows = lambda w, n: qk_dram[w, n].rearrange("(g j d) t -> g d j t", j=GH, d=DK)[i * 3 + c] if isinstance(i, int) else \
                    qk_dram[w, n].rearrange("(g j d) t -> g d j t", j=GH, d=DK)[bass.ds(i * 3 + c, 1)].rearrange("o d j t -> (o d) j t")
                for st, w, order in [((qst, 0, Q_PART), (kst, 1, K_PART))[k] for k in which]:
                    for m, n in enumerate(order):
                        sp.dma_start(st[c % 3][DK * m:DK * m + DK, :, :], rows(w, n)).then_inc(ld_stack[c % 3], 16)

            def load_v(i, c):
                src = v_dram[bass.ds(i * 3 + c, 1)].rearrange("o (k p) n -> p (o k) n", p=P)
                sp.dma_start(vg[c % 3][:, :, :], src).then_inc(ld_v[c % 3], 16)

            def load_nm(i, c):
                at_least(sp, nmt_read, i, 3, c + 1)
                for r, src in ((0, nmh), (1, nml)):
                    sp.dma_start(nm_dram[r], src[:, :]).then_inc(st_nm, 16)
                at_least(sp, st_nm, i, 3 * 32, 32 * (c + 1))
                sp.dma_start(qst[c % 3][SR:SR + 2, :, :].rearrange("r j t -> r (j t)"), nm_dram.rearrange("r p t -> r (p t)")).then_inc(ld_nm[c % 3], 16)

            def store_parts(u):
                b, w, c = UNITS[u]
                sp.wait_ge(lo_ready, u + 1)
                r0 = b * D + P * c
                sp.dma_start(qk_dram[w, :, r0:r0 + P, :].rearrange("n p t -> p n t"), parts[u % 2][:, :, :]).then_inc(st_parts[u % 2], 16)

            def store_v(t):
                sp.wait_ge(v_ready, t + 1)
                b, t0 = t // KT, t % KT * P
                dst = v_dram[b * NGRP // B:(b + 1) * NGRP // B, t0:t0 + P, :].rearrange("g p n -> p g n")
                sp.dma_start(dst, vpad[t % 2][:, :, :].rearrange("p (g j) e -> p g (j e)", j=GH)).then_inc(st_v[t % 2], 16)

            for u in range(2):
                store_parts(u)
            for k in range(2):
                sp.wait_ge(st_parts[k], 16)
            for t in range(NT):
                store_v(t)
                if t in (0, 2):
                    load_stack(0, 0, (t // 2,))
            for k in range(2):
                sp.wait_ge(st_v[k], 128)
            load_stack(0, 1)
            for u in range(2, NU):
                store_parts(u)
                if u == 4:
                    for c in range(2):
                        load_v(0, c)
                if u == 10:
                    load_nm(0, 0)
            for k in range(2):
                sp.wait_ge(st_parts[k], 128)

            def store_o(i, c):
                at_least(sp, o_ready, i, 3, c + 1)
                for j in range(GH):
                    r0 = (i * 3 + c) * (GH * DK) + DK * j
                    sp.dma_start(o_dram[bass.ds(r0, DK), :], o_sb[2 * DK * j:2 * DK * j + DK, :]).then_inc(st_o, 16)
                    sp.dma_start(den_dram[bass.ds((i * 3 + c) * GH + j, 1), :], o_sb[2 * DK * j + DK:2 * DK * j + DK + 1, :]).then_inc(st_o, 16)

            def load_rb(q):
                b, a = q // 2, q % 2
                wait_for(sp, normed, (0, 4, 5, 9)[q])
                for k in range(KC):
                    h0, n = b * NH + k * (NH // KC), NH // KC
                    sp.dma_start(rb[q][:, k, :], rec_dram[h0:h0 + n, a * HALF:a * HALF + HALF].unsqueeze(1).to_broadcast([n, DK, HALF])).then_inc(ld_rb, 16)

            def load_od(q, tiles=range(4)):
                b, a = q // 2, q % 2
                for k in tiles:
                    if q > 0:
                        sp.wait_ge(oproj_done, 4 * q - 4 + k + 1)
                    t0 = a * HALF + k * P
                    sp.dma_start(od[k][:, :, :], o_dram[b * D:b * D + D, t0:t0 + P].rearrange("(k p) t -> p k t", p=P)).then_inc(ld_od[k], 16)

            def load_x2(q, tiles=range(4)):
                if q >= 2:
                    sp.wait_ge(st_x3, 64 * (q - 1))
                for k in tiles:
                    t, slot = 4 * q + k, 4 * (q % 2) + k
                    if q >= 2:
                        sp.wait_ge(x3_tr, t - 8 + 1)
                    sp.dma_start(x3t[slot][:, :], x2_dram[P * t:P * t + P, :]).then_inc(ld_x2t[2 if t == 7 else q % 2], 16)

            den_rows = lambda x, b: x[b * NH:b * NH + NH, :].rearrange("n (a t) -> (n a) t", a=2)

            def load_denominators(b):
                sp.dma_start(den_sb[b], den_rows(den_dram, b)).then_inc(ld_den, 16)

            def store_reciprocals(b):
                sp.wait_ge(den_ready, b + 1)
                sp.dma_start(den_rows(rec_dram, b), den_sb[b]).then_inc(st_rec, 16)
                sp.wait_ge(st_rec, 16 * b + 16)

            def store_x3(q):
                for k in range(4):
                    t, slot = 4 * q + k, 4 * (q % 2) + k
                    sp.wait_ge(x3_ready, t + 1)
                    sp.dma_start(x3_dram[P * t:P * t + P, :], x3t[slot][:, :]).then_inc(st_x3, 16)

            def group(i, c):
                last = isinstance(i, int) and 3 * i + c + 2 >= NGRP
                if not last:
                    at_least(sp, score_done, i, 192, 64 * c)
                    load_stack(i, c + 2)
                if isinstance(i, int) and 3 * i + c == NGRP - 1:
                    sp.wait_ge(st_o, 128 * (NGRP - 2))
                if not (isinstance(i, int) and 3 * i + c == 0):
                    store_o(i, c - 1)
                if not last:
                    at_least(sp, pv_done, i, 48, 16 * c)
                    load_v(i, c + 2)
                if not (isinstance(i, int) and 3 * i + c + 1 >= NGRP):
                    load_nm(i, c + 1)

            over_groups(sp, group)
            sp.wait_ge(score_done, 64 * (NGRP - 1))
            sp.wait_ge(mx_done, 64 * NGRP)
            load_denominators(0)
            store_reciprocals(0)
            sp.dma_start(wo_sb[:, :, :], wo.rearrange("(k p) n -> p k n", p=P)).then_inc(ld_qkv, 16)
            load_rb(0)
            load_od(0)
            load_x2(0)
            load_rb(1)
            load_od(1, (0,))
            sp.wait_ge(st_o, 128 * NGRP)
            sp.wait_ge(score_done, 64 * NGRP)
            sp.wait_ge(exp_done, 64 * NGRP)
            sp.wait_ge(pv_done, 2 * KT * NGRP)
            load_denominators(1)
            load_od(1, range(1, 4))
            load_x2(1, range(3))
            store_reciprocals(1)
            load_x2(1, (3,))
            for q in range(4):
                if q < 2:
                    load_rb(q + 2)
                    load_od(q + 2)
                store_x3(q)
                if q < 2:
                    load_x2(q + 2)
            sp.wait_ge(st_x3, 16 * NT)
            sp.wait_ge(x3_tr, NT)

            def write_out(n):
                wait_for(sp, f_added, n * 4)
                sp.dma_start(xin[:, :, :], x3_dram.rearrange("(n k p) d -> p n k d", p=P, k=4)[:, bass.ds(n, 1)].rearrange("p o k d -> p (o k) d")).then_inc(ld_xin, 16)
                for k in range(4):
                    sp.wait_ge(out_ready, n * 4 + k + 1)
                    sp.dma_start(out[bass.ds(n * HALF + k * P, P), :], yt[:, k, :]).then_inc(st_out, 16)

            write_out(0)
            with sp.Fori(1, 4) as n:
                write_out(n)
            sp.wait_ge(st_out, 16 * NT)

        @block.gpsimd
        def _(pool):
            nc.gpsimd.memset(mhalf[:, :], -0.5).then_inc(power_chain, 1)
            pool.wait_ge(power_chain, 1)
            pool.wait_ge(pow_in_ready, 1)
            nc.gpsimd.tensor_tensor(pw[:, 3, :], pw[:, 2, :], mhalf[:, 0:NL], ALU.pow).then_inc(pow_ready, 1)

            pool.wait_ge(unit_ready, 1)
            ch = Chain(pool, power_chain)
            ch.base = 1
            tt = lambda o, a, b_, op: ch.step(nc.gpsimd.tensor_tensor(o, a, b_, op))
            ts = lambda o, a, s1, s2, o0, o1: ch.step(nc.gpsimd.tensor_scalar(o, a, s1, s2, o0, o1))
            t0, t1, t2 = (pw[:, k, :] for k in (14, 15, 3))
            for k in range(1, 10):
                c0, s0, c1, s1 = unit[:, 0, k - 1, :], unit[:, 1, k - 1, :], unit[:, 0, k, :], unit[:, 1, k, :]
                tt(t0, c0, c0, ALU.mult)
                tt(t1, s0, s0, ALU.mult)
                tt(t2, c0, s0, ALU.mult)
                tt(c1, t0, t1, ALU.subtract)
                tt(s1, t2, t2, ALU.add)
                if k % 3 == 0:
                    tt(t0, c1, c1, ALU.mult)
                    tt(t1, s1, s1, ALU.mult)
                    tt(t0, t0, t1, ALU.add)
                    ts(t0, t0, -0.5, 1.5, ALU.mult, ALU.add)
                    tt(c1, c1, t0, ALU.mult)
                    tt(s1, s1, t0, ALU.mult)

            def ln_rstd(n, s):
                pool.wait_ge(var_ready[s], n + 1)
                nc.gpsimd.tensor_tensor(rstd8[s][:, :], var8[s][:, :], mhalf[:, 0:8], ALU.pow).then_inc(rstd_ready[s], 1)

            pool.wait_ge(ld_const, 48)
            pool.wait_ge(ld_xres, 16)
            with pool.Fori(0, NL) as i:
                for s in range(2):
                    ln_rstd(i * 2, s)
                for s in range(2):
                    sl = slice(s * HALF, s * HALF + HALF)
                    ahead(pool)
                    pool.wait_ge(y_ready[s], i + 1)
                    nc.gpsimd.tensor_tensor(im_in[s][:, :], sin[:, bass.ds(i, 1), sl].rearrange("p o t -> p (o t)"), y[s][:, :], ALU.mult).then_inc(im_in_ready[s], 1)
                for s in range(2):
                    sl = slice(s * HALF, s * HALF + HALF)
                    ahead(pool)
                    pool.wait_ge(zi_ready[s], i + 1)
                    nc.gpsimd.tensor_tensor(im_p[s][:, :], sin[:, bass.ds(i, 1), sl].rearrange("p o t -> p (o t)"), zi[s][:, :], ALU.mult).then_inc(im_p_ready[s], 1)
                for s in range(2):
                    ln_rstd(i * 2 + 1, s)
                quarter = xres[:, bass.ds(i * (NT // NL), NT // NL), :]
                nc.gpsimd.tensor_tensor(quarter, quarter, pr[:, R_BOUT:R_BOUT + D].unsqueeze(1).to_broadcast([P, NT // NL, D]), ALU.add).then_inc(xres_biased, 1)
            for s in range(2):
                ln_rstd(2 * NL, s)

            def rstd_tiles(r):
                for q in range(4):
                    sl = slice(4 * q, 4 * q + 4)
                    pool.wait_ge(var4_ready, 4 * r + q + 1)
                    nc.gpsimd.tensor_tensor(rstd[:, sl], varr[:, sl], mhalf[:, sl], ALU.pow).then_inc(rstd4_ready, 1)

            rstd_tiles(0)
            pool.wait_ge(pow_in_ready, 2)
            nc.gpsimd.tensor_tensor(gs[:, 2, :], gs[:, 1, :], mhalf[:, :], ALU.pow).then_inc(pow_ready, 1)
            rstd_tiles(1)

            for c in range(24):
                if c >= 2:
                    pool.wait_ge(abs_done, c - 1)
                elif c == 0:
                    pool.wait_ge(tile_ready, 2 * NT)
                    pool.wait_ge(tmpwt_ready, 4)
                    pool.wait_ge(tr_done, 2 * NT)
                    pool.wait_ge(st_x2, 64)
                pool.dma_start(wabs[:, c % 2, :], tern[c]).then_inc(ld_abs[c % 2], 16)
                if c == 1:
                    for k in range(2):
                        nc.gpsimd.memset(kst[k][SR:SR + 2, :, :], 1.0).then_inc(ones_ready, 1)
                        pool.wait_ge(ones_ready, k + 1)
            pool.wait_ge(qk_done, 2 * KC)
            nc.gpsimd.memset(kst[2][SR:SR + 2, :, :], 1.0).then_inc(ones_ready, 1)
            pool.wait_ge(ones_ready, 3)
            pool.wait_ge(thr_ready, 1)
            pool.wait_ge(qk_done, NU)
            for k in range(2):
                pool.wait_ge(st_parts[k], 128)
            pch = Chain(pool, tern_chain)
            for c in range(24):
                w = c // 8
                pool.dma_start(wraw[:, :], tern[c]).then_inc(ld_tern, 16)
                pool.wait_ge(ld_tern, 16 * c + 16)
                pch.step(nc.gpsimd.tensor_scalar(tern_sb[:, c, :], wraw[:, :], thr[:, w:w + 1], None, ALU.is_gt))
                pch.step(nc.gpsimd.tensor_scalar(wraw[:, :], wraw[:, :], nthr[:, w:w + 1], None, ALU.is_lt))
                pch.step(nc.gpsimd.tensor_tensor(tern_sb[:, c, :], tern_sb[:, c, :].bitcast(F32), wraw[:, :], ALU.subtract))
            for r, applied in ((0, x3_ready), (4, out_ready)):
                for q in range(4):
                    pool.wait_ge(x_var, q + r + 1)
                    wait_for(pool, applied, q * 4)
                    nc.gpsimd.tensor_tensor(rstd[:, 0:4], varr[:, 0:4], mhalf[:, 0:4], ALU.pow).then_inc(x_rstd, 1)

        @block.scalar
        def _(act):
            act.wait_ge(ld_const, 48)
            act.wait_ge(func_in_ready, 1)
            nc.scalar.activation(pw[:, 5, :], pw[:, 4, :], ACT.Tanh).then_inc(func_ready, 1)
            for s in range(2):
                act.wait_ge(inproj[s], 1)
                nc.scalar.activation(h[:, s, :], ps_c[s], ACT.Identity, bias=pc[:, Q_BIN:Q_BIN + 1]).then_inc(h_ready[s], 1)

            def ln_square(n, s):
                act.wait_ge(centered[s], n + 1)
                nc.scalar.activation(sq[s][:, :], ps_c[s], ACT.Square).then_inc(squared[s], 1)
                nc.scalar.activation(hc[s][:, :], ps_c[s], ACT.Copy).then_inc(hc_copied[s], 1)

            col = lambda base, i: pc[:, bass.ds(base + i, 1)]
            with act.Fori(0, NL) as i:
                for s in range(2):
                    ln_square(2 * i, s)
                for s in range(2):
                    ahead(act)
                    act.wait_ge(z_ready[s], 2 * i + 1)
                    nc.scalar.activation(y[s][:, :], z[s][:, :], ACT.Silu, bias=col(Q_L1B, i), scale=col(Q_L1W, i)).then_inc(y_ready[s], 1)
                for s in range(2):
                    ln_square(2 * i + 1, s)
                for s in range(2):
                    ahead(act)
                    act.wait_ge(z_ready[s], 2 * i + 2)
                    nc.scalar.activation(y[s][:, :], z[s][:, :], ACT.Identity, bias=col(Q_L2B, i), scale=col(Q_L2W, i)).then_inc(yn_ready[s], 1)
                for c in range(FC):
                    for s in range(2):
                        ahead(act)
                        act.wait_ge(up_done[s], FC * i + c + 1)
                        nc.scalar.activation(g[s][:, c, :], ps_f[s][c % 2], ACT.Silu, bias=pc[:, bass.ds(Q_B1 + i * FC + c, 1)]).then_inc(g_ready[s], 1)

            for s in range(2):
                ln_square(2 * NL, s)
            for s in range(2):
                act.wait_ge(z_ready[s], 2 * NL + 1)
                nc.scalar.activation(y[s][:, :], z[s][:, :], ACT.Identity, bias=pc[:, Q_LNB:Q_LNB + 1], scale=pc[:, Q_LNW:Q_LNW + 1]).then_inc(yn_ready[s], 1)

            def evac_x(n, t):
                act.wait_ge(tr_done, n + 1)
                nc.scalar.activation(x1t[:, :, P * t:P * t + P], psum[:, 4 + n % 2, :].rearrange("p (k t) -> p k t", k=KC), ACT.Copy).then_inc(xt_ready, 1)

            for t in range(NT):
                evac_x(t, t)
                if t >= 1:
                    act.wait_ge(lg_done, t)
                    nc.scalar.activation(lg[:, t - 1, :], psum[:, 6 + (t - 1) % 2, 0:P + NG], ACT.Copy).then_inc(lg_ready, 1)
            act.wait_ge(lg_done, NT)
            nc.scalar.activation(lg[:, NT - 1, :], psum[:, 6 + (NT - 1) % 2, 0:P + NG], ACT.Copy).then_inc(lg_ready, 1)
            act.wait_ge(ght_done, 1)
            nc.scalar.activation(ght[:, :, :], psum[:, 4, :].rearrange("p (q t) -> p q t", q=4), ACT.Copy).then_inc(ght_ready, 1)
            act.wait_ge(func_in_ready, 2)
            nc.scalar.activation(gs[:, 5, :], gs[:, 4, :], ACT.Exp).then_inc(func_ready, 1)
            for q in range(4):
                act.wait_ge(wtr_done, q + 1)
                nc.scalar.activation(tmpwt[:, 4 * q:4 * q + 4, :], psum[:, 6 + q % 2, :].rearrange("p (t n) -> p t n", t=4), ACT.Copy).then_inc(tmpwt_ready, 1)
                if q >= 1:
                    for t in range(4 * q - 4, 4 * q):
                        evac_x(NT + t, t)
            def abs_chunk(c):
                act.wait_ge(ld_abs[c % 2], 16 * (c // 2) + 16)
                nc.scalar.activation(wabs[:, c % 2, :], wabs[:, c % 2, :], ACT.Abs, accum_out=absum[:, c:c + 1]).then_inc(abs_done, 1)

            def hi_part(u):
                act.wait_ge(qk_done, u + 1)
                if u >= 2:
                    act.wait_ge(st_parts[u % 2], 16 * (u // 2))
                nc.scalar.activation(parts[u % 2][:, 0, :], psum[:, qk_banks(u), :].rearrange("p a t -> p (a t)"), ACT.Copy).then_inc(hi_ready, 1)

            def mid_part(u):
                act.wait_ge(r1_ready, u + 1)
                nc.scalar.activation(parts[u % 2][:, 1, :], resid[u % 2][:, :], ACT.Copy).then_inc(mid_ready, 1)

            def high_weights(u):
                b, w, c = UNITS[u]
                act.wait_ge(qk_done, u - 1 if u > 2 else 1)
                nc.scalar.activation(wh[u % 2][:, :, :], wqkv_sb[:, w * KC:w * KC + KC, P * c:P * c + P], ACT.Copy).then_inc(wh_ready, 1)

            hi_part(0)
            for t in range(NT - 4, NT):
                evac_x(NT + t, t)
            for f, u in ((mid_part, 0), (hi_part, 1), (mid_part, 1)):
                f(u)
            act.wait_ge(st_x2, 64)
            act.wait_ge(tr_done, 2 * NT)
            act.wait_ge(bproj_done, NT)
            act.wait_ge(xt_ready, 2 * NT)
            act.wait_ge(ld_qkv, 16)
            act.wait_ge(vpad_ready, 4)
            for t in range(NT):
                act.wait_ge(v_done, t + 1)
                if t >= 2:
                    act.wait_ge(st_v[t % 2], 16 * (t // 2))
                nc.scalar.activation(vpad[t % 2][:, :, 0:DK], psum[:, v_bank(t), :].rearrange("p (h d) -> p h d", d=DK), ACT.Copy).then_inc(v_ready, 1)
                abs_chunk(t)
                if t >= NT - 4 and t < NT - 2:
                    high_weights(t - (NT - 4) + 2)
                if t < 2 * KC:
                    b, k = t // KC, t % KC
                    nc.scalar.activation(x2h[b][:, k, :], x1t[:, k, b * L:b * L + L], ACT.Copy).then_inc(xh_ready, 1)

            for u in range(2, NU):
                hi_part(u)
                if u + 2 < NU:
                    high_weights(u + 2)
                if u < NU - 1:
                    mid_part(u)
                if u < 10:
                    abs_chunk(NT + u - 2)

            def group(i, c):
                first = isinstance(i, int) and 3 * i + c == 0
                for e in range(2 * GH * KT):
                    n, a = e // 2, e % 2
                    at_least(act, score_done, i, 192, 64 * c + e + 1)
                    if e % (2 * GH) == 0:
                        at_least(act, pv_done, i, 48, 16 * c + 2 * (n // GH) - 2)
                    nc.scalar.activation(probs[n % (2 * GH)][:, a * HALF:a * HALF + HALF], psum[:, score_bank(c, e), :], ACT.Exp, scale=DK ** -0.5).then_inc(exp_done, 1)
                    if e == 2 and first:
                        mid_part(NU - 1)
                    if e == 2 * GH - 1 and not first:
                        copy_o(i, c - 1)

            def copy_o(i, c):
                at_least(act, pv_done, i, 48, 16 * c + 16)
                at_least(act, st_o, i, 3 * 128, 128 * c)
                nc.scalar.activation(o_sb[:, :], psum[:, 4:6, :].rearrange("p a t -> p (a t)"), ACT.Copy).then_inc(o_ready, 1)

            over_groups(act, group)
            copy_o(0, NGRP - 1)
            act.wait_ge(o_ready, NGRP)
            for j in range(GH):
                r0 = (NGRP - 1) * (GH * DK) + DK * j
                act.dma_start(o_dram[r0:r0 + DK, :], o_sb[2 * DK * j:2 * DK * j + DK, :]).then_inc(st_o, 16)
                n = (NGRP - 1) * GH + j
                act.dma_start(den_dram[n:n + 1, :], o_sb[2 * DK * j + DK:2 * DK * j + DK + 1, :]).then_inc(st_o, 16)
            act.wait_ge(st_o, 128 * NGRP)
            act.wait_ge(tern_chain, 72)
            def high_part(t):
                act.wait_ge(x3_tr, t + 1)
                nc.scalar.activation(x3h[:, :, P * t:P * t + P], psum[:, x3_bank(t), :].rearrange("p (k t) -> p k t", k=KC), ACT.Copy).then_inc(x3h_ready, 1)
            for t in range(NT - 4):
                high_part(t)

            def gate(n, f):
                act.wait_ge(gate_up_done, n * HC + f + 1)
                wait_for(act, hid_ready, n * HC + f - 1)
                nc.scalar.activation(sg[f % 2][:, :], psum[:, 4 + 2 * (f % 2), :], ACT.Silu, scale=pc[:, Q_GS + f:Q_GS + f + 1]).then_inc(silu_ready, 1)
                act.wait_ge(hid_ready, n * HC + f + 1)
                wait_for(act, ffn_done, n * HC + f - 1)
                nc.scalar.activation(hh[f % 2][:, :], hid[f % 2][:, :], ACT.Copy).then_inc(hh_ready, 1)

            gate(0, 0)
            for t in range(NT - 4, NT):
                high_part(t)
            for f in range(1, HC):
                gate(0, f)
            with act.Fori(1, 4) as n:
                for f in range(HC):
                    gate(n, f)

        @block.vector
        def _(dve):
            ch = Chain(dve, dve_chain)
            nc.vector.memset(w1bd[:, :, :], 0.0).then_inc(zeroed, 1)
            nc.vector.memset(w2bd[:, :, :], 0.0).then_inc(zeroed, 1)
            nc.vector.memset(wout_sb[:, :, :], 0.0).then_inc(zeroed, 1)
            nc.vector.memset(gw2_sb[:, :, :], 0.0).then_inc(zeroed, 1)
            nc.vector.memset(cos[:, :, 0:1], 1.0)
            nc.vector.memset(sin[:, :, 0:1], 0.0)
            dve.wait_ge(ld_const, 48)
            tt = lambda o, a, b_, op: ch.step(nc.vector.tensor_tensor(o, a, b_, op))
            ts = lambda o, a, s1, s2, o0, o1: ch.step(nc.vector.tensor_scalar(o, a, s1, s2, o0, o1))
            q = lambda base: pc[:, base:base + NL]
            w = lambda k: pw[:, k, :]
            tt(w(0), q(Q_RE), q(Q_RE), ALU.mult)
            tt(w(1), q(Q_IM), q(Q_IM), ALU.mult)
            tt(w(0), w(0), w(1), ALU.add)
            ts(w(8), w(0), 1e-30, None, ALU.is_ge, ALU.bypass)
            nc.vector.tensor_scalar(w(2), w(0), 1e-30, None, ALU.max).then_inc(pow_in_ready, 1)
            dve.wait_ge(pow_ready, 1)
            nc.vector.tensor_tensor(w(4), w(2), w(3), ALU.mult).then_inc(func_in_ready, 1)
            tt(w(9), w(3), w(8), ALU.mult)
            ts(w(10), w(8), -1.0, 1.0, ALU.mult, ALU.add)
            tt(w(6), q(Q_RE), w(9), ALU.mult)
            tt(w(6), w(6), w(10), ALU.add)
            tt(w(7), q(Q_IM), w(9), ALU.mult)
            nc.vector.tensor_copy(unit[:, 0, 0, :], w(6))
            ch.step(nc.vector.tensor_copy(unit[:, 1, 0, :], w(7)))
            nc.vector.memset(w(14), 0.0).then_inc(unit_ready, 1)
            tt(w(0), w(6), q(Q_LR), ALU.mult)
            tt(w(1), w(7), q(Q_LI), ALU.mult)
            tt(w(11), w(0), w(1), ALU.subtract)
            tt(w(0), w(6), q(Q_LI), ALU.mult)
            tt(w(1), w(7), q(Q_LR), ALU.mult)
            tt(w(0), w(0), w(1), ALU.add)
            ts(w(12), w(0), -1.0, None, ALU.mult, ALU.bypass)
            def double(k, l0, l1):
                if k > 0:
                    dve.wait_ge(power_chain, 1 + 5 * k + 6 * (k // 3))
                n = 2 ** k
                bc = lambda r: unit[:, r, k, l0:l1].unsqueeze(2).to_broadcast([P, l1 - l0, n])
                c0, s0, a, b_ = cos[:, l0:l1, 0:n], sin[:, l0:l1, 0:n], tab1[:, l0:l1, 0:n], tab2[:, l0:l1, 0:n]
                nc.vector.tensor_tensor(a, c0, bc(0), ALU.mult)
                tt(b_, s0, bc(1), ALU.mult)
                tt(cos[:, l0:l1, n:2 * n], a, b_, ALU.subtract)
                nc.vector.tensor_tensor(a, c0, bc(1), ALU.mult)
                tt(b_, s0, bc(0), ALU.mult)
                tt(sin[:, l0:l1, n:2 * n], a, b_, ALU.add)

            for k in range(8):
                double(k, 0, NL)
            dve.wait_ge(func_ready, 1)
            ch.step(nc.vector.tensor_copy(w(13), w(5)))

            def ln_var(n, s):
                dve.wait_ge(var_sums[s], n + 1)
                nc.vector.tensor_scalar(var8[s][:, :], ps_b[s][:, 0:8], EPS, None, ALU.add).then_inc(var_ready[s], 1)

            def ln_scale(n, s):
                dve.wait_ge(spread[s], n + 1)
                dve.wait_ge(hc_copied[s], n + 1)
                nc.vector.tensor_tensor(z[s][:, :], ps_b[s], hc[s][:, :], ALU.mult).then_inc(z_ready[s], 1)

            def layer(i):
                wcol = lambda k: pw[:, k, bass.ds(i, 1)]
                for s in range(2):
                    wait_for(dve, centered[s], i * 2)
                nc.vector.tensor_scalar(cscl[:, :], center, pc[:, bass.ds(Q_SCL + i, 1)], None, ALU.mult).then_inc(cscl_ready, 1)
                for s in range(2):
                    ln_var(2 * i, s)
                if isinstance(i, int):
                    double(8, 0, NL)
                ln_scale(2 * i, 0)
                if isinstance(i, int):
                    double(9, 0, 1)
                ln_scale(2 * i, 1)
                for s in range(2):
                    sl = slice(s * HALF, s * HALF + HALF)
                    dve.wait_ge(y_ready[s], i + 1)
                    tt(re_in[s][:, :], cos[:, bass.ds(i, 1), sl].rearrange("p o t -> p (o t)"), y[s][:, :], ALU.mult)
                    first = wcol(11) if s == 0 else zr[0][:, HALF - 1:HALF]
                    ch.step(nc.vector.tensor_tensor_scan(zr[s][:, :], wcol(13).to_broadcast([P, HALF]), re_in[s][:, :], first, ALU.mult, ALU.add))
                    dve.wait_ge(im_in_ready[s], i + 1)
                    first = wcol(12) if s == 0 else zi[0][:, HALF - 1:HALF]
                    nc.vector.tensor_tensor_scan(zi[s][:, :], wcol(13).to_broadcast([P, HALF]), im_in[s][:, :], first, ALU.mult, ALU.add).then_inc(zi_ready[s], 1)
                    nc.vector.tensor_tensor(re_p[s][:, :], cos[:, bass.ds(i, 1), sl].rearrange("p o t -> p (o t)"), zr[s][:, :], ALU.mult).then_inc(re_p_ready[s], 1)
                    if s == 0:
                        dve.wait_ge(zi_ready[0], i + 1)
                for s in range(2):
                    ln_var(2 * i + 1, s)
                for s in range(2):
                    dve.wait_ge(re_p_ready[s], i + 1)
                    dve.wait_ge(im_p_ready[s], i + 1)
                    tt(re_p[s][:, :], re_p[s][:, :], im_p[s][:, :], ALU.add)
                    nc.vector.scalar_tensor_tensor(h[:, s, :], re_p[s][:, :], pc[:, bass.ds(Q_SCL + i, 1)], h[:, s, :], ALU.mult, ALU.add).then_inc(h_ready[s], 1)
                for s in range(2):
                    ln_scale(2 * i + 1, s)
                if isinstance(i, int):
                    double(9, 1, NL)
                for s in range(2):
                    dve.wait_ge(down_done[s], i + 1)
                    nc.vector.scalar_tensor_tensor(h[:, s, :], ps_c[s], pc[:, bass.ds(Q_B2 + i, 1)], h[:, s, :], ALU.add, ALU.add).then_inc(h_ready[s], 1)

            layer(0)
            start, PER = ch.n, 6
            with dve.Fori(1, NL) as i:
                ch.base, ch.n = i * PER + (start - PER), 0
                layer(i)
                assert ch.n == PER
            ch.base, ch.n = 0, start + (NL - 1) * PER
            for s in range(2):
                ln_var(2 * NL, s)
            for s in range(2):
                ln_scale(2 * NL, s)

            def ln_tiles(r, q, projected):
                for t in range(4 * q, 4 * q + 4):
                    dve.wait_ge(projected, t + 1)
                    nc.vector.tensor_tensor(xres[:, t, :], psum[:, t % 4, :], xres[:, t, :], ALU.add).then_inc(added, 1)
                for t in range(4 * q, 4 * q + 4):
                    dve.wait_ge(added, NT * r + t + 1)
                    nc.vector.bn_stats(stats[:, t % 4, :], xres[:, t, :]).then_inc(dve_chain, 1)
                    ch.n += 1
                for t in range(4 * q, 4 * q + 4):
                    dve.wait_ge(dve_chain, ch.n - 3 if t % 4 == 0 else ch.n - 3)
                    ch.step(nc.vector.bn_aggr(mv[:, t, :], stats[:, t % 4, :]))
                sl = slice(4 * q, 4 * q + 4)
                nc.vector.tensor_scalar(varr[:, sl], mv[:, sl, 1], EPS, None, ALU.add).then_inc(var4_ready, 1)
                dve.wait_ge(rstd4_ready, 4 * r + q + 1)
                for t in range(4 * q, 4 * q + 4):
                    nc.vector.tensor_scalar(xres[:, t, :], xres[:, t, :], mv[:, t, 0:1], rstd[:, t:t + 1], ALU.subtract, ALU.mult).then_inc(tile_ready, 1)

            dve.wait_ge(xres_biased, NL)
            for q in range(4):
                ln_tiles(0, q, proj_done)

            row = lambda r0, n, t: pr[:, r0:r0 + n].unsqueeze(1).to_broadcast([P, t, n])
            over = lambda a, n: a.unsqueeze(2).to_broadcast([P, NT, n])
            G = lambda k: gs[:, k, :]
            red = lambda o, a, op: ch.step(nc.vector.tensor_reduce(o, a, AX.X, op))
            dve.wait_ge(lg_ready, NT)
            tt(gh[:, :, :], lg[:, :, P:P + NG], row(R_GB1, NG, NT), ALU.add)
            red(G(0), gh[:, :, :], ALU.add)
            ts(G(0), G(0), 1.0 / NG, None, ALU.mult, ALU.bypass)
            tt(gh[:, :, :], gh[:, :, :], over(G(0), NG), ALU.subtract)
            tt(gsq[:, :, :], gh[:, :, :], gh[:, :, :], ALU.mult)
            red(G(1), gsq[:, :, :], ALU.add)
            nc.vector.tensor_scalar(G(1), G(1), 1.0 / NG, EPS, ALU.mult, ALU.add).then_inc(pow_in_ready, 1)
            dve.wait_ge(pow_ready, 2)
            tt(gh[:, :, :], gh[:, :, :], over(G(2), NG), ALU.mult)
            tt(gh[:, :, :], gh[:, :, :], row(R_GAM, NG, NT), ALU.mult)
            tt(gh[:, :, :], gh[:, :, :], row(R_BET, NG, NT), ALU.add)
            nc.vector.tensor_scalar(gh[:, :, :], gh[:, :, :], 0.0, None, ALU.max).then_inc(gh_ready, 1)
            E_ = lambda k: ge[:, k, :, :]
            revb = rev.unsqueeze(1).to_broadcast([P, NT, NE])
            dve.wait_ge(gates_done, 1)
            tt(E_(0), psum[:, 5, 0:P].rearrange("p (t e) -> p t e", t=NT), row(R_GB2, NE, NT), ALU.add)

            def top(k, gates, best):
                red(best, gates, ALU.max)
                tt(E_(2), gates, over(best, NE), ALU.is_equal)
                tt(E_(2), E_(2), revb, ALU.mult)
                red(G(6), E_(2), ALU.max)
                tt(oh[:, k, :, :], E_(2), over(G(6), NE), ALU.is_equal)

            top(0, E_(0), G(3))
            ts(E_(3), oh[:, 0, :, :], -3e38, None, ALU.mult, ALU.bypass)
            tt(E_(1), E_(0), E_(3), ALU.add)
            top(1, E_(1), G(7))
            nc.vector.tensor_tensor(G(4), G(7), G(3), ALU.subtract).then_inc(func_in_ready, 1)
            nc.vector.tensor_copy(E_(4), oh[:, 0, :, :]).then_inc(oh_ready, 1)
            dve.wait_ge(func_ready, 2)
            ts(G(8), G(5), 1.0, None, ALU.add, ALU.bypass)
            ch.step(nc.vector.reciprocal(G(8), G(8)))
            tt(G(9), G(5), G(8), ALU.mult)
            dve.wait_ge(cnt_done, 1)
            red(cnt[:, :, :], psum[:, 4, 0:2 * P].rearrange("p (k t e) -> p k e t", k=2, t=NT), ALU.add)
            ts(cnt[:, :, :], cnt[:, :, :], float(CAPACITY), 1.0 / ER, ALU.is_le, ALU.mult)
            for k in range(2):
                tt(E_(k), oh[:, k, :, :], over(G(8 + k), NE), ALU.mult)
                tt(E_(k), E_(k), cnt[:, k, :].unsqueeze(1).to_broadcast([P, NT, NE]), ALU.mult)
            tt(wexp[:, :, :], E_(0), E_(1), ALU.add)
            for q in range(4):
                sl = slice(4 * q, 4 * q + 4)
                nc.vector.tensor_tensor(tmpw[:, sl, :].rearrange("p t (e r) -> p t e r", e=NE), lg[:, sl, 0:P].rearrange("p t (e r) -> p t e r", e=NE),
                                        wexp[:, sl, :].unsqueeze(3).to_broadcast([P, 4, NE, ER]), ALU.mult).then_inc(tmpw_ready, 1)
            for q in range(4):
                ln_tiles(1, q, bproj_done)

            def first_part(u):
                dve.wait_ge(hi_ready, u + 1)
                if u >= 2:
                    dve.wait_ge(lo_ready, u - 1)
                nc.vector.tensor_tensor(resid[u % 2][:, :], psum[:, qk_banks(u), :].rearrange("p a t -> p (a t)"), parts[u % 2][:, 0, :], ALU.subtract).then_inc(r1_ready, 1)

            def last_part(u):
                dve.wait_ge(mid_ready, u + 1)
                nc.vector.tensor_tensor(parts[u % 2][:, 2, :], resid[u % 2][:, :], parts[u % 2][:, 1, :], ALU.subtract).then_inc(lo_ready, 1)

            def maximum(i, c, m):
                qt, j, a = m // (2 * GH), m // 2 % GH, m % 2
                at_least(dve, mx_done, i, 192, 64 * c + m + 1)
                nc.vector.tensor_reduce(mx[c % 2][:, j, qt, a:a + 1], psum[:, max_bank(c, m), :], AX.X, ALU.max).then_inc(mx_read, 2)

            def reduce_maxima(i, c):
                at_least(dve, mx_read, i, 2 * 192, 2 * (64 * c + 64))
                at_least(dve, nmt_done, i, 3, c)
                nc.vector.tensor_reduce(nm[:, :].rearrange("p (j q) -> p j q", j=GH), mx[c % 2][:, :, :, :], AX.X, ALU.max, negate=True).then_inc(nm_ready, 1)

            def split_maxima(i, c):
                at_least(dve, nmt_done, i, 3, c + 1)
                if not (isinstance(i, int) and 3 * i + c == 0):
                    dve.wait_ge(ld_nm[(c - 1) % 3], ((i + (c - 1) // 3) + 1) * 16)
                ch2.step(nc.vector.tensor_copy(nmh[:, :], psum[0:GH * KT, turn_bank(c), 0:P]))
                nc.vector.tensor_tensor(nml[:, :], psum[0:GH * KT, turn_bank(c), 0:P], nmh[:, :], ALU.subtract).then_inc(nmt_read, 1)

            def first_maxima_of(kind, n, start=0, end=None):
                for what in first_maxima_after(kind, n)[start:end]:
                    if what == "reduce":
                        reduce_maxima(0, 0)
                    elif what == "turn":
                        split_maxima(0, 0)
                    else:
                        maximum(0, *what)

            ch2 = Chain(dve, nmh_ready)
            for f, u in ((first_part, 0), (last_part, 0)):
                f(u)
            dve.wait_ge(tmpwt_ready, 4)
            dve.wait_ge(bproj_done, NT)
            dve.wait_ge(tr_done, 2 * NT)
            dve.wait_ge(st_x2, 64)
            for k in range(2):
                nc.vector.memset(vpad[k][:, :, DK:DK + 1], 1.0).then_inc(vpad_ready, 1)
                nc.vector.memset(vpad[k][:, :, DK + 1:], 0.0).then_inc(vpad_ready, 1)
            for f, u in ((first_part, 1), (last_part, 1)):
                f(u)
            def low_x2(b, k):
                if k == 0:
                    dve.wait_ge(v_done, KT * b + KT)
                    dve.wait_ge(qk_done, 2)
                dve.wait_ge(xh_ready, KC * b + k + 1)
                cols = slice(b * L, b * L + L)
                nc.vector.tensor_tensor(x2l[:, k, cols], x1t[:, k, cols], x2h[b][:, k, :].bitcast(F32), ALU.subtract).then_inc(xl_ready, 1)

            def low_weights(u):
                b, w, c = UNITS[u]
                dve.wait_ge(wh_ready, u - 1)
                nc.vector.tensor_tensor(wl[u % 2][:, :, :], wqkv_sb[:, w * KC:w * KC + KC, P * c:P * c + P], wh[u % 2][:, :, :].bitcast(F32), ALU.subtract).then_inc(wl_ready, 1)

            for t in range(NT):
                first_maxima_of("v", t)
                if NT - 7 <= t < NT - 7 + KC:
                    low_x2(0, t - (NT - 7))
                if t in (NT - 3, NT - 2):
                    low_weights(t - (NT - 3) + 2)
            first_maxima_of("u", 2)
            for u in range(2, NU):
                if u < 2 + KC:
                    low_x2(1, u - 2)
                if u == 12:
                    dve.wait_ge(abs_done, 24)
                    nc.vector.tensor_reduce(absum3[:, :], absum[:, :].rearrange("p (w c) -> p w c", w=3), AX.X, ALU.add).then_inc(abs_sum, 1)
                if u == 13:
                    dve.wait_ge(abs_all, 1)
                    ts(thr[:, :], psum[:, 2, 0:3], 1.0 / (D * HID), THRESH, ALU.mult, ALU.mult)
                    nc.vector.tensor_scalar(nthr[:, :], thr[:, :], -1.0, None, ALU.mult).then_inc(thr_ready, 1)
                first_part(u)
                if u + 1 < NU:
                    first_maxima_of("u", u + 1, 0, 2)
                if u + 2 < NU:
                    low_weights(u + 2)
                if u + 1 < NU:
                    first_maxima_of("u", u + 1, 2)
                if u < NU - 1:
                    last_part(u)

            def group(i, c):
                ch2.base, ch2.n = i * 3 + c + 1, 0
                g = 3 * i + c if isinstance(i, int) else 1
                if g + 1 < NGRP:
                    for m in range(32, 64):
                        maximum(i, c + 1, m)
                        if g == 0 and m == 34:
                            last_part(NU - 1)
                    reduce_maxima(i, c + 1)
                    if g + 2 < NGRP:
                        maximum(i, c + 2, 0)
                    split_maxima(i, c + 1)
                if g + 2 < NGRP:
                    for m in range(1, 32):
                        maximum(i, c + 2, m)

            over_groups(dve, group)

            def reciprocals(b):
                dve.wait_ge(ld_den, 16 * b + 16)
                nc.vector.reciprocal(den_sb[b], den_sb[b]).then_inc(den_ready, 1)

            reciprocals(0)

            def normalise(q, k):
                if k == 0:
                    dve.wait_ge(ld_rb, 64 * q + 64)
                dve.wait_ge(ld_od[k], 16 * q + 16)
                nc.vector.tensor_tensor(od[k][:, :, :], od[k][:, :, :], rb[q][:, :, P * k:P * k + P], ALU.mult).then_inc(normed, 1)

            def ln_stats(r, q, x, added):
                for k in range(4):
                    dve.wait_ge(added, q * 4 + k + 1)
                    nc.vector.bn_stats(stats[:, k, :], x(k)).then_inc(x_stats, 1)
                dve.wait_ge(x_stats, q * 4 + 4 * r + 4)
                nc.vector.memset(varr[:, 0:4], EPS).then_inc(x_mv, 1)
                for k in range(4):
                    nc.vector.bn_aggr(mv[:, k, :], stats[:, k, :]).then_inc(x_mv, 1)
                dve.wait_ge(x_mv, q * 5 + 5 * r + 5)
                nc.vector.tensor_tensor(varr[:, 0:4], mv[:, 0:4, 1], varr[:, 0:4], ALU.add).then_inc(x_var, 1)

            def ln_apply(r, q, x, ready):
                dve.wait_ge(x_rstd, q + r + 1)
                for k in range(4):
                    nc.vector.tensor_scalar(x(k), x(k), mv[:, k, 0:1], rstd[:, k:k + 1], ALU.subtract, ALU.mult).then_inc(ready, 1)

            for k in range(4):
                normalise(0, k)

            def low_parts(q):
                for t in range(4 * q, 4 * q + 4):
                    dve.wait_ge(x3h_ready, t + 1)
                    nc.vector.tensor_tensor(x3l[:, :, P * t:P * t + P], psum[:, x3_bank(t), :].rearrange("p (k t) -> p k t", k=KC), x3h[:, :, P * t:P * t + P].bitcast(F32), ALU.subtract).then_inc(x3l_ready, 1)

            for q in range(4):
                x = lambda k: x3t[4 * (q % 2) + k][:, :]
                for k in range(4):
                    if k == 0:
                        dve.wait_ge(ld_x2t[q % 2], (64, 48, 128, 112)[q])
                    if q == 1 and k == 3:
                        dve.wait_ge(ld_x2t[2], 16)
                    dve.wait_ge(oproj_done, 4 * q + k + 1)
                    nc.vector.tensor_tensor(x(k), psum[:, k, :], x(k), ALU.add).then_inc(x_added, 1)
                    if k > 0 and q < 3:
                        normalise(q + 1, k - 1)
                    if q == 0 and k == 1:
                        reciprocals(1)
                if q < 3:
                    normalise(q + 1, 3)
                if q == 3:
                    low_parts(2)
                ln_stats(0, q, x, x_added)
                if q in (1, 2):
                    low_parts(q - 1)
                ln_apply(0, q, x, x3_ready)
            yk = lambda k: yt[:, k, :]

            def hidden(n, f):
                dve.wait_ge(silu_ready, n * HC + f + 1)
                wait_for(dve, hl_ready, n * HC + f - 1)
                nc.vector.scalar_tensor_tensor(hid[f % 2][:, :], psum[:, 5 + 2 * (f % 2), :], pc[:, Q_US + f:Q_US + f + 1], sg[f % 2][:, :], ALU.mult, ALU.mult).then_inc(hid_ready, 1)
                dve.wait_ge(hh_ready, n * HC + f + 1)
                wait_for(dve, ffn_done, n * HC + f - 1)
                nc.vector.tensor_tensor(hl[f % 2][:, :], hid[f % 2][:, :], hh[f % 2][:, :].bitcast(F32), ALU.subtract).then_inc(hl_ready, 1)

            def finish(n, step):
                if step == 0:
                    dve.wait_ge(ld_xin, n * 16 + 16)
                    for k in range(4):
                        dve.wait_ge(yt_ready, n * 4 + k + 1)
                        nc.vector.tensor_tensor(yk(k), yk(k), xin[:, k, :], ALU.add).then_inc(f_added, 1)
                elif step == 1:
                    ln_stats(4, n, yk, f_added)
                elif step == 2:
                    ln_apply(4, n, yk, out_ready)

            def block_of_tokens(n, first, last):
                for f in range(1, HC):
                    hidden(n, f)
                    if not first:
                        finish(n - 1, f - 1)
                if not last:
                    hidden(n + 1, 0)
                dve.wait_ge(ffn_done, n * HC + HC)
                wait_for(dve, st_out, n * 64)
                for k in range(4):
                    nc.vector.tensor_tensor(yk(k), psum[:, k, :], pr[:, R_DS:R_DS + D], ALU.mult).then_inc(yt_ready, 1)

            hidden(0, 0)
            low_parts(3)
            dve.wait_ge(x3_tr, NT)
            dve.wait_ge(st_x3, 16 * NT)
            block_of_tokens(0, True, False)
            with dve.Fori(1, 3) as n:
                block_of_tokens(n, False, False)
            block_of_tokens(3, False, True)
            for step in range(3):
                finish(3, step)

        @block.tensor
        def _(pe):
            mm = nc.tensor.matmul
            pe.wait_ge(ld_win, 16)
            for s in range(2):
                pe.wait_ge(ld_x[s], 32)
                for k in range(KC):
                    for b in range(B):
                        t0 = b * L + s * HALF
                        last = mm(ps_c[s][DH * b:DH * b + DH, :], win_sb[:, k, :], xt[:, k, t0:t0 + HALF], start=(k == 0), stop=(k == KC - 1))
                last.then_inc(inproj[s], 1)
            pe.wait_ge(ld_const, 48)

            def ln_center(n, s):
                pe.wait_ge(h_ready[s], n + 1)
                mm(ps_c[s], center, h[:, s, :], start=True, stop=True).then_inc(centered[s], 1)

            def ln_sums(n, s):
                pe.wait_ge(squared[s], n + 1)
                for t in range(4):
                    last = mm(ps_b[s][:, 2 * t:2 * t + 2], sq[s][:, P * t:P * t + P], blk_mean, start=True, stop=True)
                last.then_inc(var_sums[s], 1)

            def ln_spread(n, s):
                pe.wait_ge(rstd_ready[s], n + 1)
                for t in range(4):
                    for b in range(B):
                        last = mm(ps_b[s][DH * b:DH * b + DH, P * t:P * t + P], rstd8[s][:, 2 * t + b:2 * t + b + 1].to_broadcast([P, DH]), ident, start=True, stop=True)
                last.then_inc(spread[s], 1)

            with pe.Fori(0, NL) as i:
                for f in (ln_center, ln_sums, ln_spread):
                    for s in range(2):
                        f(2 * i, s)
                pe.wait_ge(cscl_ready, i + 1)
                for s in range(2):
                    pe.wait_ge(hc_copied[s], i * 2 + 1)
                    mm(ps_c[s], center, h[:, s, :], start=True, stop=False)
                for s in range(2):
                    pe.wait_ge(re_p_ready[s], i + 1)
                    mm(ps_c[s], cscl[:, :], re_p[s][:, :], start=False, stop=False)
                    pe.wait_ge(im_p_ready[s], i + 1)
                    mm(ps_c[s], cscl[:, :], im_p[s][:, :], start=False, stop=True).then_inc(centered[s], 1)
                for f in (ln_sums, ln_spread):
                    for s in range(2):
                        f(2 * i + 1, s)
                pe.wait_ge(ld_w, 64 * (i + 1))
                for c in range(FC + 2):
                    for s in range(2):
                        if c == 0:
                            pe.wait_ge(yn_ready[s], i + 1)
                        if c < FC:
                            if c >= 2:
                                pe.wait_ge(g_ready[s], FC * i + c - 1)
                            mm(ps_f[s][c % 2], w1bd[:, c, :], y[s][:, :], start=True, stop=True).then_inc(up_done[s], 1)
                        if c >= 2:
                            pe.wait_ge(g_ready[s], FC * i + c - 1)
                            last = mm(ps_c[s], w2bd[:, c - 2, :], g[s][:, c - 2, :], start=(c == 2), stop=(c == FC + 1))
                            if c == FC + 1:
                                last.then_inc(down_done[s], 1)

            for f in (ln_center, ln_sums, ln_spread):
                for s in range(2):
                    f(2 * NL, s)

            def out_proj(q):
                for t in range(4 * q, 4 * q + 4):
                    b, s = t // (NT // B), (t // 4) % 2
                    if t < 4:
                        pe.wait_ge(yn_ready[0], NL + 1)
                        pe.wait_ge(yn_ready[1], NL + 1)
                        pe.wait_ge(ld_bw, 16 * 9)
                    else:
                        pe.wait_ge(added, t - 3)
                    mm(psum[:, t % 4, :], y[s][:, P * (t % 4):P * (t % 4) + P], wout_sb[:, b, :], start=True, stop=True).then_inc(proj_done, 1)

            def transpose_x(n, t):
                pe.wait_ge(tile_ready, n + 1)
                if n >= 2:
                    pe.wait_ge(xt_ready, n - 1)
                if n == NT:
                    pe.wait_ge(ght_ready, 1)
                for k in range(KC):
                    last = nc.tensor.transpose(psum[:, 4 + n % 2, P * k:P * k + P], xres[:, t, P * k:P * k + P], ident)
                last.then_inc(tr_done, 1)

            def lora_gate(t):
                pe.wait_ge(xt_ready, t + 1)
                if t >= 2:
                    pe.wait_ge(lg_ready, t - 1)
                for k in range(KC):
                    last = mm(psum[:, 6 + t % 2, 0:P + NG], x1t[:, k, P * t:P * t + P], ag_sb[:, k, :], start=(k == 0), stop=(k == KC - 1))
                last.then_inc(lg_done, 1)

            def main_proj(q, tiles=range(4), chunks=range(KC)):
                for t in (4 * q + j for j in tiles):
                    pe.wait_ge(added, NT + t - 3)
                    for k in chunks:
                        mm(psum[:, t % 4, :], x1t[:, k, P * t:P * t + P], main_sb[:, k, :], start=(k == 0), stop=False)

            def maximum(i, c, m):
                qt, j, a = m // (2 * GH), m // 2 % GH, m % 2
                if m == 0:
                    pe.wait_ge(ld_stack[c % 3], ((i + c // 3) + 1) * 192)
                if m == 2:
                    at_least(pe, nmt_read, i, 3, c)
                at_least(pe, mx_read, i, 2 * 192, 2 * (64 * c + m - 2))
                mm(psum[:, max_bank(c, m), :], qst[c % 3][0:SR, j, P * qt:P * qt + P], kst[c % 3][0:SR, j, a * HALF:a * HALF + HALF], start=True, stop=True).then_inc(mx_done, 1)

            def turn_maxima(i, c):
                at_least(pe, nm_ready, i, 3, c + 1)
                nc.tensor.transpose(psum[0:GH * KT, turn_bank(c), 0:P], nm[:, :], ident).then_inc(nmt_done, 1)

            def first_maxima_of(kind, n, start=0, end=None):
                for what in first_maxima_after(kind, n)[start:end]:
                    if what == "turn":
                        turn_maxima(0, 0)
                    elif what != "reduce":
                        maximum(0, *what)

            def project_unit(u):
                b, w, c = UNITS[u]
                if u >= 2:
                    pe.wait_ge(r1_ready, u - 1)
                if u == 3:
                    pe.wait_ge(v_ready, NT)
                if u >= 2:
                    pe.wait_ge(xl_ready, KC * b + KC)
                    pe.wait_ge(wl_ready, u - 1)
                for a in range(2):
                    first_maxima_of("u", u, 2 * a, 2 * a + 2)
                    out = psum[:, qk_banks(u), :][:, a, :]
                    for k in range(KC):
                        if u < 2:
                            last = mm(out, wqkv_sb[:, w * KC + k, P * c:P * c + P], x1t[:, k, b * L + a * HALF:b * L + a * HALF + HALF], start=(k == 0), stop=(k == KC - 1))
                        else:
                            xh, xl = x2h[b][:, k, a * HALF:a * HALF + HALF], x2l[:, k, b * L + a * HALF:b * L + a * HALF + HALF]
                            mm(out, wh[u % 2][:, k, :], xh, start=(k == 0), stop=False)
                            mm(out, wh[u % 2][:, k, :], xl, start=False, stop=False)
                            last = mm(out, wl[u % 2][:, k, :], xh, start=False, stop=(k == KC - 1))
                last.then_inc(qk_done, 1)

            def project_v(t):
                if t == 1:
                    pe.wait_ge(r1_ready, 2)
                if t >= 2:
                    pe.wait_ge(v_ready, t - 1)
                for k in range(KC):
                    last = mm(psum[:, v_bank(t), :], x1t[:, k, P * t:P * t + P], wqkv_sb[:, 2 * KC + k, :], start=(k == 0), stop=(k == KC - 1))
                last.then_inc(v_done, 1)

            out_proj(0)
            for q in range(4):
                if q < 3:
                    out_proj(q + 1)
                for t in range(4 * q, 4 * q + 4):
                    transpose_x(t, t)
                    if t >= 1:
                        lora_gate(t - 1)
            lora_gate(NT - 1)
            main_proj(0, range(3))
            pe.wait_ge(gh_ready, 1)
            for q in range(4):
                last = nc.tensor.transpose(psum[:, 4, P * q:P * q + P], gh[:, 4 * q:4 * q + 4, :].rearrange("p t n -> p (t n)"), ident)
            last.then_inc(ght_done, 1)
            main_proj(0, (3,), (0,))
            pe.wait_ge(ght_ready, 1)
            for q in range(4):
                last = mm(psum[:, 5, 4 * NE * q:4 * NE * q + 4 * NE], ght[:, q, :], gw2_sb[:, :, :].rearrange("p t e -> p (t e)"), start=True, stop=True)
            last.then_inc(gates_done, 1)
            main_proj(0, (3,), range(1, KC - 1))
            pe.wait_ge(oh_ready, 1)
            mm(psum[:, 4, 0:2 * P], ones, oh[:, :, :, :].rearrange("p k t e -> p (k t e)"), start=True, stop=True).then_inc(cnt_done, 1)
            for q in range(4):
                if q >= 1:
                    main_proj(q, range(3))
                pe.wait_ge(tmpw_ready, q + 1)
                if q == 0:
                    pe.wait_ge(lg_ready, NT)
                if q >= 2:
                    pe.wait_ge(tmpwt_ready, q - 1)
                for t in range(4):
                    last = nc.tensor.transpose(psum[:, 6 + q % 2, P * t:P * t + P], tmpw[:, 4 * q + t, :], ident)
                last.then_inc(wtr_done, 1)
                main_proj(q, (3,), range(KC) if q >= 1 else (KC - 1,))
                pe.wait_ge(tmpwt_ready, q + 1)
                for t in range(4 * q, 4 * q + 4):
                    mm(psum[:, t % 4, :], tmpwt[:, t, :], lorab_sb[:, :], start=False, stop=True).then_inc(bproj_done, 1)
                if q >= 1:
                    for t in range(4 * q - 4, 4 * q):
                        transpose_x(NT + t, t)
            pe.wait_ge(ld_qkv, 16)
            pe.wait_ge(xt_ready, NT + KT)
            pe.wait_ge(added, 2 * NT)
            project_unit(0)
            for t in range(NT - 4, NT):
                transpose_x(NT + t, t)

            pe.wait_ge(xt_ready, 2 * NT)
            project_unit(1)
            for t in range(NT):
                project_v(t)
                first_maxima_of("v", t)
            for u in range(2, NU):
                if u == 13:
                    pe.wait_ge(abs_sum, 1)
                    mm(psum[:, 2, 0:3], ones, absum3[:, :], start=True, stop=True).then_inc(abs_all, 1)
                project_unit(u)
            pe.wait_ge(ones_ready, 3)
            pe.wait_ge(thr_ready, 1)

            def scores(i, c, e):
                n, a = e // 2, e % 2
                kt, j = n // GH, n % GH
                at_least(pe, exp_done, i, 192, 64 * c + e - 2)
                mm(psum[:, score_bank(c, e), :], kst[c % 3][0:SR + 2, j, P * kt:P * kt + P], qst[c % 3][0:SR + 2, j, a * HALF:a * HALF + HALF], start=True, stop=True).then_inc(score_done, 1)

            def gather(i, c, kt, a):
                at_least(pe, exp_done, i, 192, 64 * c + 2 * GH * kt + 2 * GH)
                if kt == 0 and a == 0:
                    at_least(pe, o_ready, i, 3, c)
                    pe.wait_ge(ld_v[c % 3], ((i + c // 3) + 1) * 16)
                for j in range(GH):
                    r = slice(2 * DK * j, 2 * DK * j + 2 * DK)
                    last = mm(psum[r, 4 + a, :], vg[c % 3][:, kt, r], probs[(GH * kt + j) % (2 * GH)][:, a * HALF:a * HALF + HALF], start=(kt == 0), stop=(kt == KT - 1))
                last.then_inc(pv_done, 1)

            def group(i, c):
                g = 3 * i + c if isinstance(i, int) else 1
                if g == 0:
                    pe.wait_ge(r1_ready, NU - 1)
                pe.wait_ge(ld_nm[c % 3], ((i + c // 3) + 1) * 16)
                for h in range(2 * KT):
                    kt, a = h // 2, h % 2
                    ahead_by = 1 if h < KT else 2
                    for k in range(4):
                        if g + ahead_by < NGRP:
                            maximum(i, c + ahead_by, 4 * ((h + KT) % (2 * KT)) + k)
                        scores(i, c, 4 * h + k)
                        if h == KT and k == 0 and g + 1 < NGRP:
                            turn_maxima(i, c + 1)
                    if g == 0 and h == 2:
                        pe.wait_ge(r1_ready, NU)
                    if kt > 0:
                        gather(i, c, kt - 1, a)
                    elif g > 0:
                        gather(i, c - 1, KT - 1, a)

            over_groups(pe, group)
            for a in range(2):
                gather(0, NGRP - 1, KT - 1, a)

            def out_projection(q):
                if q == 0:
                    pe.wait_ge(ld_qkv, 32)
                    pe.wait_ge(exp_done, 64 * NGRP)
                for k in range(4):
                    pe.wait_ge(normed, 4 * q + k + 1)
                    if q > 0:
                        pe.wait_ge(x_added, 4 * q - 4 + k + 1)
                    for c in range(KC):
                        last = mm(psum[:, k, :], od[k][:, c, :], wo_sb[:, c, :], start=(c == 0), stop=(c == KC - 1))
                    last.then_inc(oproj_done, 1)

            out_projection(0)

            def transpose_x3(q):
                for k in range(4):
                    t = 4 * q + k
                    pe.wait_ge(x3_ready, t + 1)
                    if q in (1, 2):
                        pe.wait_ge(x3l_ready, t - 3)
                    for c in range(KC):
                        last = nc.tensor.transpose(psum[:, x3_bank(t), P * c:P * c + P], x3t[4 * (q % 2) + k][:, P * c:P * c + P], ident)
                    last.then_inc(x3_tr, 1)
            def gate_up(n, f):
                wait_for(pe, hid_ready, n * HC + f - 1)
                cols = slice(P * (f % 8), P * (f % 8) + P)
                for w in range(2):
                    for k in range(KC):
                        for x in (x3h, x3l):
                            last = mm(psum[:, 4 + 2 * (f % 2) + w, :], tern_sb[:, 8 * w + 2 * k + f // 8, cols], x[:, k, bass.ds(n * HALF, HALF)],
                                      start=(k == 0 and x is x3h), stop=(k == KC - 1 and x is x3l))
                last.then_inc(gate_up_done, 1)

            def down(n, f):
                pe.wait_ge(hl_ready, n * HC + f + 1)
                if f == 0:
                    wait_for(pe, yt_ready, n * 4)
                cols = slice(D * (f % 2), D * (f % 2) + D)
                for k in range(4):
                    if f == 0 and isinstance(n, int) and n == 0:
                        pe.wait_ge(x3l_ready, NT - 3 + k)
                    for x in (hh, hl):
                        last = mm(psum[:, k, :], x[f % 2][:, P * k:P * k + P], tern_sb[:, 16 + f // 2, cols], start=(f == 0 and x is hh), stop=(f == HC - 1 and x is hl))
                last.then_inc(ffn_done, 1)

            for q in range(3):
                out_projection(q + 1)
                transpose_x3(q)
            pe.wait_ge(tern_chain, 72)
            pe.wait_ge(x3l_ready, NT - 6)
            gate_up(0, 0)
            pe.wait_ge(x3l_ready, NT - 4)
            gate_up(0, 1)
            transpose_x3(3)

            def ffn_block(n, last):
                for f in range(HC):
                    down(n, f)
                    if f + 2 < HC:
                        gate_up(n, f + 2)
                    elif not last:
                        gate_up(n + 1, f + 2 - HC)

            ffn_block(0, False)
            with pe.Fori(1, 3) as n:
                ffn_block(n, False)
            ffn_block(3, True)


def kernel(**inputs):
    import numpy as np
    import concourse.bacc as bacc
    from concourse import mybir
    from concourse.bass_utils import run_bass_kernel_spmd

    a = {name: np.asarray(value) for name, value in inputs.items()}
    attn = lambda name: a["L0_attn_" + name]
    ffn = lambda name: a["L0_ffn_" + name]
    tf = lambda name: a["L1_ffn_" + name]
    x = attn("x").reshape(TOK, D)
    by_half = lambda w: w.T.reshape(KC, P, 2, L).transpose(0, 2, 1, 3).reshape(2 * KC, P, L)
    by_pair = lambda w: w.T.reshape(HC // 2, 2, P, D).transpose(0, 2, 1, 3).reshape(HC // 2, P, L)
    both = lambda v: np.concatenate([v, v], -1)
    consts = np.zeros((P, C_END), np.float32)
    consts[:, C_ID:C_ID + P] = np.eye(P)
    consts[:, C_CEN:C_CEN + P] = np.kron(np.eye(B), np.eye(DH) - 1 / DH)
    consts[:, C_ONE:C_ONE + P] = 1
    consts[:, C_BLK:C_BLK + B] = np.kron(np.eye(B), np.ones((DH, 1))) / DH
    consts[:, C_REV:] = NE - np.arange(NE)
    columns = [both(attn(n)).T for n in ("ln1_w", "ln1_b", "phz_re", "phz_im", "lc_re", "lc_im", "sc_lin", "ln2_w", "ln2_b", "b2")]
    columns += [np.broadcast_to(both(attn(n))[:, None], (P, 4)) for n in ("bin", "lnl_w", "lnl_b")]
    columns += [both(attn("b1").reshape(NL, FC, DH)).reshape(NL * FC, P).T]
    columns += [tf(n).reshape(HC, P).T for n in ("gate_scale", "up_scale")]
    row = np.concatenate([attn("bout"), tf("down_scale").ravel(), ffn("gb1"), ffn("ln_gamma"), ffn("ln_beta"), ffn("gb2")])
    arrays = {
        "x_tok": x,
        "x_feat": x.T,
        "win": attn("Win").T,
        "w1": attn("W1").transpose(0, 2, 1),
        "w2": attn("W2").transpose(0, 2, 1),
        "wout": attn("Wout").T,
        "main_w": ffn("weight").T,
        "ag_w": np.concatenate([ffn("lora_A").transpose(1, 0, 2).reshape(D, NE * ER), ffn("gw1").T], 1),
        "lora_b": ffn("lora_B").reshape(NE * ER, D),
        "gw2": ffn("gw2").T,
        "wqkv": np.stack([a["L1_attn_w_" + c].T for c in "qkv"]),
        "wo": a["L1_attn_w_o"].T,
        "tern": np.concatenate([by_half(tf("gate_w")), by_half(tf("up_w")), by_pair(tf("down_w"))]),
        "consts": consts,
        "pcol": np.concatenate(columns, 1),
        "prow": np.broadcast_to(row, (P, row.size)),
    }
    arrays = {name: np.ascontiguousarray(value) for name, value in arrays.items()}
    nc = bacc.Bacc("TRN2", target_bir_lowering=False, num_devices=1)
    args = [nc.dram_tensor(name, value.shape, mybir.dt.from_np(value.dtype), kind="ExternalInput").ap() for name, value in arrays.items()]
    out = nc.dram_tensor("out", [TOK, D], F32, kind="ExternalOutput").ap()
    build(nc, *args, out)
    result = run_bass_kernel_spmd(nc, [arrays], core_ids=[0])
    return result.results[0]["out"].reshape(B, L, D)
```
